# Optimizing a Trainium2 kernel written in Bass

```python
import numpy as np
import jax
import jax.numpy as jnp

def _softmax(x, axis=-1):
    return jax.nn.softmax(x, axis=axis)

def _gelu(x):
    return jax.nn.gelu(x, approximate=True)

def _silu(x):
    return jax.nn.silu(x)

def _sigmoid(x):
    return jax.nn.sigmoid(x)

def _layernorm(x, axis=-1, eps=1e-05):
    m = jnp.mean(x, axis=axis, keepdims=True)
    v = jnp.var(x, axis=axis, keepdims=True)
    return (x - m) / jnp.sqrt(v + eps)

def _scatter_add(tgt, idx, src, axis=0):
    return tgt.at[idx].add(src)

def _segment_sum(src, seg, n):
    return jax.ops.segment_sum(src, seg, n)
kernel_name = 'mk_decoder_postln_d1_seqx_r4_aee5e3'

def setup_inputs(seed: int=0):
    np.random.seed(seed)
    _w = jnp.asarray

    def _rec_inputs():
        import jax
        import jax.numpy as jnp
        _rk = jax.random.key(seed)
        x = -0.0005207 + 1.001 * jax.random.normal(jax.random.fold_in(_rk, 1), (8, 256, 256), jnp.float32)
        _lenS = 256 - jax.random.randint(jax.random.fold_in(_rk, 7), (8,), 0, max(1, 256 // 4) + 1, jnp.int32)
        _lenS2 = 256 - jax.random.randint(jax.random.fold_in(_rk, 8), (8,), 0, max(1, 256 // 4) + 1, jnp.int32)
        _ctx_1024P = jax.random.normal(jax.random.fold_in(_rk, 11), (8, 16, 256), jnp.float32)
        _ctx_1024c = jax.random.dirichlet(jax.random.fold_in(_rk, 511), 0.3 * jnp.ones((16,), jnp.float32), (8, 256))
        _ctx_1024t = jnp.einsum('bsk,bkd->bsd', _ctx_1024c, _ctx_1024P)
        _ctx_1024t = _ctx_1024t * jax.lax.rsqrt(jnp.mean(jnp.square(_ctx_1024t)) + 1e-12) * 0.953939
        ctx_1024 = -0.000514642 + 1.00011 * (_ctx_1024t + 0.3 * jax.random.normal(jax.random.fold_in(_rk, 611), (8, 256, 256), jnp.float32))
        return (x, ctx_1024)
    x, ctx_1024 = _rec_inputs()

    def _L0_attn_setup():
        import jax, jax.numpy as jnp
        import numpy as np
        B, L, D, S = (4, 512, 256, 16)
        key = jax.random.key(seed)
        ks = jax.random.split(key, 8)
        inv_d = 1.0 / np.sqrt(D)
        inv_s = 1.0 / np.sqrt(S)
        A_log = jnp.broadcast_to(jnp.clip(jnp.log(jnp.arange(1, S + 1, dtype=jnp.float32)), -7.0, None), (D, S))
        return {'x': jax.random.normal(ks[0], (B, L, D), jnp.float32), 'A_log': A_log, 'W_B': jax.random.uniform(ks[1], (S, D), jnp.float32, -inv_d, inv_d), 'W_C': jax.random.uniform(ks[2], (D, S), jnp.float32, -inv_s, inv_s), 'D_skip': jnp.ones((D,), jnp.float32), 'log_dt': jax.random.normal(ks[3], (D,), jnp.float32) * 0.01 - 4.0, 'W_in': jax.random.uniform(ks[4], (2 * D, D), jnp.float32, -inv_d, inv_d), 'b_in': jax.random.uniform(ks[5], (2 * D,), jnp.float32, -inv_d, inv_d), 'W_out': jax.random.uniform(ks[6], (D, D), jnp.float32, -inv_d, inv_d), 'b_out': jax.random.uniform(ks[7], (D,), jnp.float32, -inv_d, inv_d), 'ln_g': jnp.ones((D,), jnp.float32), 'ln_b': jnp.zeros((D,), jnp.float32)}
    _L0_attn_all = _L0_attn_setup()
    _L0_attn_in = {k: v for k, v in _L0_attn_all.items() if k in ('A_log', 'W_B', 'W_C', 'D_skip', 'log_dt', 'W_in', 'b_in', 'W_out', 'b_out', 'ln_g', 'ln_b')}
    del _L0_attn_all

    def _L0_xattn_setup():
        import jax, jax.numpy as jnp
        import numpy as np
        B, S, E, NH = (1, 512, 256, 8)
        DH = E // NH
        EPS_BACKEND = 1e-06
        EPS_NORM = 1e-05
        key = jax.random.key(seed)
        ks = jax.random.split(key, 8)
        q = jax.random.normal(ks[0], (B, S, E), jnp.float32)
        k = jax.random.normal(ks[1], (B, S, E), jnp.float32)
        v = jax.random.normal(ks[2], (B, S, E), jnp.float32)
        igate_w = jax.random.normal(ks[3], (NH, 3 * E), jnp.float32) * 0.02
        igate_b = jax.random.normal(ks[4], (NH,), jnp.float32) * 0.1
        fgate_w = jax.random.normal(ks[5], (NH, 3 * E), jnp.float32) * 0.02
        fgate_b = jnp.linspace(3.0, 6.0, NH).astype(jnp.float32)
        norm_w = 1.0 + 0.1 * jax.random.normal(ks[6], (E,), jnp.float32)
        return dict(q=q, k=k, v=v, igate_w=igate_w, igate_b=igate_b, fgate_w=fgate_w, fgate_b=fgate_b, norm_w=norm_w)
    _L0_xattn_all = _L0_xattn_setup()
    _L0_xattn_in = {k: v for k, v in _L0_xattn_all.items() if k in ('igate_w', 'igate_b', 'fgate_w', 'fgate_b', 'norm_w')}
    del _L0_xattn_all

    def _L0_ffn_setup():
        import jax, jax.numpy as jnp
        import numpy as np
        DIM = 256
        MOE_INTER = 256
        SHARED_INTER = 256
        N_EXPERTS = 6
        TOP_K = 2
        ROUTE_SCALE = 1.0
        B, S = (8, 1024)
        STD = 0.02 / np.sqrt(DIM)
        STD_I = 0.02 / np.sqrt(MOE_INTER)
        key = jax.random.key(seed)
        ks = jax.random.split(key, 10)
        inp = {'x': jax.random.normal(ks[0], (B, S, DIM), dtype=jnp.float32), 'gate_w': jax.random.normal(ks[1], (N_EXPERTS, DIM), dtype=jnp.float32) * STD, 'gate_b': jnp.zeros((N_EXPERTS,), dtype=jnp.float32), 'ew1': jax.random.normal(ks[2], (N_EXPERTS, MOE_INTER, DIM), dtype=jnp.float32) * STD, 'ew2': jax.random.normal(ks[3], (N_EXPERTS, DIM, MOE_INTER), dtype=jnp.float32) * STD_I, 'ew3': jax.random.normal(ks[4], (N_EXPERTS, MOE_INTER, DIM), dtype=jnp.float32) * STD, 'fc1': jax.random.normal(ks[5], (SHARED_INTER, DIM), dtype=jnp.float32) * STD, 'fc2': jax.random.normal(ks[6], (SHARED_INTER, DIM), dtype=jnp.float32) * STD, 'fc3': jax.random.normal(ks[7], (DIM, SHARED_INTER), dtype=jnp.float32) * STD_I}
        return inp
    _L0_ffn_all = _L0_ffn_setup()
    _L0_ffn_in = {k: v for k, v in _L0_ffn_all.items() if k in ('gate_w', 'gate_b', 'ew1', 'ew2', 'ew3', 'fc1', 'fc2', 'fc3')}
    del _L0_ffn_all
    return {'x': x, 'ctx_1024': ctx_1024, 'L0_attn_A_log': _L0_attn_in['A_log'], 'L0_attn_W_B': _L0_attn_in['W_B'], 'L0_attn_W_C': _L0_attn_in['W_C'], 'L0_attn_D_skip': _L0_attn_in['D_skip'], 'L0_attn_log_dt': _L0_attn_in['log_dt'], 'L0_attn_W_in': _L0_attn_in['W_in'], 'L0_attn_b_in': _L0_attn_in['b_in'], 'L0_attn_W_out': _L0_attn_in['W_out'], 'L0_attn_b_out': _L0_attn_in['b_out'], 'L0_attn_ln_g': _L0_attn_in['ln_g'], 'L0_attn_ln_b': _L0_attn_in['ln_b'], 'L0_xattn_igate_w': _L0_xattn_in['igate_w'], 'L0_xattn_igate_b': _L0_xattn_in['igate_b'], 'L0_xattn_fgate_w': _L0_xattn_in['fgate_w'], 'L0_xattn_fgate_b': _L0_xattn_in['fgate_b'], 'L0_xattn_norm_w': _L0_xattn_in['norm_w'], 'L0_ffn_gate_w': _L0_ffn_in['gate_w'], 'L0_ffn_gate_b': _L0_ffn_in['gate_b'], 'L0_ffn_ew1': _L0_ffn_in['ew1'], 'L0_ffn_ew2': _L0_ffn_in['ew2'], 'L0_ffn_ew3': _L0_ffn_in['ew3'], 'L0_ffn_fc1': _L0_ffn_in['fc1'], 'L0_ffn_fc2': _L0_ffn_in['fc2'], 'L0_ffn_fc3': _L0_ffn_in['fc3']}

def reference(x, ctx_1024, L0_attn_A_log, L0_attn_W_B, L0_attn_W_C, L0_attn_D_skip, L0_attn_log_dt, L0_attn_W_in, L0_attn_b_in, L0_attn_W_out, L0_attn_b_out, L0_attn_ln_g, L0_attn_ln_b, L0_xattn_igate_w, L0_xattn_igate_b, L0_xattn_fgate_w, L0_xattn_fgate_b, L0_xattn_norm_w, L0_ffn_gate_w, L0_ffn_gate_b, L0_ffn_ew1, L0_ffn_ew2, L0_ffn_ew3, L0_ffn_fc1, L0_ffn_fc2, L0_ffn_fc3):
    import jax
    import jax.numpy as jnp

    def _L0_attn_ref(x, A_log, W_B, W_C, D_skip, log_dt, W_in, b_in, W_out, b_out, ln_g, ln_b):
        import jax, jax.numpy as jnp
        import numpy as np
        B, L, D, S = (4, 512, 256, 16)
        Bb, Ll, Dd = x.shape
        residual = x
        mu = x.mean(-1, keepdims=True)
        var = ((x - mu) ** 2).mean(-1, keepdims=True)
        xn = (x - mu) / jnp.sqrt(var + 1e-05) * ln_g + ln_b
        xz = xn @ W_in.T + b_in
        x_proj, z = jnp.split(xz, 2, axis=-1)
        z = jax.nn.silu(z)
        dt = jnp.clip(jnp.exp(log_dt), 0.0001, 1.0)
        A_bar = jnp.exp(-jnp.exp(A_log) * dt[:, None])
        A_bar = jnp.clip(A_bar, 1e-08, 1.0 - 1e-08)
        B_proj = x_proj @ W_B.T * dt.mean()
        t_idx = jnp.arange(Ll, dtype=jnp.float32)
        log_A = jnp.log(A_bar)
        A_mean = jnp.exp(t_idx[:, None, None] * log_A[None]).mean(axis=1)
        kernel = jnp.flip(A_mean.T, -1)[:, None, :]
        lhs = jnp.transpose(B_proj, (0, 2, 1))
        x_mean = jax.lax.conv_general_dilated(lhs, kernel, window_strides=(1,), padding=((Ll - 1, 0),), dimension_numbers=('NCH', 'OIH', 'NCH'), feature_group_count=kernel.shape[0])
        x_mean = jnp.transpose(x_mean, (0, 2, 1))
        y = x_mean @ W_C.T + D_skip * x_proj
        y = y * z
        y = y @ W_out.T + b_out
        return y + residual

    def _L0_xattn_ref(q, k, v, igate_w, igate_b, fgate_w, fgate_b, norm_w):
        import jax, jax.numpy as jnp
        import numpy as np
        B, S, E, NH = (1, 512, 256, 8)
        DH = E // NH
        EPS_BACKEND = 1e-06
        EPS_NORM = 1e-05
        Bq, Sq, Eq = q.shape
        nh = igate_w.shape[0]
        dh = Eq // nh
        gate_in = jnp.concatenate([q, k, v], axis=-1)
        ig = jnp.transpose(gate_in @ igate_w.T + igate_b, (0, 2, 1))
        fg = jnp.transpose(gate_in @ fgate_w.T + fgate_b, (0, 2, 1))
        qh = q.reshape(Bq, Sq, nh, dh).transpose(0, 2, 1, 3)
        kh = k.reshape(Bq, Sq, nh, dh).transpose(0, 2, 1, 3)
        vh = v.reshape(Bq, Sq, nh, dh).transpose(0, 2, 1, 3)
        log_f_cum = jnp.cumsum(jax.nn.log_sigmoid(fg), axis=-1)
        log_fg_mat = log_f_cum[:, :, :, None] - log_f_cum[:, :, None, :]
        ltr = jnp.tril(jnp.ones((Sq, Sq), dtype=bool))
        log_D = jnp.where(ltr, log_fg_mat + ig[:, :, None, :], -jnp.inf)
        max_log_D = jnp.max(log_D, axis=-1, keepdims=True)
        D = jnp.exp(log_D - max_log_D)
        qk = jnp.einsum('bhsd,bhtd->bhst', qh, kh) / jnp.sqrt(jnp.float32(dh))
        C = qk * D
        normalizer = jnp.maximum(jnp.abs(jnp.sum(C, axis=-1, keepdims=True)), jnp.exp(-max_log_D))
        h = jnp.einsum('bhst,bhtd->bhsd', C / (normalizer + EPS_BACKEND), vh)
        mean = jnp.mean(h, axis=-1, keepdims=True)
        var = jnp.var(h, axis=-1, keepdims=True)
        h_norm = (h - mean) / jnp.sqrt(var + EPS_NORM)
        h_norm = h_norm * norm_w.reshape(nh, dh)[None, :, None, :]
        return h_norm.transpose(0, 2, 1, 3).reshape(Bq, Sq, Eq)

    def _L0_ffn_ref(x, gate_w, gate_b, ew1, ew2, ew3, fc1, fc2, fc3):
        import jax, jax.numpy as jnp
        import numpy as np
        DIM = 256
        MOE_INTER = 256
        SHARED_INTER = 256
        N_EXPERTS = 6
        TOP_K = 2
        ROUTE_SCALE = 1.0
        B, S = (8, 1024)
        STD = 0.02 / np.sqrt(DIM)
        STD_I = 0.02 / np.sqrt(MOE_INTER)
        orig_shape = x.shape
        xt = x.reshape(-1, DIM)
        logits = xt @ gate_w.T + gate_b
        probs = jax.nn.sigmoid(logits)
        w, idx = jax.lax.top_k(probs, TOP_K)
        w = w / (jnp.sum(w, axis=-1, keepdims=True) + 1e-08)
        w = w * ROUTE_SCALE
        ge = jnp.sum(jax.nn.one_hot(idx, N_EXPERTS, dtype=w.dtype) * w[..., None], axis=1)
        y = jnp.zeros_like(xt)
        for e in range(N_EXPERTS):
            h = jax.nn.silu(xt @ ew1[e].T) * (xt @ ew3[e].T)
            y = y + ge[:, e:e + 1] * (h @ ew2[e].T)
        z = jax.nn.silu(xt @ fc1.T) * (xt @ fc2.T) @ fc3.T
        return (y + z).reshape(orig_shape)
    x = _layernorm(x + _L0_attn_ref(x, L0_attn_A_log, L0_attn_W_B, L0_attn_W_C, L0_attn_D_skip, L0_attn_log_dt, L0_attn_W_in, L0_attn_b_in, L0_attn_W_out, L0_attn_b_out, L0_attn_ln_g, L0_attn_ln_b), axis=-1)
    x = _layernorm(x + _L0_xattn_ref(x, ctx_1024, ctx_1024, L0_xattn_igate_w, L0_xattn_igate_b, L0_xattn_fgate_w, L0_xattn_fgate_b, L0_xattn_norm_w), axis=-1)
    x = _layernorm(x + _L0_ffn_ref(x, L0_ffn_gate_w, L0_ffn_gate_b, L0_ffn_ew1, L0_ffn_ew2, L0_ffn_ew3, L0_ffn_fc1, L0_ffn_fc2, L0_ffn_fc3), axis=-1)
    return x

_drawn_inputs = setup_inputs


def setup_inputs(seed=0):
    import zlib

    import numpy as np

    out = dict(_drawn_inputs(seed))
    spreads = {'L0_attn_D_skip': (1.0, 0.6),
     'L0_attn_ln_g': (1.0, 0.6),
     'L0_attn_ln_b': (0.0, 0.784),
     'L0_ffn_gate_b': (0.0, 2.0)}
    factors = {'L0_attn_A_log': 57.842,
     'L0_attn_W_B': 64.0,
     'L0_attn_W_C': 64.0,
     'L0_attn_log_dt': 8.0,
     'L0_attn_b_in': 8.0,
     'L0_attn_b_out': 2.928,
     'L0_xattn_igate_b': 64.0,
     'L0_ffn_gate_w': 64.0,
     'L0_ffn_ew1': 64.0,
     'L0_ffn_ew2': 64.0,
     'L0_ffn_ew3': 64.0,
     'L0_ffn_fc1': 64.0,
     'L0_ffn_fc2': 64.0,
     'L0_ffn_fc3': 64.0}
    for name, (base, spread) in spreads.items():
        noise = np.random.default_rng([zlib.crc32(name.encode()), seed]).standard_normal(out[name].shape)
        drawn = base * np.exp(spread * noise) if base else spread * noise
        out[name] = jnp.asarray(drawn.astype(out[name].dtype))
    for name, factor in factors.items():
        out[name] = (out[name] * factor).astype(out[name].dtype)
    return out
```

```python
import math

import concourse.bass as bass
from concourse import mybir

F32 = mybir.dt.float32
F32R = mybir.dt.float32r
BF16 = mybir.dt.bfloat16
I32 = mybir.dt.int32
ALU = mybir.AluOpType
ACT = mybir.ActivationFunctionType
X = mybir.AxisListType.X

P = 128
B, S, D = 8, 256, 256
T = B * S // P
KC = D // P
NG = 4
GT = T // NG
GN = GT * P
NS = 16
NH, DH = 8, 32
HG = P // DH
DV = DH + 1
NE = 6
EPS = 1e-5
LOG_FLOOR = -math.log(1e-8)
QK_SCALE = DH ** -0.5
MASKED = -1e30

C_LOGDT, C_DSKIP, C_BIN, C_LNG, C_LNB, C_ALOG, C_GB = 0, 2, 4, 8, 10, 12, 44
N_COLS = 46


def build(nc, x, ctx, ctx_t, cols, rows, win_t, wb_t, wc_t, wout_t, gates_t, moe_w, router_t, out):
    class Region:

        def __init__(self, start):
            self.at = start

        def __call__(self, name, shape, dt=F32):
            size = int(np_prod(shape[1:])) * (2 if dt == BF16 else 4)
            t = nc.alloc_sbuf_tensor_at(name, shape, dt, offset=self.at)
            self.at += (size + 31) // 32 * 32
            return t

    def np_prod(xs):
        n = 1
        for v in xs:
            n *= v
        return n

    keep = Region((nc.sbuf_base + 31) // 32 * 32)
    x_tm = keep("x_tm", [P, T, D])
    x1 = keep("x1", [P, T, D])
    xq_t = keep("xq_t", [P, KC, B * S])
    acc = keep("acc", [P, T, D])
    z_t = acc[:, :, :].rearrange("p t d -> p (t d)").rearrange("p (c n) -> p c n", c=KC)
    split_at = keep.at
    xh = keep("xh", [P, KC, B * S], F32R)
    xl = keep("xl", [P, KC, B * S], F32R)
    ident = keep("ident", [P, P])
    mirror = keep("mirror", [P, P])
    ident_b = keep("ident_b", [P, P], BF16)
    mask_b = keep("mask_b", [P, HG, P], BF16)
    block_mask = keep("block_mask", [P, HG, DV])
    onehot_f = keep("onehot_f", [2 * NH, NH, P])
    onehot = keep("onehot", [2 * NH, NH, P], F32R)
    inv_d = keep("inv_d", [P, P])
    ones = keep("ones", [P, S])
    pow_e = keep("pow_e", [P, 16])
    prio = keep("prio", [P, NE])
    col = keep("col", [P, N_COLS])
    row = keep("row", [P, 2 * D + NE])
    b_out_row, norm_w_row, gate_b_row = row[:, 0:D], row[:, D:2 * D], row[:, 2 * D:]
    wb = keep("wb", [P, KC, NS])
    wc = keep("wc", [NS, D])
    gw = keep("gw", [P, 3 * KC, 2 * NH])
    gw_ctx = keep("gw_ctx", [P, KC, 2 * NH])
    stats = keep("stats", [P, T, 6])
    mv = keep("mv", [P, T, 2])
    rstd = keep("rstd", [P, T])
    small = keep("small", [P, T, 2 * NH])
    tok = keep("tok", [P, 4, B * NH])
    wr = keep("wr", [P, KC, NE])
    wrh = keep("wrh", [P, KC, NE], F32R)
    wrl = keep("wrl", [P, KC, NE], F32R)
    raw = keep("raw", [P, 3, KC, D])
    expert0_at = keep.at
    wh0 = keep("wh0", [P, 3, KC, D], F32R)
    wl0 = keep("wl0", [P, 3, KC, D], F32R)
    shared_at = keep.at

    ra = Region(shared_at)
    decay_pow = ra("decay_pow", [P, KC, NS, S])
    xm_t = ra("xm_t", [NS, B * S])
    cx_t = ra("cx_t", [P, KC, B * S])
    win = ra("win", [P, KC, 2 * D])
    ra_top = ra.at
    rt = Region(shared_at)
    toep = rt("toep", [P, NS, S])
    yh = rt("yh", [P, KC, GN], F32R)
    yl = rt("yl", [P, KC, GN], F32R)
    ybuf = rt("ybuf", [P, KC, GN])
    rw_ = Region(expert0_at)
    wih = rw_("wih", [P, KC, 2 * D], F32R)
    wil = rw_("wil", [P, KC, 2 * D], F32R)
    rs = Region(ra_top)
    wout = rs("wout", [P, KC, D])
    woh = rs("woh", [P, KC, D], F32R)
    wol = rs("wol", [P, KC, D], F32R)
    tsteps_i = rs("tsteps_i", [P, S], I32)
    tsteps = rs("tsteps", [P, S])
    dt = rs("dt", [P, KC])
    dt_mean = rs("dt_mean", [P, 1])
    log_a = rs("log_a", [P, KC, NS])
    b_in2 = rs("b_in2", [P, 4])
    amean = rs("amean", [P, 2 * NS])
    amean_t = rs("amean_t", [2 * NS, P])
    zpad = rs("zpad", [NS, P])
    bproj = rs("bproj", [P, 2, NS, B])
    bmir = rs("bmir", [P, 2, NS, B])
    xm = rs("xm", [P, 2, NS, B])
    rb = Region(shared_at)
    kbd = [rb(f"kbd{i}", [P, KC, HG, S]) for i in range(2)]
    ctb = [rb(f"ctb{i}", [P, 2, D]) for i in range(2)]
    qb = [rb(f"qb{i}", [P, KC, S]) for i in range(2)]
    gmb = [rb(f"gmb{i}", [2 * NH, 2, S], F32R) for i in range(2)]
    vb = [rb(f"vb{i}", [P, 2, NH, DV]) for i in range(2)]
    wv = rb("wv", [P, NH, DV])
    dec = rb("dec", [P, 2, HG, P])
    cmat = rb("cmat", [P, 4, HG, P])
    state = rb("state", [P, KC, HG, DV])
    nm = rb("nm", [P, 2, NH, DV])
    sq = rb("sq", [P, 2, NH, DH])
    hn = rb("hn", [P, 2, NH, DH])
    carry = rb("carry", [P, NH, DV])
    vsum = rb("vsum", [P, 2, NH])
    vmean = rb("vmean", [P, 2, NH])
    ssum = rb("ssum", [P, 2, NH])
    nrm = rb("nrm", [P, 2, NH])
    rec = rb("rec", [P, 2, NH])
    rec2 = rb("rec2", [P, 2, NH])
    var = rb("var", [P, 2, NH])
    rsd = rb("rsd", [P, 2, NH])
    rr = rb("rr", [P, 2, NH])
    rr_ = Region(split_at)
    gsel = rr_("gsel", [P, 2, 2, 2, B, NH])
    fa = rr_("fa", [P, S])
    fe = rr_("fe", [P, S])
    fl = rr_("fl", [P, S])
    fm = rr_("fm", [P, S])
    ls = rr_("ls", [P, S])
    fcum = rr_("fcum", [P, S])
    g = rr_("g", [P, S])
    mx = rr_("mx", [P, S])
    nmx = rr_("nmx", [P, S])
    mld = rr_("mld", [P, S])
    em = rr_("em", [P, S])
    e1 = rr_("e1", [P, P])
    wx = rr_("wx", [P, P])
    nr127 = rr_("nr127", [P, 1])
    gm = rr_("gm", [P, 2, S], F32R)
    re_ = Region(shared_at)
    wh1 = re_("wh1", [P, 3, KC, D], F32R)
    wl1 = re_("wl1", [P, 3, KC, D], F32R)
    sil = re_("sil", [P, KC, GN])
    hbuf = re_("hbuf", [P, KC, GN])
    hh = [re_(f"hh{i}", [P, KC, GN], F32R) for i in range(2)]
    hl = [re_(f"hl{i}", [P, KC, GN], F32R) for i in range(2)]
    wh, wl = [wh0, wh1], [wl0, wl1]
    lg = re_("lg", [P, T, NE])
    pe_ = re_("pe_", [P, T, NE])
    pr = re_("pr", [P, T, NE])
    eq = re_("eq", [P, T, NE])
    kk = re_("kk", [P, T, NE])
    oh1 = re_("oh1", [P, T, NE])
    p1 = re_("p1", [P, T, NE])
    oh2 = re_("oh2", [P, T, NE])
    ge = re_("ge", [P, T, NE])
    m1 = re_("m1", [P, T])
    m2 = re_("m2", [P, T])
    km = re_("km", [P, T])
    rw = re_("rw", [P, T])
    assert max(rs.at, rb.at, re_.at) <= nc.sbuf_usable_end, (rs.at, rb.at, re_.at)

    ps = nc.alloc_psum_tensor("ps", [P, 8, 512], F32)
    apad = nc.dram_tensor("apad", [NS, 3 * P], F32).ap()
    gmd = nc.dram_tensor("gmd", [2, B, NH, 2 * S], F32).ap()

    names = {}

    def sem(name):
        assert name not in names
        names[name] = nc.alloc_semaphore(name)
        return names[name]

    def wait(eng, s, n):
        if not isinstance(n, int) or n > 0:
            eng.wait_ge(s, n)

    s_col, s_row, s_win, s_wb, s_wc, s_wout, s_gw, s_wr, s_cxt = (
        sem(f"loaded_{n}") for n in ("col", "row", "win", "wb", "wc", "wout", "gw", "wr", "cxt"))
    s_x = [sem(f"loaded_x{n}") for n in range(NG)]
    s_const = sem("constants_made")
    s_ident, s_inv = sem("ident_made"), sem("inv_made")
    s_onehot = sem("onehot_made")
    s_mirror, s_mir, s_mirc = sem("mirror_made"), sem("bproj_mirrored"), sem("bproj_mirror_copied")
    s_tstep_i, s_edt, s_ea = (
        sem(n) for n in ("tstep_i", "exp_log_dt", "exp_a_log"))
    s_decay_step = sem("decay_step")
    s_dmul, s_dexp, s_amean, s_am_sb, s_am_t, s_amt_sb, s_pad, s_toep = (
        sem(n) for n in ("decay_scaled", "decay_exp", "decay_summed", "decay_mean_copied", "decay_mean_t",
                         "decay_mean_t_copied", "decay_stored", "toeplitz_loaded"))
    s_dtm, s_bias, s_bin2, s_winf, s_wih, s_wil, s_woh, s_wol, s_gwc = (
        sem(n) for n in ("dt_mean_copied", "bias_summed", "bias_made", "win_scaled", "win_hi", "win_lo", "wout_hi",
                         "wout_lo", "gate_ctx_weights"))
    lns = [{k: sem(f"{k}_{i}") for k in ("stats", "aggr", "vareps", "rstd", "normed", "turned", "hi", "lo")}
           for i in range(2)]
    s_proj, s_projc, s_x2b, s_bp, s_bps, s_conv, s_xm, s_xmt, s_xmtc = (
        sem(n) for n in ("projected", "projected_copied", "x2b_made", "bproj_summed", "bproj_scaled", "conv_done",
                         "conv_copied", "conv_t", "conv_t_copied"))
    s_wcd, s_u, s_y, s_yh, s_yl, s_o, s_r, s_st1, s_ag1, s_ve1, s_rs1, s_x1, s_x1t, s_q, s_g = (
        sem(n) for n in ("mixed", "skip_added", "gated", "gated_hi", "gated_lo", "out_projected", "residual1",
                         "stats_r1", "aggr_r1", "vareps_r1", "rstd_r1", "x1_made", "x1_turned", "q_copied",
                         "gates_summed"))
    s_gc, s_gs, s_gt, s_fa, s_fe, s_fl, s_em, s_e1, s_wx, s_gh, s_gl, s_tt, s_tok, s_gmd = (
        sem(n) for n in ("gates_copied", "gates_ordered", "gates_turned", "f_abs", "f_exp", "f_ln", "exp_neg_max",
                         "carry_weight", "key_weight", "gm_hi", "gm_lo", "rows_turned", "rows_copied", "gm_stored"))
    s_row_step = sem("row_step")
    s_kz, s_vone = sem("kbd_cleared"), sem("value_ones")
    s_in = [sem(f"batch_loaded{i}") for i in range(2)]
    (s_vs, s_vm, s_vb, s_wv, s_free, s_sc, s_dec, s_c, s_st, s_sbd, s_int, s_car, s_n0, s_n1, s_sq, s_ss, s_nrm,
     s_nre, s_rec, s_rec2, s_var, s_vare, s_rsd, s_rr, s_hn, s_hw, s_r2) = (
        sem(n) for n in ("v_summed", "v_mean", "v_centred", "v_weighted", "batch_freed", "scores_ready", "decay_done",
                         "c_done", "state_summed", "state_masked", "carry_summed", "carry_scaled", "num0_copied",
                         "num1_summed", "squared", "squares_summed", "norm_max", "norm_eps", "norm_rec", "rec_squared",
                         "var_scaled", "var_eps", "var_rsqrt", "head_scale", "head_normed", "head_weighted",
                         "residual2"))
    s_nr0 = sem("norm_positive")
    s_raw, s_wh, s_wl, s_wr2, s_ab, s_sil, s_h, s_hh, s_hl, s_yr, s_acc = (
        sem(n) for n in ("raw_loaded", "expert_hi", "expert_lo", "router_split", "up_ready", "silu_done",
                         "hidden_done", "hidden_hi", "hidden_lo", "down_ready", "acc_done"))
    s_lg, s_gate, s_pexp = sem("logits_summed"), sem("gating_step"), sem("router_exp")
    s_fst, s_fag, s_fve, s_frs, s_fout, s_store = (
        sem(n) for n in ("stats_out", "aggr_out", "vareps_out", "rstd_out", "out_made", "out_stored"))

    U = 4 * (NE + 1)

    def tile_ps(bank, k):
        return ps[:, bank, k * P:(k + 1) * P]

    block_cm = nc.Block()
    with block_cm as block:

        @block.sync
        def _(sp):
            xv = x.rearrange("(t p) d -> p t d", p=P)
            sp.dma_start(col[:], cols).then_inc(s_col, 16)
            sp.dma_start(x_tm[:, 0:GT, :], xv[:, 0:GT, :]).then_inc(s_x[0], 16)
            sp.dma_start(win[:], win_t.rearrange("(c p) n -> p c n", p=P)).then_inc(s_win, 16)
            for n in range(1, NG):
                sp.dma_start(x_tm[:, n * GT:(n + 1) * GT, :], xv[:, n * GT:(n + 1) * GT, :]).then_inc(s_x[n], 16)
            sp.dma_start(wb[:], wb_t.rearrange("(c p) n -> p c n", p=P)).then_inc(s_wb, 16)
            sp.dma_start(row[:], rows.partition_broadcast(P)).then_inc(s_row, 16)
            sp.dma_start(wc[:], wc_t).then_inc(s_wc, 16)
            sp.dma_start(wout[:], wout_t.rearrange("(c p) n -> p c n", p=P)).then_inc(s_wout, 16)
            sp.dma_start(gw[:], gates_t.rearrange("(c p) n -> p c n", p=P)).then_inc(s_gw, 16)
            sp.dma_start(cx_t[:], ctx_t.rearrange("(c p) n -> p c n", p=P)).then_inc(s_cxt, 16)
            sp.dma_start(wr[:], router_t.rearrange("(c p) n -> p c n", p=P)).then_inc(s_wr, 16)
            sp.wait_ge(s_const, 1)
            sp.dma_start(apad[:, 0:P], zpad[:]).then_inc(s_pad, 16)
            sp.wait_ge(s_amt_sb, 1)
            sp.dma_start(bass.AP(apad.tensor, P, [[P, 2], [3 * P, NS], [1, P]]), amean_t[:]).then_inc(s_pad, 16)
            sp.wait_ge(s_pad, 32)
            sp.dma_start(toep[:], bass.AP(apad.tensor, 1, [[1, P], [3 * P, NS], [1, S]])).then_inc(s_toep, 16)
            sp.dma_start(raw[:], moe_w[0].rearrange("m (c p) n -> p m c n", p=P)).then_inc(s_raw, 16)

            sp.wait_ge(s_gh, 2)
            sp.wait_ge(s_gl, 2)
            sp.dma_start(gmd.rearrange("a b h n -> (a b h) n"), gm[:, :, :].rearrange("p a n -> p (a n)").bitcast(F32)).then_inc(s_gmd, 16)
            sp.wait_ge(s_gmd, 16)
            sp.wait_ge(s_kz, 2)
            sp.wait_ge(s_q, 2 * NG)
            cxv = ctx_t.rearrange("(c h p) n -> p c h n", h=HG, p=DH)
            ctv = ctx.rearrange("(t p) d -> p t d", p=P)

            def load(b, i):
                for h in range(HG):
                    sp.dma_start(kbd[i][h * DH:(h + 1) * DH, :, h, :], cxv[:, :, h, bass.ds(b * S, S)]).then_inc(s_in[i], 16)
                sp.dma_start(ctb[i][:], ctv[:, bass.ds(b * 2, 2), :]).then_inc(s_in[i], 16)
                sp.dma_start(gmb[i][:, :, :].rearrange("p a n -> p (a n)").bitcast(F32),
                             gmd[:, bass.ds(b, 1), :, :].rearrange("a b h n -> (a b h) n")
                             if isinstance(b, int) else
                             bass.AP(gmd.tensor, b * (NH * 2 * S), [[B * NH * 2 * S, 2], [2 * S, NH], [1, 2 * S]])
                             ).then_inc(s_in[i], 16)
                sp.dma_start(qb[i][:], xq_t[:, :, bass.ds(b * S, S)]).then_inc(s_in[i], 16)

            for i in range(2):
                load_static(sp, nc, i, kbd, ctb, qb, gmb, cxv, ctv, gmd, xq_t, s_in)
            with sp.Fori(0, B // 2 - 1) as it:
                for i in range(2):
                    sp.wait_ge(s_free, it * 2 + (i + 3))
                    load(it * 2 + (i + 2), i)

            for e in range(1, NE + 1):
                sp.wait_ge(s_wl, 3 * e)
                sp.dma_start(raw[:], moe_w[e].rearrange("m (c p) n -> p m c n", p=P)).then_inc(s_raw, 16)
            ov = out.rearrange("(t p) d -> p t d", p=P)
            for n in range(NG):
                sp.wait_ge(s_fout, GT * (n + 1))
                sp.dma_start(ov[:, n * GT:(n + 1) * GT, :], acc[:, n * GT:(n + 1) * GT, :]).then_inc(s_store, 16)
            sp.wait_ge(s_store, 16 * NG)

        @block.gpsimd
        def _(pool):
            gp = nc.gpsimd
            gp.memset(zpad[:], 0.0).then_inc(s_const, 1)
            gp.iota(tsteps_i[:], [[1, S]], base=0, channel_multiplier=0).then_inc(s_tstep_i, 1)
            gp.memset(ident[:], 0.0).then_inc(s_ident, 1)
            pool.wait_ge(s_ident, 1)
            gp.affine_select(out=ident[:], in_=ident[:], compare_op=ALU.not_equal, fill=1.0, base=0,
                             pattern=[[-1, P]], channel_multiplier=1).then_inc(s_ident, 1)
            gp.memset(mirror[:], 0.0).then_inc(s_mirror, 1)
            pool.wait_ge(s_mirror, 1)
            gp.affine_select(out=mirror[:], in_=mirror[:], compare_op=ALU.not_equal, fill=1.0, base=1 - P,
                             pattern=[[1, P]], channel_multiplier=1).then_inc(s_mirror, 1)
            pool.wait_ge(s_winf, KC)
            gp.tensor_copy(wih[:], win[:]).then_inc(s_wih, 1)
            pool.wait_ge(s_wih, 1)
            gp.tensor_tensor(wil[:], win[:], wih[:].bitcast(F32), ALU.subtract).then_inc(s_wil, 1)
            gp.memset(pow_e[:], -0.5).then_inc(s_const, 1)
            gp.memset(ones[:], 1.0).then_inc(s_const, 1)

            def rsqrt(eps_sem, n, lo, hi, src, done):
                pool.wait_ge(eps_sem, n)
                gp.tensor_tensor(src[:, lo:hi], src[:, lo:hi], pow_e[:, 0:hi - lo], ALU.pow).then_inc(done, 1)

            pool.wait_ge(s_const, 3)
            for n in range(NG):
                rsqrt(lns[0]["vareps"], n + 1, n * GT, (n + 1) * GT, rstd, lns[0]["rstd"])
            pool.wait_ge(s_wout, 16)
            gp.tensor_copy(woh[:], wout[:]).then_inc(s_woh, 1)
            pool.wait_ge(s_woh, 1)
            gp.tensor_tensor(wol[:], wout[:], woh[:].bitcast(F32), ALU.subtract).then_inc(s_wol, 1)
            pool.wait_ge(s_gw, 16)
            gp.tensor_tensor(gw_ctx[:], gw[:, KC:2 * KC, :], gw[:, 2 * KC:3 * KC, :], ALU.add).then_inc(s_gwc, 1)
            gp.memset(mask_b[:], 0.0).then_inc(s_const, 1)
            gp.memset(ident_b[:], 0.0).then_inc(s_const, 1)
            gp.memset(block_mask[:], 1.0).then_inc(s_const, 1)
            gp.memset(onehot_f[:], 0.0).then_inc(s_const, 1)
            pool.wait_ge(s_const, 7)
            gp.affine_select(out=mask_b[:], in_=mask_b[:], compare_op=ALU.is_ge, fill=MASKED, base=0,
                             pattern=[[0, HG], [1, P]], channel_multiplier=-1).then_inc(s_const, 1)
            gp.affine_select(out=ident_b[:], in_=ident_b[:], compare_op=ALU.not_equal, fill=1.0, base=0,
                             pattern=[[-1, P]], channel_multiplier=1).then_inc(s_const, 1)
            gp.affine_select(out=block_mask[:], in_=block_mask[:], compare_op=ALU.is_ge, fill=0.0, base=0,
                             pattern=[[-DH, HG], [0, DV]], channel_multiplier=1).then_inc(s_const, 1)
            pool.wait_ge(s_const, 10)
            gp.affine_select(out=block_mask[:], in_=block_mask[:], compare_op=ALU.is_ge, fill=0.0, base=DH - 1,
                             pattern=[[DH, HG], [0, DV]], channel_multiplier=-1).then_inc(s_const, 1)
            gp.affine_select(out=onehot_f[:], in_=onehot_f[:], compare_op=ALU.not_equal, fill=1.0, base=0,
                             pattern=[[-1, NH], [0, P]], channel_multiplier=1).then_inc(s_onehot, 1)
            pool.wait_ge(s_onehot, 1)
            gp.affine_select(out=onehot_f[:], in_=onehot_f[:], compare_op=ALU.not_equal, fill=1.0, base=-NH,
                             pattern=[[-1, NH], [0, P]], channel_multiplier=1).then_inc(s_onehot, 1)
            pool.wait_ge(s_onehot, 2)
            gp.tensor_copy(onehot[:], onehot_f[:]).then_inc(s_onehot, 1)
            gp.iota(prio[:], [[-1, NE]], base=NE, channel_multiplier=0,
                    allow_small_or_imprecise_dtypes=True).then_inc(s_const, 1)
            pool.wait_ge(s_row, 16)
            for t in range(T):
                pool.wait_ge(lns[0]["normed"], t + 1)
                gp.tensor_tensor(x_tm[:, t, :], x_tm[:, t, :], x_tm[:, t, :], ALU.add).then_inc(s_x2b, 1)
            for t in range(T):
                pool.wait_ge(s_x2b, t + 1)
                gp.tensor_tensor(x_tm[:, t, :], x_tm[:, t, :], b_out_row, ALU.add).then_inc(s_x2b, 1)
            pool.wait_ge(s_proj, 4 * NG)
            split_expert(pool, gp, nc, raw, wh, wl, s_raw, s_wh, s_wl, 0)
            pool.wait_ge(s_wr, 16)
            gp.tensor_copy(wrh[:], wr[:]).then_inc(s_wr2, 1)
            pool.wait_ge(s_wr2, 1)
            gp.tensor_tensor(wrl[:], wr[:], wrh[:].bitcast(F32), ALU.subtract).then_inc(s_wr2, 1)
            for n in range(NG):
                for c in range(KC):
                    pool.wait_ge(s_yh, KC * n + c + 1)
                    gp.tensor_tensor(yl[:, c, :], ybuf[:, c, :], yh[:, c, :].bitcast(F32),
                                     ALU.subtract).then_inc(s_yl, 1)
                rsqrt(s_ve1, n + 1, n * GT, (n + 1) * GT, rstd, s_rs1)

            pool.wait_ge(s_g, NG)
            for i in range(2):
                gp.memset(kbd[i][:], 0.0).then_inc(s_kz, 1)
                gp.memset(vb[i][:, :, :, DH:DV], 1.0).then_inc(s_vone, 1)
            pool.wait_ge(s_tok, 2)
            pool.wait_ge(s_vone, 2)
            for first in (s_vb, s_r2):
                pool.sem_inc(first, 1)
            with pool.Fori(0, B // 2) as it:
                for i in range(2):
                    b = it * 2 + i
                    pool.wait_ge(s_vm, b + 1)
                    pool.wait_ge(s_free, b + 1)
                    gp.tensor_tensor(vb[i][:, :, :, 0:DH],
                                     ctb[i][:, :, :].rearrange("p c (h d) -> p c h d", h=NH),
                                     vmean[:, :, :].unsqueeze(3).broadcast_to([P, 2, NH, DH]),
                                     ALU.subtract).then_inc(s_vb, 1)
                    pool.wait_ge(s_vb, b + 2)
                    pool.wait_ge(s_free, b + 2)
                    gp.tensor_tensor(wv[:], vb[i][:, 0, :, :],
                                     tok[:, 3, bass.ds(b * NH, NH)].unsqueeze(2).broadcast_to([P, NH, DV]),
                                     ALU.mult).then_inc(s_wv, 1)
                    pool.wait_ge(s_vare, b + 1)
                    gp.tensor_tensor(rsd[:].rearrange("p a h -> p (a h)"), var[:].rearrange("p a h -> p (a h)"),
                                     pow_e[:, 0:2 * NH], ALU.pow).then_inc(s_rsd, 1)
                    pool.wait_ge(s_hn, b + 2)
                    hnv = hn[:].rearrange("p a h d -> p a (h d)")
                    gp.tensor_tensor(hnv, hnv, norm_w_row.unsqueeze(1).broadcast_to([P, 2, D]),
                                     ALU.mult).then_inc(s_hw, 1)
                    pool.wait_ge(s_hw, b + 1)
                    gp.tensor_tensor(x_tm[:, bass.ds(b * 2, 2), :], hnv, x1[:, bass.ds(b * 2, 2), :],
                                     ALU.add).then_inc(s_r2, 1)
            for n in range(NG):
                rsqrt(lns[1]["vareps"], n + 1, n * GT, (n + 1) * GT, rstd, lns[1]["rstd"])
            for u in range(U):
                e, n = divmod(u, 4)
                for f in range(KC):
                    pool.wait_ge(s_hh, KC * u + f + 1)
                    wait(pool, s_yr, 2 * (u - 1))
                    gp.tensor_tensor(hl[u % 2][:, f, :], hbuf[:, f, :], hh[u % 2][:, f, :].bitcast(F32),
                                     ALU.subtract).then_inc(s_hl, 1)
                if n == 1 and e < NE:
                    wait(pool, s_yr, 2 * 4 * e)
                    split_expert(pool, gp, nc, raw, wh, wl, s_raw, s_wh, s_wl, e + 1)
                if e == NE:
                    rsqrt(s_fve, n + 1, n * GT, (n + 1) * GT, rstd, s_frs)

        @block.scalar
        def _(act):
            sc = nc.scalar
            act.wait_ge(s_col, 16)
            sc.activation(dt[:], col[:, C_LOGDT:C_LOGDT + KC], ACT.Exp).then_inc(s_edt, 1)
            act.wait_ge(s_decay_step, 1)
            sc.activation(log_a[:], log_a[:], ACT.Exp).then_inc(s_ea, 1)
            for q in range(4):
                for c in range(KC):
                    act.wait_ge(s_dmul, 4 * (KC * q + c + 1))
                    v = decay_pow[:, c, 4 * q:4 * q + 4, :]
                    sc.activation(v, v, ACT.Exp).then_inc(s_dexp, 1)

            def hi_parts(ln, n, first_bank, after=None):
                for c in range(KC):
                    act.wait_ge(ln["turned"], KC * n + c + 1)
                    sc.activation(xh[:, c, n * GN:(n + 1) * GN], ps[:, first_bank + c, :], ACT.Copy)\
                        .then_inc(ln["hi"], 1)

            def projections(n):
                for j in range(4):
                    act.wait_ge(s_proj, 4 * n + j + 1)
                    act.wait_ge(s_bin2, 1)
                    dst = xq_t if j < KC else z_t
                    sc.activation(dst[:, j % KC, n * GN:(n + 1) * GN], ps[:, 2 + j, :],
                                  ACT.Identity if j < KC else ACT.Silu,
                                  bias=b_in2[:, j:j + 1]).then_inc(s_projc, 1)

            hi_parts(lns[0], 0, 0)
            act.wait_ge(s_amean, 1)
            sc.activation(amean[:], ps[:, 7, 0:2 * NS], ACT.Copy).then_inc(s_am_sb, 1)
            sc.activation(dt_mean[:], ps[:, 7, 32:33], ACT.Copy).then_inc(s_dtm, 1)
            act.wait_ge(s_am_t, 1)
            sc.activation(amean_t[:], ps[0:2 * NS, 7, 64:64 + P], ACT.Copy).then_inc(s_amt_sb, 1)
            for n in range(NG):
                if n + 1 < NG:
                    hi_parts(lns[0], n + 1, 0)
                projections(n)
            act.wait_ge(s_mir, 1)
            sc.activation(bmir[:].rearrange("p c s b -> p (c s b)"), ps[:, 6, 0:2 * NS * B], ACT.Copy)\
                .then_inc(s_mirc, 1)
            act.wait_ge(s_conv, 1)
            sc.activation(xm[:].rearrange("p c s b -> p (c s b)"), ps[:, 7, 0:2 * NS * B], ACT.Copy).then_inc(s_xm, 1)
            for n in range(NG):
                act.wait_ge(s_xmt, n + 1)
                sc.activation(xm_t[:, n * GN:(n + 1) * GN], ps[0:NS, n, :], ACT.Copy).then_inc(s_xmtc, 1)
            for n in range(NG + 1):
                if n < NG:
                    for c in range(KC):
                        act.wait_ge(s_y, KC * n + c + 1)
                        wait(act, s_o, 2 * n)
                        sc.activation(yh[:, c, :], ybuf[:, c, :], ACT.Copy).then_inc(s_yh, 1)
                if n >= 1:
                    for c in range(KC):
                        act.wait_ge(s_x1t, KC * (n - 1) + c + 1)
                        sc.activation(xq_t[:, c, (n - 1) * GN:n * GN], ps[:, c, :], ACT.Copy).then_inc(s_q, 1)

            act.wait_ge(s_g, NG)
            sc.activation(small[:].rearrange("p t g -> p (t g)"), ps[:, 6, 0:T * 2 * NH], ACT.Copy).then_inc(s_gc, 1)
            act.wait_ge(s_gt, 1)
            sc.activation(fa[:], ps[:, 7, S:2 * S], ACT.Abs, bias=col[:, C_GB + 1:C_GB + 2]).then_inc(s_fa, 1)
            act.wait_ge(s_fa, 1)
            sc.activation(fe[:], fa[:], ACT.Exp, scale=-1.0).then_inc(s_fe, 1)
            act.wait_ge(s_fe, 1)
            sc.activation(fl[:], fe[:], ACT.Ln, bias=1.0).then_inc(s_fl, 1)
            act.wait_ge(s_row_step, 6)
            sc.activation(wx[:], g[:, 0:P], ACT.Exp, bias=nr127[:, 0:1]).then_inc(s_wx, 1)
            act.wait_ge(s_row_step, 5)
            sc.activation(e1[:], mx[:, P:S], ACT.Exp, scale=-1.0, bias=mx[:, P - 1:P]).then_inc(s_e1, 1)
            act.wait_ge(s_row_step, 8)
            sc.activation(em[:], mld[:], ACT.Exp, scale=-1.0).then_inc(s_em, 1)

            act.sem_inc(s_dec, 2)
            act.sem_inc(s_n0, 1)
            with act.Fori(0, B // 2) as it:
                for i in range(2):
                    b = it * 2 + i
                    for gi in range(4):
                        act.wait_ge(s_sc, b * 4 + (gi + 1))
                        act.wait_ge(s_c, b * 4 + (gi + 1))
                        sc.activation(dec[:, gi % 2, :, :].rearrange("p h s -> p (h s)"), ps[:, gi % 2, :],
                                      ACT.Exp).then_inc(s_dec, 1)
                    act.wait_ge(s_free, b + 3)
                    act.wait_ge(s_hn, b + 1)
                    sc.activation(nm[:, 0, :, :].rearrange("p h d -> p (h d)"), ps[:, 4, 0:NH * DV],
                                  ACT.Copy).then_inc(s_n0, 1)
                    act.wait_ge(s_n0, b + 2)
                    act.wait_ge(s_n1, b + 2)
                    act.wait_ge(s_ss, b + 1)
                    sc.activation(sq[:], nm[:, :, :, 0:DH], ACT.Square).then_inc(s_sq, 1)

            def silu(u):
                for f in range(KC):
                    act.wait_ge(s_ab, KC * u + f + 1)
                    wait(act, s_h, KC * (u - 1) + f + 1)
                    sc.activation(sil[:, f, :], ps[:, 2 * f, :], ACT.Silu).then_inc(s_sil, 1)
                    act.wait_ge(s_h, KC * u + f + 1)
                    wait(act, s_yr, 2 * (u - 1))
                    sc.activation(hh[u % 2][:, f, :], hbuf[:, f, :], ACT.Copy).then_inc(s_hh, 1)

            for n in range(NG):
                hi_parts(lns[1], n, 6)
            silu(0)
            act.wait_ge(s_gate, 1)
            sc.activation(pe_[:], lg[:], ACT.Exp, scale=-1.0).then_inc(s_pexp, 1)
            for u in range(1, U):
                silu(u)

        @block.vector
        def _(dve):
            v = nc.vector

            def stats_of(n, src, sems, done_norm, dst, src_ready=None):
                st, ag, ve, rs_ = sems
                for t in range(n * GT, (n + 1) * GT):
                    v.bn_stats(stats[:, t, :], src[:, t, :]).then_inc(st, 1)
                for t in range(n * GT, (n + 1) * GT):
                    dve.wait_ge(st, t + 1)
                    v.bn_aggr(mv[:, t, :], stats[:, t, :]).then_inc(ag, 1)
                dve.wait_ge(ag, (n + 1) * GT)
                v.tensor_scalar(rstd[:, n * GT:(n + 1) * GT], mv[:, n * GT:(n + 1) * GT, 1], EPS, None,
                                ALU.add).then_inc(ve, 1)
                dve.wait_ge(rs_, n + 1)
                for t in range(n * GT, (n + 1) * GT):
                    v.tensor_scalar(dst(t), src[:, t, :], mv[:, t, 0:1], rstd[:, t:t + 1],
                                    ALU.subtract, ALU.mult).then_inc(done_norm, 1)

            v.memset(inv_d[:], 1.0 / D).then_inc(s_inv, 1)
            dve.wait_ge(s_col, 16)
            v.tensor_scalar(log_a[:], col[:, C_ALOG:C_ALOG + KC * NS].rearrange("p (c s) -> p c s", c=KC),
                            80.0, None, ALU.min).then_inc(s_decay_step, 1)
            dve.wait_ge(s_edt, 1)
            v.tensor_scalar(dt[:], dt[:], 1e-4, 1.0, ALU.max, ALU.min).then_inc(s_decay_step, 1)
            dve.wait_ge(s_decay_step, 2)
            dve.wait_ge(s_ea, 1)
            v.tensor_tensor(log_a[:], log_a[:], dt[:].unsqueeze(2).broadcast_to([P, KC, NS]), ALU.mult)\
                .then_inc(s_decay_step, 1)
            dve.wait_ge(s_decay_step, 3)
            v.tensor_scalar(log_a[:], log_a[:], LOG_FLOOR, -1.0, ALU.min, ALU.mult).then_inc(s_decay_step, 1)
            dve.wait_ge(s_tstep_i, 1)
            v.tensor_copy(tsteps[:], tsteps_i[:]).then_inc(s_decay_step, 1)
            dve.wait_ge(s_decay_step, 5)
            dve.wait_ge(s_decay_step, 4)
            for q in range(4):
                for c in range(KC):
                    for s in range(4 * q, 4 * q + 4):
                        v.tensor_scalar(decay_pow[:, c, s, :], tsteps[:], log_a[:, c, s:s + 1], None, ALU.mult)\
                            .then_inc(s_dmul, 1)
            dve.wait_ge(s_win, 16)
            dve.wait_ge(s_bias, 1)
            v.tensor_tensor(b_in2[:], ps[:, 7, 200:204], col[:, C_BIN:C_BIN + 4], ALU.add).then_inc(s_bin2, 1)
            for c in range(KC):
                v.tensor_scalar(win[:, c, :], win[:, c, :], col[:, C_LNG + c:C_LNG + c + 1], None, ALU.mult)\
                    .then_inc(s_winf, 1)

            def lo_parts(ln, n, first_bank):
                for c in range(KC):
                    dve.wait_ge(ln["hi"], KC * n + c + 1)
                    v.tensor_tensor(xl[:, c, n * GN:(n + 1) * GN], ps[:, first_bank + c, :],
                                    xh[:, c, n * GN:(n + 1) * GN].bitcast(F32), ALU.subtract)\
                        .then_inc(ln["lo"], 1)

            ln = lns[0]
            for n in range(NG + 1):
                if n < NG:
                    dve.wait_ge(s_x[n], 16)
                    stats_of(n, x_tm, (ln["stats"], ln["aggr"], ln["vareps"], ln["rstd"]), ln["normed"],
                             lambda t: x1[:, t, :])
                if n >= 1:
                    lo_parts(ln, n - 1, 0)
            dve.wait_ge(s_bp, NG)
            dve.wait_ge(s_dtm, 1)
            v.tensor_scalar(bproj[:].rearrange("p c s b -> p (c s b)"), ps[:, 6, 0:2 * NS * B], dt_mean[:, 0:1],
                            None, ALU.mult).then_inc(s_bps, 1)
            for n in range(NG + 1):
                if n < NG:
                    for c in range(KC):
                        sl = slice(n * GN, (n + 1) * GN)
                        dve.wait_ge(s_wcd, KC * n + c + 1)
                        wait(dve, s_yl, KC * (n - 1) + c + 1)
                        v.scalar_tensor_tensor(ybuf[:, c, :], xq_t[:, c, sl], col[:, C_DSKIP + c:C_DSKIP + c + 1],
                                               ps[:, 4 + c, :], ALU.mult, ALU.add).then_inc(s_u, 1)
                        dve.wait_ge(s_u, KC * n + c + 1)
                        v.tensor_tensor(ybuf[:, c, :], ybuf[:, c, :], z_t[:, c, sl], ALU.mult).then_inc(s_y, 1)
                if n >= 1:
                    m = n - 1
                    dve.wait_ge(s_x2b, 2 * T)
                    for k in range(2):
                        dve.wait_ge(s_o, 2 * m + k + 1)
                        xt = x_tm[:, m * GT + 2 * k:m * GT + 2 * k + 2, :].rearrange("p t d -> p (t d)")
                        v.tensor_tensor(xt, ps[:, 2 + k, :], xt, ALU.add).then_inc(s_r, 1)
                    dve.wait_ge(s_r, 2 * n)
                    stats_of(m, x_tm, (s_st1, s_ag1, s_ve1, s_rs1), s_x1, lambda t: x1[:, t, :])

            dve.wait_ge(s_gc, 1)
            gv = small[:].rearrange("p (b c) (i h) -> p c i b h", c=2, i=2)
            for c in range(2):
                for dup in range(2):
                    v.tensor_copy(gsel[:, c, :, dup, :, :], gv[:, c, :, :, :]).then_inc(s_gs, 1)
            dve.wait_ge(s_gt, 1)
            dve.wait_ge(s_fa, 1)
            v.tensor_scalar(fm[:], ps[:, 7, S:2 * S], col[:, C_GB + 1:C_GB + 2], 0.0, ALU.add, ALU.min)\
                .then_inc(s_row_step, 1)
            dve.wait_ge(s_row_step, 1)
            dve.wait_ge(s_fl, 1)
            v.tensor_tensor(ls[:], fm[:], fl[:], ALU.subtract).then_inc(s_row_step, 1)
            dve.wait_ge(s_row_step, 2)
            v.tensor_tensor_scan(fcum[:], ones[:], ls[:], 0.0, ALU.mult, ALU.add).then_inc(s_row_step, 1)
            dve.wait_ge(s_row_step, 3)
            v.scalar_tensor_tensor(g[:], ps[:, 7, 0:S], col[:, C_GB:C_GB + 1], fcum[:], ALU.add, ALU.subtract)\
                .then_inc(s_row_step, 1)
            dve.wait_ge(s_row_step, 4)
            v.tensor_tensor_scan(mx[:], g[:], g[:], -3e38, ALU.max, ALU.max).then_inc(s_row_step, 1)
            dve.wait_ge(s_row_step, 5)
            v.tensor_scalar(nr127[:], mx[:, P - 1:P], -1.0, None, ALU.mult).then_inc(s_row_step, 1)
            v.tensor_scalar(nmx[:], mx[:], -1.0, None, ALU.mult).then_inc(s_row_step, 1)
            v.tensor_tensor(mld[:], fcum[:], mx[:], ALU.add).then_inc(s_row_step, 1)
            v.tensor_copy(gm[:, 0, :], g[:]).then_inc(s_gh, 1)
            dve.wait_ge(s_row_step, 7)
            v.tensor_copy(gm[:, 1, :], nmx[:]).then_inc(s_gh, 1)
            dve.wait_ge(s_gh, 2)
            H = B * NH
            v.tensor_tensor(gm[H:, 0, :], g[H:, :], gm[H:, 0, :].bitcast(F32), ALU.subtract).then_inc(s_gl, 1)
            v.tensor_tensor(gm[H:, 1, :], nmx[H:, :], gm[H:, 1, :].bitcast(F32), ALU.subtract).then_inc(s_gl, 1)
            dve.wait_ge(s_tt, 1)
            v.tensor_copy(tok[:, 0:3, :].rearrange("p k r -> p (k r)"), ps[:, 6, 0:3 * H]).then_inc(s_tok, 1)
            v.tensor_scalar(tok[:, 3, :], ps[:, 6, 3 * H:4 * H], QK_SCALE, None, ALU.mult).then_inc(s_tok, 1)

            dve.wait_ge(s_tok, 2)
            dve.sem_inc(s_c, 2)
            for first in (s_n1, s_ss, s_sbd, s_car, s_hn):
                dve.sem_inc(first, 1)
            with dve.Fori(0, B // 2) as it:
                for i in range(2):
                    b = it * 2 + i
                    dve.wait_ge(s_in[i], it * (16 * 7) + 16 * 7)
                    v.tensor_reduce(vsum[:], ctb[i][:].rearrange("p c (h d) -> p c h d", h=NH), X, ALU.add)\
                        .then_inc(s_vs, 1)
                    dve.wait_ge(s_vs, b + 1)
                    dve.wait_ge(s_vb, b + 1)
                    v.tensor_scalar(vmean[:], vsum[:], 1.0 / DH, None, ALU.mult).then_inc(s_vm, 1)

                    def decayed(gi):
                        dve.wait_ge(s_dec, b * 4 + (gi + 3))
                        dve.wait_ge(s_free, b + 2)
                        v.scalar_tensor_tensor(cmat[:, gi, :, :].rearrange("p h s -> p (h s)"),
                                               ps[:, 2 + gi % 2, :], QK_SCALE,
                                               dec[:, gi % 2, :, :].rearrange("p h s -> p (h s)"),
                                               ALU.mult, ALU.mult).then_inc(s_c, 1)
                    decayed(0)
                    decayed(1)
                    dve.wait_ge(s_st, b + 1)
                    v.tensor_tensor(state[:].rearrange("p c h d -> p c (h d)"),
                                    ps[:, 7, 0:2 * HG * DV].rearrange("p (c n) -> p c n", c=KC),
                                    block_mask[:].rearrange("p h d -> p (h d)").unsqueeze(1)
                                    .broadcast_to([P, KC, HG * DV]), ALU.mult).then_inc(s_sbd, 1)
                    decayed(2)
                    decayed(3)
                    dve.wait_ge(s_int, b + 1)
                    v.tensor_tensor(carry[:], ps[:, 6, 0:NH * DV].rearrange("p (h d) -> p h d", h=NH),
                                    tok[:, 2, bass.ds(b * NH, NH)].unsqueeze(2).broadcast_to([P, NH, DV]),
                                    ALU.mult).then_inc(s_car, 1)
                    dve.wait_ge(s_car, b + 2)
                    dve.wait_ge(s_free, b + 3)
                    v.tensor_tensor(nm[:, 1, :, :].rearrange("p h d -> p (h d)"), ps[:, 5, 0:NH * DV],
                                    carry[:].rearrange("p h d -> p (h d)"), ALU.add).then_inc(s_n1, 1)
                    dve.wait_ge(s_n1, b + 2)
                    dve.wait_ge(s_n0, b + 2)
                    v.tensor_tensor(nrm[:], nm[:, :, :, DH], tok[:, 0:2, bass.ds(b * NH, NH)], ALU.max)\
                        .then_inc(s_nr0, 1)
                    dve.wait_ge(s_nr0, b + 1)
                    v.scalar_tensor_tensor(nrm[:], nm[:, :, :, DH], -1.0, nrm[:], ALU.mult, ALU.max)\
                        .then_inc(s_nrm, 1)
                    dve.wait_ge(s_nrm, b + 1)
                    v.tensor_scalar(nrm[:], nrm[:], 1e-6, None, ALU.add).then_inc(s_nre, 1)
                    dve.wait_ge(s_nre, b + 1)
                    v.reciprocal(rec[:], nrm[:]).then_inc(s_rec, 1)
                    dve.wait_ge(s_rec, b + 1)
                    v.tensor_tensor(rec2[:], rec[:], rec[:], ALU.mult).then_inc(s_rec2, 1)
                    dve.wait_ge(s_sq, b + 1)
                    v.tensor_reduce(ssum[:], sq[:], X, ALU.add).then_inc(s_ss, 1)
                    dve.wait_ge(s_ss, b + 2)
                    dve.wait_ge(s_rec2, b + 1)
                    v.tensor_tensor(ssum[:], ssum[:], rec2[:], ALU.mult).then_inc(s_var, 1)
                    dve.wait_ge(s_var, b + 1)
                    v.tensor_scalar(var[:], ssum[:], 1.0 / DH, EPS, ALU.mult, ALU.add).then_inc(s_vare, 1)
                    dve.wait_ge(s_rsd, b + 1)
                    v.tensor_tensor(rr[:], rsd[:], rec[:], ALU.mult).then_inc(s_rr, 1)
                    dve.wait_ge(s_rr, b + 1)
                    dve.wait_ge(s_r2, b + 1)
                    v.tensor_tensor(hn[:], nm[:, :, :, 0:DH], rr[:].unsqueeze(3).broadcast_to([P, 2, NH, DH]),
                                    ALU.mult).then_inc(s_hn, 1)

            ln = lns[1]
            for n in range(NG):
                dve.wait_ge(s_r2, 2 * (n + 1) + 1)
                stats_of(n, x_tm, (ln["stats"], ln["aggr"], ln["vareps"], ln["rstd"]), ln["normed"],
                         lambda t: acc[:, t, :])
                lo_parts(ln, n, 6)

            def hidden(u):
                for f in range(KC):
                    dve.wait_ge(s_sil, KC * u + f + 1)
                    wait(dve, s_hl, KC * (u - 1) + f + 1)
                    v.tensor_tensor(hbuf[:, f, :], sil[:, f, :], ps[:, 2 * f + 1, :], ALU.mult).then_inc(s_h, 1)

            def accumulate(u):
                e, n = divmod(u, 4)
                for k in range(GT):
                    t = n * GT + k
                    dve.wait_ge(s_yr, 2 * u + k // 2 + 1)
                    y = ps[:, 4 + k // 2, (k % 2) * D:(k % 2 + 1) * D]
                    if e == 0:
                        v.tensor_tensor(acc[:, t, :], y, acc[:, t, :], ALU.add).then_inc(s_acc, 1)
                    else:
                        dve.wait_ge(s_acc, GT * (u - 4) + k + 1)
                        v.scalar_tensor_tensor(acc[:, t, :], y, ge[:, t, e - 1:e], acc[:, t, :],
                                               ALU.mult, ALU.add).then_inc(s_acc, 1)
                if e == NE:
                    dve.wait_ge(s_acc, GT * (u + 1))
                    stats_of(n, acc, (s_fst, s_fag, s_fve, s_frs), s_fout, lambda t: acc[:, t, :])

            def gating():
                bc = [P, T, NE]
                step = [0]

                def then(ins):
                    step[0] += 1
                    ins.then_inc(s_gate, 1)
                    dve.wait_ge(s_gate, step[0])

                dve.wait_ge(s_lg, 1)
                then(v.tensor_tensor(lg[:], ps[:, 7, 0:T * NE].rearrange("p (t e) -> p t e", t=T),
                                     gate_b_row.unsqueeze(1).broadcast_to(bc), ALU.add))
                hidden(0)
                dve.wait_ge(s_pexp, 1)
                then(v.tensor_scalar(pe_[:], pe_[:], 1.0, None, ALU.add))
                then(v.reciprocal(pr[:], pe_[:]))

                def pick(p, m, onehot_out):
                    then(v.tensor_reduce(m[:], p[:], X, ALU.max))
                    then(v.tensor_tensor(eq[:], p[:], m[:].unsqueeze(2).broadcast_to(bc), ALU.is_equal))
                    then(v.tensor_tensor(kk[:], eq[:], prio[:].unsqueeze(1).broadcast_to(bc), ALU.mult))
                    then(v.tensor_reduce(km[:], kk[:], X, ALU.max))
                    then(v.tensor_tensor(onehot_out[:], kk[:], km[:].unsqueeze(2).broadcast_to(bc), ALU.is_equal))

                pick(pr, m1, oh1)
                then(v.scalar_tensor_tensor(p1[:], oh1[:], -2.0, pr[:], ALU.mult, ALU.add))
                pick(p1, m2, oh2)
                then(v.tensor_tensor(oh1[:], oh1[:], oh2[:], ALU.add))
                then(v.tensor_tensor(oh1[:], oh1[:], pr[:], ALU.mult))
                then(v.tensor_tensor(m1[:], m1[:], m2[:], ALU.add))
                then(v.tensor_scalar(m1[:], m1[:], 1e-8, None, ALU.add))
                then(v.reciprocal(rw[:], m1[:]))
                then(v.tensor_tensor(ge[:], oh1[:], rw[:].unsqueeze(2).broadcast_to(bc), ALU.mult))

            gating()
            for u in range(1, U):
                hidden(u)
                accumulate(u - 1)
            accumulate(U - 1)

        @block.tensor
        def _(pe):
            te = nc.tensor

            def three(out_, wh_, wl_, rh_, rl_, first, last):
                te.matmul(out_, wh_, rh_, start=first, stop=False)
                te.matmul(out_, wl_, rh_, start=False, stop=False)
                return te.matmul(out_, wh_, rl_, start=False, stop=last)

            pe.wait_ge(s_ident, 2)
            pe.wait_ge(s_inv, 1)
            pe.wait_ge(s_decay_step, 2)
            for c in range(KC):
                te.matmul(ps[:, 7, 32:33], inv_d[:], dt[:, c:c + 1], start=c == 0, stop=c == KC - 1)
            pe.wait_ge(s_win, 16)
            for j in range(4):
                for c in range(KC):
                    last = te.matmul(ps[:, 7, 200 + j:201 + j], win[:, c, j * P:(j + 1) * P],
                                     col[:, C_LNB + c:C_LNB + c + 1], start=c == 0, stop=c == KC - 1)
            last.then_inc(s_bias, 1)

            def turn(lnx, n, src, first_bank):
                pe.wait_ge(lnx["normed"], GT * (n + 1))
                wait(pe, lnx["lo"], KC * n)
                for c in range(KC):
                    for k in range(GT):
                        last_ = te.transpose(tile_ps(first_bank + c, k), src[:, n * GT + k, c * P:(c + 1) * P],
                                             ident[:])
                    last_.then_inc(lnx["turned"], 1)

            def project(n):
                pe.wait_ge(lns[0]["lo"], KC * (n + 1))
                pe.wait_ge(s_wil, 1)
                for j in range(4):
                    wait(pe, s_projc, 4 * (n - 1) + j + 1)
                    for c in range(KC):
                        sl = slice(n * GN, (n + 1) * GN)
                        last_ = three(ps[:, 2 + j, :], wih[:, c, j * P:(j + 1) * P], wil[:, c, j * P:(j + 1) * P],
                                      xh[:, c, sl], xl[:, c, sl], c == 0, c == KC - 1)
                    last_.then_inc(s_proj, 1)

            def b_proj(n):
                pe.wait_ge(s_projc, 4 * n + KC)
                pe.wait_ge(s_wb, 16)
                for k in range(GT):
                    t = n * GT + k
                    o = (t % 2) * NS * B + t // 2
                    for c in range(KC):
                        last_ = te.matmul(ps[:, 6, o:o + NS * B:B], xq_t[:, c, t * P:(t + 1) * P], wb[:, c, :],
                                          start=c == 0, stop=c == KC - 1)
                last_.then_inc(s_bp, 1)

            def decay_sums(q):
                pe.wait_ge(s_dexp, KC * (q + 1))
                for s in range(4 * q, 4 * q + 4):
                    for half in range(2):
                        for c in range(KC):
                            last_ = te.matmul(ps[:, 7, half * NS + s:half * NS + s + 1],
                                              decay_pow[:, c, s, half * P:(half + 1) * P], inv_d[:, 0:1],
                                              start=c == 0, stop=c == KC - 1)
                return last_

            for q in range(4):
                pe.wait_ge(s_bin2, 1)
                last = decay_sums(q)
                if q == 1:
                    turn(lns[0], 0, x1, 0)
            last.then_inc(s_amean, 1)
            pe.wait_ge(s_am_sb, 1)
            pe.wait_ge(s_dtm, 1)
            te.transpose(ps[0:2 * NS, 7, 64:64 + P], amean[:], ident[:]).then_inc(s_am_t, 1)
            for n in range(NG):
                if n + 1 < NG:
                    turn(lns[0], n + 1, x1, 0)
                project(n)
                if n >= 1:
                    b_proj(n - 1)
            b_proj(NG - 1)

            pe.wait_ge(s_bps, 1)
            pe.wait_ge(s_mirror, 2)
            te.matmul(ps[:, 6, 0:2 * NS * B], mirror[:], bproj[:].rearrange("p c s b -> p (c s b)"),
                      start=True, stop=True).then_inc(s_mir, 1)
            pe.wait_ge(s_mirc, 1)
            pe.wait_ge(s_toep, 16)
            for s in range(NS):
                te.matmul(ps[:, 7, s * B:(s + 1) * B], toep[:, s, 0:P], bmir[:, 0, s, :], start=True, stop=True)
                o = ps[:, 7, NS * B + s * B:NS * B + (s + 1) * B]
                te.matmul(o, toep[:, s, P:S], bmir[:, 0, s, :], start=True, stop=False)
                last = te.matmul(o, toep[:, s, 0:P], bmir[:, 1, s, :], start=False, stop=True)
            last.then_inc(s_conv, 1)
            pe.wait_ge(s_xm, 1)
            pe.wait_ge(s_projc, 4 * NG)
            pe.wait_ge(lns[0]["lo"], KC * NG)
            for n in range(NG):
                for k in range(GT):
                    t = n * GT + k
                    last = te.transpose(ps[0:NS, n, k * P:(k + 1) * P], xm[:, t % 2, :, t // 2], ident[:])
                last.then_inc(s_xmt, 1)

            def mix(n):
                pe.wait_ge(s_xmtc, n + 1)
                pe.wait_ge(s_wc, 16)
                for c in range(KC):
                    wait(pe, s_u, KC * (n - 1) + c + 1)
                    te.matmul(ps[:, 4 + c, :], wc[:, c * P:(c + 1) * P], xm_t[:, n * GN:(n + 1) * GN],
                              start=True, stop=True).then_inc(s_wcd, 1)

            def out_project(n):
                pe.wait_ge(s_xmtc, NG)
                pe.wait_ge(s_wol, 1)
                pe.wait_ge(s_yl, KC * (n + 1))
                for k in range(GT):
                    wait(pe, s_r, 2 * (n - 1) + k // 2 + 1)
                    for c in range(KC):
                        last_ = three(ps[:, 2 + k // 2, (k % 2) * D:(k % 2 + 1) * D], yh[:, c, k * P:(k + 1) * P],
                                      yl[:, c, k * P:(k + 1) * P], woh[:, c, :], wol[:, c, :], c == 0, c == KC - 1)
                    if k % 2:
                        last_.then_inc(s_o, 1)

            def gates(n):
                pe.wait_ge(s_x1, GT * (n + 1))
                wait(pe, s_q, KC * n)
                for c in range(KC):
                    for k in range(GT):
                        last_ = te.transpose(tile_ps(c, k), x1[:, n * GT + k, c * P:(c + 1) * P], ident[:])
                    last_.then_inc(s_x1t, 1)
                pe.wait_ge(s_q, KC * (n + 1))
                pe.wait_ge(s_gwc, 1)
                pe.wait_ge(s_cxt, 16)
                for k in range(GT):
                    t = n * GT + k
                    for c in range(KC):
                        te.matmul(ps[:, 6, t * 16:(t + 1) * 16], xq_t[:, c, t * P:(t + 1) * P], gw[:, c, :],
                                  start=c == 0, stop=False)
                    for c in range(KC):
                        last_ = te.matmul(ps[:, 6, t * 16:(t + 1) * 16], cx_t[:, c, t * P:(t + 1) * P],
                                          gw_ctx[:, c, :], start=False, stop=c == KC - 1)
                last_.then_inc(s_g, 1)

            for n in range(NG + 1):
                if n < NG:
                    mix(n)
                if n >= 1:
                    out_project(n - 1)
                    gates(n - 1)

            pe.wait_ge(s_gs, 4)
            for c in range(2):
                for i in range(2):
                    last = te.transpose(ps[:, 7, i * S + c * P:i * S + (c + 1) * P],
                                        gsel[:, c, i, :, :, :].rearrange("p a b h -> p (a b h)"), ident[:])
            last.then_inc(s_gt, 1)
            H = B * NH
            pe.wait_ge(s_em, 1)
            pe.wait_ge(s_e1, 1)
            pe.wait_ge(s_wx, 1)
            for k, src in enumerate((em[0:H, 0:P], em[0:H, P:S], e1[0:H, :], wx[0:H, :])):
                last = te.transpose(ps[:, 6, k * H:(k + 1) * H], src, ident[0:H, 0:H])
            last.then_inc(s_tt, 1)

            pe.wait_ge(s_tok, 2)
            pe.wait_ge(s_const, 12)
            pe.wait_ge(s_onehot, 3)
            pe.sem_inc(s_free, 2)
            with pe.Fori(0, B // 2) as it:
                for i in range(2):
                    b = it * 2 + i

                    def scores(gi):
                        c, hg = divmod(gi, 2)
                        pe.wait_ge(s_dec, b * 4 + (gi + 1))
                        o = ps[:, gi % 2, :]
                        te.matmul(o, ident_b[:], mask_b[:].rearrange("p h s -> p (h s)"), start=True, stop=False)
                        te.matmul(o, gmb[i][:, 0, c * P:(c + 1) * P],
                                  onehot[:, hg * HG:(hg + 1) * HG, :].rearrange("p h s -> p (h s)"),
                                  start=False, stop=False)
                        for h in range(HG):
                            te.matmul(o[:, h * P:(h + 1) * P], onehot[:, hg * HG + h, :],
                                      gmb[i][:, 1, c * P:(c + 1) * P], start=False, stop=h == HG - 1)
                        pe.wait_ge(s_c, b * 4 + (gi + 1))
                        for h in range(HG):
                            last_ = te.matmul(ps[:, 2 + gi % 2, h * P:(h + 1) * P],
                                              kbd[i][:, hg, h, c * P:(c + 1) * P], qb[i][:, hg, c * P:(c + 1) * P],
                                              start=True, stop=True)
                        last_.then_inc(s_sc, 1)

                    def numerator(gi):
                        c, hg = divmod(gi, 2)
                        pe.wait_ge(s_c, b * 4 + (gi + 3))
                        pe.wait_ge(s_n1 if c else s_n0, b + 1)
                        for h in range(HG):
                            hd = hg * HG + h
                            last_ = te.matmul(ps[:, 4 + c, hd * DV:(hd + 1) * DV], cmat[:, gi, h, :],
                                              vb[i][:, c, hd, :], start=True, stop=True)
                        return last_

                    pe.wait_ge(s_in[i], it * (16 * 7) + 16 * 7)
                    scores(0)
                    scores(1)
                    pe.wait_ge(s_wv, b + 1)
                    pe.wait_ge(s_sbd, b + 1)
                    for hg in range(2):
                        last = te.matmul(ps[:, 7, hg * HG * DV:(hg + 1) * HG * DV], ctb[i][:, 0, hg * P:(hg + 1) * P],
                                         wv[:, hg * HG:(hg + 1) * HG, :].rearrange("p h d -> p (h d)"),
                                         start=True, stop=True)
                    last.then_inc(s_st, 1)
                    scores(2)
                    numerator(0)
                    scores(3)
                    numerator(1)
                    pe.wait_ge(s_sbd, b + 2)
                    pe.wait_ge(s_car, b + 1)
                    for hg in range(2):
                        last = te.matmul(ps[:, 6, hg * HG * DV:(hg + 1) * HG * DV], qb[i][:, hg, P:S],
                                         state[:, hg, :, :].rearrange("p h d -> p (h d)"), start=True, stop=True)
                    last.then_inc(s_int, 1)
                    numerator(2)
                    numerator(3).then_inc(s_free, 1)

            pe.wait_ge(s_car, B + 1)
            pe.wait_ge(s_n0, B + 1)
            pe.wait_ge(s_n1, B + 1)

            def up(u):
                e, n = divmod(u, 4)
                pe.wait_ge(s_wl, 3 * (e + 1))
                sl = slice(n * GN, (n + 1) * GN)
                for f in range(KC):
                    wait(pe, s_h, KC * (u - 1) + f + 1)
                    for m in range(2):
                        for c in range(KC):
                            fs = slice(f * P, (f + 1) * P)
                            last_ = three(ps[:, 2 * f + m, :], wh[e % 2][:, m, c, fs], wl[e % 2][:, m, c, fs],
                                          xh[:, c, sl], xl[:, c, sl], c == 0, c == KC - 1)
                    last_.then_inc(s_ab, 1)

            def down(u):
                e, n = divmod(u, 4)
                pe.wait_ge(s_hl, KC * (u + 1))
                for k in range(GT):
                    wait(pe, s_acc, GT * (u - 1) + 2 * (k // 2) + 2)
                    for f in range(KC):
                        last_ = three(ps[:, 4 + k // 2, (k % 2) * D:(k % 2 + 1) * D],
                                      hh[u % 2][:, f, k * P:(k + 1) * P], hl[u % 2][:, f, k * P:(k + 1) * P],
                                      wh[e % 2][:, 2, f, :], wl[e % 2][:, 2, f, :], f == 0, f == KC - 1)
                    if k % 2:
                        last_.then_inc(s_yr, 1)

            for n in range(NG):
                turn(lns[1], n, acc, 6)
            pe.wait_ge(lns[1]["lo"], KC * NG)
            pe.wait_ge(s_wr2, 2)
            for t in range(T):
                for c in range(KC):
                    ts = slice(t * P, (t + 1) * P)
                    last = three(ps[:, 7, t * NE:(t + 1) * NE], xh[:, c, ts], xl[:, c, ts], wrh[:, c, :], wrl[:, c, :],
                                 c == 0, c == KC - 1)
            last.then_inc(s_lg, 1)
            up(0)
            for u in range(1, U):
                up(u)
                down(u - 1)
            down(U - 1)


def split_expert(pool, gp, nc, raw, wh, wl, s_raw, s_wh, s_wl, e):
    pool.wait_ge(s_raw, 16 * (e + 1))
    for m in range(3):
        gp.tensor_copy(wh[e % 2][:, m], raw[:, m]).then_inc(s_wh, 1)
        pool.wait_ge(s_wh, 3 * e + m + 1)
        gp.tensor_tensor(wl[e % 2][:, m], raw[:, m], wh[e % 2][:, m].bitcast(F32), ALU.subtract).then_inc(s_wl, 1)


def load_static(sp, nc, i, kbd, ctb, qb, gmb, cxv, ctv, gmd, xq_t, s_in):
    for h in range(HG):
        sp.dma_start(kbd[i][h * DH:(h + 1) * DH, :, h, :], cxv[:, :, h, i * S:(i + 1) * S]).then_inc(s_in[i], 16)
    sp.dma_start(ctb[i][:], ctv[:, 2 * i:2 * i + 2, :]).then_inc(s_in[i], 16)
    sp.dma_start(gmb[i][:, :, :].rearrange("p a n -> p (a n)").bitcast(F32),
                 bass.AP(gmd.tensor, i * (NH * 2 * S), [[B * NH * 2 * S, 2], [2 * S, NH], [1, 2 * S]])
                 ).then_inc(s_in[i], 16)
    sp.dma_start(qb[i][:], xq_t[:, :, i * S:(i + 1) * S]).then_inc(s_in[i], 16)


def kernel(**inputs):
    import numpy as np
    import concourse.bacc as bacc
    from concourse import mybir as mb
    from concourse.bass_utils import run_bass_kernel_spmd

    a = {k.replace("L0_", ""): np.asarray(v) for k, v in inputs.items()}

    def by_part(v):
        return v.reshape(-1, P).T

    def per_row(v):
        return np.tile(v, 2 * B).reshape(P, 1)

    arrays = {
        "x": a["x"].reshape(B * S, D),
        "ctx": a["ctx_1024"].reshape(B * S, D),
        "ctx_t": a["ctx_1024"].reshape(B * S, D).T,
        "cols": np.concatenate(
            [by_part(a["attn_log_dt"]), by_part(a["attn_D_skip"]), by_part(a["attn_b_in"]), by_part(a["attn_ln_g"]),
             by_part(a["attn_ln_b"]), a["attn_A_log"].reshape(KC, P, NS).transpose(1, 0, 2).reshape(P, KC * NS),
             per_row(a["xattn_igate_b"]), per_row(a["xattn_fgate_b"])], axis=1),
        "rows": np.concatenate([a["attn_b_out"], a["xattn_norm_w"], a["ffn_gate_b"]]),
        "win_t": a["attn_W_in"].T,
        "wb_t": a["attn_W_B"].T,
        "wc_t": a["attn_W_C"].T,
        "wout_t": a["attn_W_out"].T,
        "gates_t": np.concatenate([a["xattn_igate_w"], a["xattn_fgate_w"]], axis=0).T,
        "moe_w": np.stack(
            [np.stack([a["ffn_fc1"].T, a["ffn_fc2"].T, a["ffn_fc3"].T])]
            + [np.stack([a["ffn_ew1"][e].T, a["ffn_ew3"][e].T, a["ffn_ew2"][e].T]) for e in range(NE)]),
        "router_t": a["ffn_gate_w"].T,
    }
    arrays = {f"in_{k}": np.ascontiguousarray(v) for k, v in arrays.items()}
    nc = bacc.Bacc("TRN2", target_bir_lowering=False, num_devices=1)
    args = [nc.dram_tensor(k, v.shape, mb.dt.from_np(v.dtype), kind="ExternalInput").ap() for k, v in arrays.items()]
    o = nc.dram_tensor("out_x", (B * S, D), mb.dt.float32, kind="ExternalOutput").ap()
    build(nc, *args, o)
    r = run_bass_kernel_spmd(nc, [arrays], core_ids=[0])
    return r.results[0]["out_x"].reshape(B, S, D)
```

```python
import math

import concourse.bass as bass
from concourse import mybir

F32 = mybir.dt.float32
F32R = mybir.dt.float32r
BF16 = mybir.dt.bfloat16
I32 = mybir.dt.int32
ALU = mybir.AluOpType
ACT = mybir.ActivationFunctionType
X = mybir.AxisListType.X

P = 128
B, S, D = 8, 256, 256
T = B * S // P
KC = D // P
NG = 4
GT = T // NG
GN = GT * P
NS = 16
NH, DH = 8, 32
HG = P // DH
DV = DH + 1
NE = 6
EPS = 1e-5
LOG_FLOOR = -math.log(1e-8)
QK_SCALE = DH ** -0.5
MASKED = -1e30

C_LOGDT, C_DSKIP, C_BIN, C_LNG, C_LNB, C_ALOG, C_GB = 0, 2, 4, 8, 10, 12, 44
N_COLS = 46


def build(nc, x, ctx, ctx_t, cols, rows, win_t, wb_t, wc_t, wout_t, gates_t, moe_w, router_t, out):
    class Region:

        def __init__(self, start):
            self.at = start

        def __call__(self, name, shape, dt=F32):
            size = int(np_prod(shape[1:])) * (2 if dt == BF16 else 4)
            t = nc.alloc_sbuf_tensor_at(name, shape, dt, offset=self.at)
            self.at += (size + 31) // 32 * 32
            return t

    def np_prod(xs):
        n = 1
        for v in xs:
            n *= v
        return n

    keep = Region((nc.sbuf_base + 31) // 32 * 32)
    x_tm = keep("x_tm", [P, T, D])
    x1 = keep("x1", [P, T, D])
    xq_t = keep("xq_t", [P, KC, B * S])
    acc = keep("acc", [P, T, D])
    z_t = acc[:, :, :].rearrange("p t d -> p (t d)").rearrange("p (c n) -> p c n", c=KC)
    split_at = keep.at
    xh = keep("xh", [P, KC, B * S], F32R)
    xl = keep("xl", [P, KC, B * S], F32R)
    ident = keep("ident", [P, P])
    mirror = keep("mirror", [P, P])
    ident_b = keep("ident_b", [P, P], BF16)
    mask_b = keep("mask_b", [P, HG, P], BF16)
    block_mask = keep("block_mask", [P, HG, DV])
    onehot_f = keep("onehot_f", [2 * NH, NH, P])
    inv_d = keep("inv_d", [P, P])
    ones = keep("ones", [P, S])
    pow_e = keep("pow_e", [P, 16])
    prio = keep("prio", [P, NE])
    col = keep("col", [P, N_COLS])
    row = keep("row", [P, 2 * D + NE])
    b_half = row[:, 0:D]
    b_out_row, norm_w_row, gate_b_row = row[:, 0:D], row[:, D:2 * D], row[:, 2 * D:]
    wb = keep("wb", [P, KC, NS])
    wc = keep("wc", [3 * NS, D])
    wc3 = keep("wc3", [3 * NS, D], F32R)
    gw = keep("gw", [P, 3 * KC, 2 * NH])
    gw_ctx = keep("gw_ctx", [P, KC, 2 * NH])
    stats = keep("stats", [P, T, 6])
    mv = keep("mv", [P, T, 2])
    rstd = keep("rstd", [P, T])
    shift = keep("shift", [P, T])
    small = keep("small", [P, T, 2 * NH])
    tok = keep("tok", [P, 4, B * NH])
    wr = keep("wr", [P, KC, NE])
    wrh = keep("wrh", [P, KC, NE], F32R)
    wrl = keep("wrl", [P, KC, NE], F32R)
    raw = keep("raw", [P, 3, KC, D])
    expert0_at = keep.at
    wh0 = keep("wh0", [P, 3, KC, D], F32R)
    wl0 = keep("wl0", [P, 3, KC, D], F32R)
    shared_at = keep.at

    ra = Region(shared_at)
    decay_pow = ra("decay_pow", [P, NS, KC, P])
    rt = Region(shared_at)
    toep = rt("toep", [P, NS, S])
    yset_at = rt.at
    rt.at += 3 * 4 * KC * GN
    ra = Region(max(ra.at, rt.at))
    xm_t = ra("xm_t", [3 * NS, B * S], F32R)
    cx_t = ra("cx_t", [P, KC, B * S])
    win = ra("win", [P, KC, 2 * D])
    ra_top = ra.at
    rw_ = Region(expert0_at)
    wih = rw_("wih", [P, KC, 2 * D], F32R)
    wil = rw_("wil", [P, KC, 2 * D], F32R)
    rs = Region(ra_top)
    wout = rs("wout", [P, KC, D])
    woh = rs("woh", [P, KC, D], F32R)
    wol = rs("wol", [P, KC, D], F32R)
    tsteps_i = rs("tsteps_i", [P, P], I32)
    tsteps = rs("tsteps", [P, P])
    half_pow = rs("half_pow", [P, KC, NS, 2])
    dt = rs("dt", [P, KC])
    dt_mean = rs("dt_mean", [P, 1])
    log_a = rs("log_a", [P, KC, NS])
    b_in2 = rs("b_in2", [P, 4])
    amean = rs("amean", [P, 2 * NS])
    amean_t = rs("amean_t", [2 * NS, P])
    zpad = rs("zpad", [NS, P])
    bproj = rs("bproj", [P, 2, NS, B])
    bmir = rs("bmir", [P, 2, NS, B])
    xmh = rs("xmh", [P, 2, NS, B], F32R)
    xm3 = rs("xm3", [P, 2, 3, NS, B])
    rb = Region(shared_at)
    kbd = [rb(f"kbd{i}", [P, KC, HG, S]) for i in range(2)]
    ctb = [rb(f"ctb{i}", [P, 2, D]) for i in range(2)]
    qb = [rb(f"qb{i}", [P, KC, S]) for i in range(2)]
    decl = [rb(f"decl{i}", [4 * NH, S], F32R) for i in range(2)]
    decr = [rb(f"decr{i}", [4 * NH, NH, S], F32R) for i in range(2)]
    vb = [rb(f"vb{i}", [P, 2, NH, DV]) for i in range(2)]
    wv = rb("wv", [P, NH, DV])
    dec = rb("dec", [P, 2, HG, P])
    cmat = rb("cmat", [P, 4, HG, P])
    state = rb("state", [P, KC, HG, DV])
    nm = [rb(f"nm{i}", [P, 2, NH, DV]) for i in range(2)]
    sq = rb("sq", [P, 2, NH, DH])
    hn = rb("hn", [P, 2, NH, DH])
    carry = rb("carry", [P, NH, DV])
    vsum = rb("vsum", [P, 2, NH])
    vmean = rb("vmean", [P, 2, NH])
    ssum = rb("ssum", [P, 2, NH])
    nrm = rb("nrm", [P, 2, NH])
    rec = rb("rec", [P, 2, NH])
    rec2 = rb("rec2", [P, 2, NH])
    var = rb("var", [P, 2, NH])
    rsd = rb("rsd", [P, 2, NH])
    rr = rb("rr", [P, 2, NH])
    rr_ = Region(split_at)
    gsel = rr_("gsel", [P, 2, 2, 2, B, NH])
    fa = rr_("fa", [P, S])
    fe = rr_("fe", [P, S])
    fl = rr_("fl", [P, S])
    fm = rr_("fm", [P, S])
    ls = rr_("ls", [P, S])
    fcum = rr_("fcum", [P, S])
    g = rr_("g", [P, S])
    mx = rr_("mx", [P, S])
    nmx = rr_("nmx", [P, S])
    mld = rr_("mld", [P, S])
    em = rr_("em", [P, S])
    e1 = rr_("e1", [P, P])
    wx = rr_("wx", [P, P])
    nr127 = rr_("nr127", [P, 1])
    gm = rr_("gm", [P, 2, S], F32R)
    assert rr_.at <= split_at + 16384 + 32
    ry_ = Region(rr_.at)
    rx_ = Region(yset_at)
    yh = [r(f"yh{i}", [P, KC, GN], F32R) for i, r in enumerate((rx_, ry_))]
    yl = [r(f"yl{i}", [P, KC, GN], F32R) for i, r in enumerate((rx_, ry_))]
    ybuf = [r(f"ybuf{i}", [P, KC, GN]) for i, r in enumerate((rx_, ry_))]
    assert rx_.at <= ra_top
    re_ = Region(shared_at)
    wh1 = re_("wh1", [P, 3, KC, D], F32R)
    wl1 = re_("wl1", [P, 3, KC, D], F32R)
    sil = re_("sil", [P, KC, GN])
    hbuf = re_("hbuf", [P, KC, GN])
    hh = [re_(f"hh{i}", [P, KC, GN], F32R) for i in range(2)]
    hl = [re_(f"hl{i}", [P, KC, GN], F32R) for i in range(2)]
    wh, wl = [wh0, wh1], [wl0, wl1]
    lg = re_("lg", [P, T, NE])
    pe_ = re_("pe_", [P, T, NE])
    pr = re_("pr", [P, T, NE])
    eq = re_("eq", [P, T, NE])
    kk = re_("kk", [P, T, NE])
    oh1 = re_("oh1", [P, T, NE])
    p1 = re_("p1", [P, T, NE])
    oh2 = re_("oh2", [P, T, NE])
    ge = re_("ge", [P, T, NE])
    lgt = re_("lgt", [NE, B * S])
    m1 = re_("m1", [P, T])
    m2 = re_("m2", [P, T])
    km = re_("km", [P, T])
    rw = re_("rw", [P, T])
    assert max(rs.at, rb.at, re_.at) <= nc.sbuf_usable_end, (rs.at, rb.at, re_.at)

    ps = nc.alloc_psum_tensor("ps", [P, 8, 512], F32)
    apad = nc.dram_tensor("apad", [NS, 3 * P], F32).ap()
    gd = nc.dram_tensor("gd", [2, B, NH, S], F32).ap()
    md = nc.dram_tensor("md", [2, B, NH, NH, S], F32).ap()

    names = {}

    def sem(name):
        assert name not in names
        names[name] = nc.alloc_semaphore(name)
        return names[name]

    def wait(eng, s, n):
        if not isinstance(n, int) or n > 0:
            eng.wait_ge(s, n)

    s_col, s_row, s_win, s_wb, s_wc, s_wout, s_gw, s_wr, s_cxt = (
        sem(f"loaded_{n}") for n in ("col", "row", "win", "wb", "wc", "wout", "gw", "wr", "cxt"))
    s_x = [sem(f"loaded_x{n}") for n in range(NG)]
    s_bhalf = sem("b_out_halved")
    s_p128 = sem("powers_of_128")
    s_const = sem("constants_made")
    s_ident, s_inv = sem("ident_made"), sem("inv_made")
    s_onehot = sem("onehot_made")
    s_mirror, s_mir, s_mirc = sem("mirror_made"), sem("bproj_mirrored"), sem("bproj_mirror_copied")
    s_tstep_i, s_edt, s_ea = (
        sem(n) for n in ("tstep_i", "exp_log_dt", "exp_a_log"))
    s_decay_step = sem("decay_step")
    s_neg = sem("means_negated")
    s_zp, s_zc, s_shift = sem("z_projected"), sem("z_copied"), sem("shift_r1")
    s_wc3, s_xm3 = sem("wc_split"), sem("conv_split")
    s_dmul, s_dexp, s_amean, s_am_sb, s_am_t, s_amt_sb, s_pad, s_toep = (
        sem(n) for n in ("decay_scaled", "decay_exp", "decay_summed", "decay_mean_copied", "decay_mean_t",
                         "decay_mean_t_copied", "decay_stored", "toeplitz_loaded"))
    s_dtm, s_bias, s_bin2, s_winf, s_wih, s_wil, s_woh, s_wol, s_gwc = (
        sem(n) for n in ("dt_mean_copied", "bias_summed", "bias_made", "win_scaled", "win_hi", "win_lo", "wout_hi",
                         "wout_lo", "gate_ctx_weights"))
    lns = [{k: sem(f"{k}_{i}") for k in ("stats", "aggr", "vareps", "rstd", "normed", "turned", "hi", "lo")}
           for i in range(2)]
    s_proj, s_projc, s_x2b, s_bp, s_bps, s_conv, s_xm, s_xmt, s_xmtc = (
        sem(n) for n in ("projected", "projected_copied", "x2b_made", "bproj_summed", "bproj_scaled", "conv_done",
                         "conv_copied", "conv_t", "conv_t_copied"))
    s_wcd, s_u, s_y, s_yh, s_yl, s_o, s_r, s_st1, s_ag1, s_ve1, s_rs1, s_x1, s_x1t, s_q, s_g = (
        sem(n) for n in ("mixed", "skip_added", "gated", "gated_hi", "gated_lo", "out_projected", "residual1",
                         "stats_r1", "aggr_r1", "vareps_r1", "rstd_r1", "x1_made", "x1_turned", "q_copied",
                         "gates_summed"))
    s_gc, s_gs, s_gt, s_fa, s_fe, s_fl, s_em, s_e1, s_wx, s_gh, s_gl, s_tt, s_tok, s_gmd = (
        sem(n) for n in ("gates_copied", "gates_ordered", "gates_turned", "f_abs", "f_exp", "f_ln", "exp_neg_max",
                         "carry_weight", "key_weight", "gm_hi", "gm_lo", "rows_turned", "rows_copied", "gm_stored"))
    s_row_step = sem("row_step")
    s_kz, s_vone = sem("kbd_cleared"), sem("value_ones")
    s_in = [sem(f"batch_loaded{i}") for i in range(2)]
    (s_vs, s_vm, s_vb, s_wv, s_sc, s_dec, s_c, s_st, s_sbd, s_int, s_car, s_n0, s_n1, s_sq, s_rsd, s_rr, s_hn,
     s_hw, s_r2) = (
        sem(n) for n in ("v_summed", "v_mean", "v_centred", "v_weighted", "scores_ready", "decay_done", "c_done",
                         "state_summed", "state_masked", "carry_summed", "carry_scaled", "num0_copied",
                         "num1_summed", "squared", "var_rsqrt", "head_scale", "head_normed", "head_weighted",
                         "residual2"))
    s_norm_step, s_var_step = sem("norm_step"), sem("var_step")
    s_num, s_zero, s_oneh = (
        sem(n) for n in ("numerators", "zeros_stored", "onehot_placed"))
    s_raw, s_wh, s_wl, s_wr2, s_ab, s_sil, s_h, s_hh, s_hl, s_yr, s_acc = (
        sem(n) for n in ("raw_loaded", "expert_hi", "expert_lo", "router_split", "up_ready", "silu_done",
                         "hidden_done", "hidden_hi", "hidden_lo", "down_ready", "acc_done"))
    s_lg, s_lgc, s_gate, s_pexp = sem("logits_summed"), sem("logits_copied"), sem("gating_step"), sem("router_exp")
    s_fst, s_fag, s_fve, s_frs, s_fout, s_store = (
        sem(n) for n in ("stats_out", "aggr_out", "vareps_out", "rstd_out", "out_made", "out_stored"))

    U = 4 * (NE + 1)

    def tile_ps(bank, k):
        return ps[:, bank, k * P:(k + 1) * P]

    def gate_ps(t):
        return ps[:, 6, t * 2 * NH:(t + 1) * 2 * NH]

    block_cm = nc.Block()
    with block_cm as block:

        @block.sync
        def _(sp):
            xv = x.rearrange("(t p) d -> p t d", p=P)
            sp.dma_start(col[:], cols).then_inc(s_col, 16)
            sp.dma_start(x_tm[:, 0:GT, :], xv[:, 0:GT, :]).then_inc(s_x[0], 16)
            sp.dma_start(win[:], win_t.rearrange("(c p) n -> p c n", p=P)).then_inc(s_win, 16)
            for n in range(1, NG):
                sp.dma_start(x_tm[:, n * GT:(n + 1) * GT, :], xv[:, n * GT:(n + 1) * GT, :]).then_inc(s_x[n], 16)
            sp.dma_start(wb[:], wb_t.rearrange("(c p) n -> p c n", p=P)).then_inc(s_wb, 16)
            sp.dma_start(row[:], rows.partition_broadcast(P)).then_inc(s_row, 16)
            for k in range(3):
                sp.dma_start(wc[k * NS:(k + 1) * NS, :], wc_t).then_inc(s_wc, 16)
            sp.dma_start(wout[:], wout_t.rearrange("(c p) n -> p c n", p=P)).then_inc(s_wout, 16)
            sp.dma_start(gw[:], gates_t.rearrange("(c p) n -> p c n", p=P)).then_inc(s_gw, 16)
            sp.dma_start(cx_t[:], ctx_t.rearrange("(c p) n -> p c n", p=P)).then_inc(s_cxt, 16)
            sp.dma_start(wr[:], router_t.rearrange("(c p) n -> p c n", p=P)).then_inc(s_wr, 16)
            sp.wait_ge(s_const, 1)
            sp.dma_start(apad[:, 0:P], zpad[:]).then_inc(s_pad, 16)
            sp.wait_ge(s_amt_sb, 1)
            sp.dma_start(bass.AP(apad.tensor, P, [[P, 2], [3 * P, NS], [1, P]]), amean_t[:]).then_inc(s_pad, 16)
            sp.wait_ge(s_pad, 32)
            sp.dma_start(toep[:], bass.AP(apad.tensor, 1, [[1, P], [3 * P, NS], [1, S]])).then_inc(s_toep, 16)
            sp.dma_start(raw[:], moe_w[0].rearrange("m (c p) n -> p m c n", p=P)).then_inc(s_raw, 16)

            cxv = ctx_t.rearrange("(c h p) n -> p c h n", h=HG, p=DH)
            ctv = ctx.rearrange("(t p) d -> p t d", p=P)

            def load_k(i, b):
                for h in range(HG):
                    sp.dma_start(kbd[i][h * DH:(h + 1) * DH, :, h, :], cxv[:, :, h, bass.ds(b * S, S)])\
                        .then_inc(s_in[i], 16)

            def load_ctx_q(i, b):
                sp.dma_start(ctb[i][:], ctv[:, bass.ds(b * 2, 2), :]).then_inc(s_in[i], 16)
                sp.dma_start(qb[i][:], xq_t[:, :, bass.ds(b * S, S)]).then_inc(s_in[i], 16)

            def load_gates(i, b):
                sp.dma_start(decl[i][0:2 * NH, :].bitcast(F32),
                             bass.AP(gd.tensor, b * (NH * S), [[B * NH * S, 2], [S, NH], [1, S]])).then_inc(s_in[i], 16)
                sp.dma_start(decr[i][2 * NH:, :, :].rearrange("p h n -> p (h n)").bitcast(F32),
                             bass.AP(md.tensor, b * (NH * NH * S),
                                     [[B * NH * NH * S, 2], [NH * S, NH], [1, NH * S]])).then_inc(s_in[i], 16)

            sp.wait_ge(s_kz, 2)
            sp.dma_start(md.rearrange("a b h k n -> (a b h k n)").rearrange("(p n) -> p n", p=P),
                         kbd[0][:].rearrange("p c h n -> p (c h n)")).then_inc(s_zero, 16)
            sp.wait_ge(s_zero, 16)
            for i in range(2):
                load_k(i, i)
            sp.wait_ge(s_vone, 4)
            for i in range(2):
                for half in range(2):
                    sp.dma_start(decr[i][0:2 * NH, :, half * P:(half + 1) * P].bitcast(F32), onehot_f[:])\
                        .then_inc(s_oneh, 16)
            sp.wait_ge(s_yl, KC * NG)
            sp.wait_ge(s_o, 2 * NG)
            sp.wait_ge(s_q, KC * NG)
            for i in range(2):
                load_ctx_q(i, i)
            sp.wait_ge(s_gh, 2)
            sp.wait_ge(s_gl, 2)
            sp.dma_start(gd.rearrange("a b h n -> (a b h) n"), gm[:, 0, :].bitcast(F32)).then_inc(s_gmd, 16)
            sp.dma_start(bass.AP(md.tensor, 0, [[NH * NH * S, 2 * B], [NH * S + S, NH], [1, S]]),
                         gm[:, 1, :].bitcast(F32)).then_inc(s_gmd, 16)
            sp.wait_ge(s_gmd, 32)
            for i in range(2):
                load_gates(i, i)
            with sp.Fori(0, B // 2 - 1) as it:
                for i in range(2):
                    b = it * 2 + (i + 2)
                    sp.wait_ge(s_num, it * 8 + (i * 4 + 2))
                    load_k(i, b)
                    load_ctx_q(i, b)
                    load_gates(i, b)

            for e in range(1, NE + 1):
                sp.wait_ge(s_wl, 3 * e)
                sp.dma_start(raw[:], moe_w[e].rearrange("m (c p) n -> p m c n", p=P)).then_inc(s_raw, 16)
            ov = out.rearrange("(t p) d -> p t d", p=P)
            for n in range(NG):
                sp.wait_ge(s_fout, GT * (n + 1))
                sp.dma_start(ov[:, n * GT:(n + 1) * GT, :], acc[:, n * GT:(n + 1) * GT, :]).then_inc(s_store, 16)
            sp.wait_ge(s_store, 16 * NG)

        @block.gpsimd
        def _(pool):
            gp = nc.gpsimd
            gp.memset(zpad[:], 0.0).then_inc(s_const, 1)
            gp.iota(tsteps_i[:], [[1, P]], base=0, channel_multiplier=0).then_inc(s_tstep_i, 1)
            gp.memset(pow_e[:], -0.5).then_inc(s_const, 1)
            gp.memset(ones[:], 1.0).then_inc(s_const, 1)
            gp.memset(ident[:], 0.0).then_inc(s_ident, 1)
            pool.wait_ge(s_ident, 1)
            gp.affine_select(out=ident[:], in_=ident[:], compare_op=ALU.not_equal, fill=1.0, base=0,
                             pattern=[[-1, P]], channel_multiplier=1).then_inc(s_ident, 1)
            gp.memset(mirror[:], 0.0).then_inc(s_mirror, 1)
            pool.wait_ge(s_mirror, 1)
            gp.affine_select(out=mirror[:], in_=mirror[:], compare_op=ALU.not_equal, fill=1.0, base=1 - P,
                             pattern=[[1, P]], channel_multiplier=1).then_inc(s_mirror, 1)

            def rsqrt(eps_sem, n, lo, hi, src, done):
                pool.wait_ge(eps_sem, n)
                gp.tensor_tensor(src[:, lo:hi], src[:, lo:hi], pow_e[:, 0:hi - lo], ALU.pow).then_inc(done, 1)

            pool.wait_ge(s_const, 3)
            for n in range(NG):
                rsqrt(lns[0]["vareps"], n + 1, n * GT, (n + 1) * GT, rstd, lns[0]["rstd"])
                if n == 0:
                    pool.wait_ge(s_gw, 16)
                    gp.tensor_tensor(gw_ctx[:], gw[:, KC:2 * KC, :], gw[:, 2 * KC:3 * KC, :], ALU.add)\
                        .then_inc(s_gwc, 1)
            pool.wait_ge(s_wout, 16)
            gp.tensor_copy(woh[:], wout[:]).then_inc(s_woh, 1)
            pool.wait_ge(s_woh, 1)
            gp.tensor_tensor(wol[:], wout[:], woh[:].bitcast(F32), ALU.subtract).then_inc(s_wol, 1)
            gp.memset(mask_b[:], 0.0).then_inc(s_const, 1)
            gp.memset(ident_b[:], 0.0).then_inc(s_const, 1)
            gp.memset(block_mask[:], 1.0).then_inc(s_const, 1)
            gp.memset(onehot_f[:], 0.0).then_inc(s_const, 1)
            pool.wait_ge(s_const, 7)
            gp.affine_select(out=mask_b[:], in_=mask_b[:], compare_op=ALU.is_ge, fill=MASKED, base=0,
                             pattern=[[0, HG], [1, P]], channel_multiplier=-1).then_inc(s_const, 1)
            gp.affine_select(out=ident_b[:], in_=ident_b[:], compare_op=ALU.not_equal, fill=1.0, base=0,
                             pattern=[[-1, P]], channel_multiplier=1).then_inc(s_const, 1)
            gp.affine_select(out=block_mask[:], in_=block_mask[:], compare_op=ALU.is_ge, fill=0.0, base=0,
                             pattern=[[-DH, HG], [0, DV]], channel_multiplier=1).then_inc(s_const, 1)
            pool.wait_ge(s_const, 10)
            gp.affine_select(out=block_mask[:], in_=block_mask[:], compare_op=ALU.is_ge, fill=0.0, base=DH - 1,
                             pattern=[[DH, HG], [0, DV]], channel_multiplier=-1).then_inc(s_const, 1)
            gp.affine_select(out=onehot_f[:], in_=onehot_f[:], compare_op=ALU.not_equal, fill=1.0, base=0,
                             pattern=[[-1, NH], [0, P]], channel_multiplier=1).then_inc(s_onehot, 1)
            pool.wait_ge(s_onehot, 1)
            gp.affine_select(out=onehot_f[:], in_=onehot_f[:], compare_op=ALU.not_equal, fill=1.0, base=-NH,
                             pattern=[[-1, NH], [0, P]], channel_multiplier=1).then_inc(s_onehot, 1)
            gp.iota(prio[:], [[-1, NE]], base=NE, channel_multiplier=0,
                    allow_small_or_imprecise_dtypes=True).then_inc(s_const, 1)
            pool.wait_ge(s_bhalf, 1)
            for n in range(NG):
                pool.wait_ge(lns[0]["normed"], GT * (n + 1))
                xg = x_tm[:, n * GT:(n + 1) * GT, :]
                gp.tensor_tensor(xg, xg, b_half.unsqueeze(1).broadcast_to([P, GT, D]), ALU.add).then_inc(s_x2b, 1)
            pool.wait_ge(s_conv, 1)
            for i in range(2):
                gp.memset(kbd[i][:], 0.0).then_inc(s_kz, 1)

            def root_and_shift(n):
                rsqrt(s_ve1, n + 1, n * GT, (n + 1) * GT, rstd, s_rs1)
                pool.wait_ge(s_rs1, n + 1)
                gs = slice(n * GT, (n + 1) * GT)
                pool.wait_ge(s_neg, n + 1)
                gp.tensor_tensor(shift[:, gs], shift[:, gs], rstd[:, gs], ALU.mult).then_inc(s_shift, 1)

            for n in range(NG):
                for c in range(KC):
                    pool.wait_ge(s_yh, KC * n + c + 1)
                    gp.tensor_tensor(yl[n % 2][:, c, :], ybuf[n % 2][:, c, :], yh[n % 2][:, c, :].bitcast(F32),
                                     ALU.subtract).then_inc(s_yl, 1)
                if n >= 1:
                    root_and_shift(n - 1)
            root_and_shift(NG - 1)

            pool.wait_ge(s_o, 2 * NG)
            for i in range(2):
                gp.memset(decl[i][:].bitcast(F32), 1.0).then_inc(s_vone, 1)
            for i in range(2):
                gp.memset(vb[i][:, :, :, DH:DV], 1.0).then_inc(s_vone, 1)
            split_expert(pool, gp, nc, raw, wh, wl, s_raw, s_wh, s_wl, 0)
            pool.wait_ge(s_wr, 16)
            gp.tensor_copy(wrh[:], wr[:]).then_inc(s_wr2, 1)
            pool.wait_ge(s_wr2, 1)
            gp.tensor_tensor(wrl[:], wr[:], wrh[:].bitcast(F32), ALU.subtract).then_inc(s_wr2, 1)
            pool.wait_ge(s_tok, 2)

            def values(b, i):
                pool.wait_ge(s_vm, b + 1)
                gp.tensor_tensor(vb[i][:, :, :, 0:DH],
                                 ctb[i][:, :, :].rearrange("p c (h d) -> p c h d", h=NH),
                                 vmean[:, :, :].unsqueeze(3).broadcast_to([P, 2, NH, DH]),
                                 ALU.subtract).then_inc(s_vb, 1)
                pool.wait_ge(s_vb, b + 1)
                wait(pool, s_st, b)
                gp.tensor_tensor(wv[:], vb[i][:, 0, :, :],
                                 tok[:, 3, bass.ds(b * NH, NH)].unsqueeze(2).broadcast_to([P, NH, DV]),
                                 ALU.mult).then_inc(s_wv, 1)

            def head_root(b):
                pool.wait_ge(s_var_step, b * 3 + 3)
                gp.tensor_tensor(rsd[:].rearrange("p a h -> p (a h)"), var[:].rearrange("p a h -> p (a h)"),
                                 pow_e[:, 0:2 * NH], ALU.pow).then_inc(s_rsd, 1)

            def residual(b):
                pool.wait_ge(s_hn, b + 1)
                hnv = hn[:].rearrange("p a h d -> p a (h d)")
                gp.tensor_tensor(hnv, hnv, norm_w_row.unsqueeze(1).broadcast_to([P, 2, D]), ALU.mult)\
                    .then_inc(s_hw, 1)
                pool.wait_ge(s_hw, b + 1)
                gp.tensor_tensor(x_tm[:, bass.ds(b * 2, 2), :], hnv, x1[:, bass.ds(b * 2, 2), :],
                                 ALU.add).then_inc(s_r2, 1)

            values(0, 0)
            values(1, 1)

            def pool_step(b, i, last=False):
                head_root(b - 1)
                if not last:
                    values(b + 1, 1 - i)
                residual(b - 1)

            with pool.Fori(0, B // 2 - 1) as it:
                pool_step(it * 2 + 1, 1)
                pool_step(it * 2 + 2, 0)
            pool_step(B - 1, 1, last=True)
            for n in range(2):
                rsqrt(lns[1]["vareps"], n + 1, n * GT, (n + 1) * GT, rstd, lns[1]["rstd"])
            head_root(B - 1)
            rsqrt(lns[1]["vareps"], 3, 2 * GT, 3 * GT, rstd, lns[1]["rstd"])
            residual(B - 1)

            rsqrt(lns[1]["vareps"], 4, 3 * GT, 4 * GT, rstd, lns[1]["rstd"])
            for u in range(U):
                e, n = divmod(u, 4)
                for f in range(KC):
                    pool.wait_ge(s_hh, KC * u + f + 1)
                    wait(pool, s_yr, 2 * (u - 1))
                    gp.tensor_tensor(hl[u % 2][:, f, :], hbuf[:, f, :], hh[u % 2][:, f, :].bitcast(F32),
                                     ALU.subtract).then_inc(s_hl, 1)
                if n == 1 and e < NE:
                    wait(pool, s_yr, 2 * 4 * e)
                    split_expert(pool, gp, nc, raw, wh, wl, s_raw, s_wh, s_wl, e + 1)
                if e == NE and n >= 1:
                    rsqrt(s_fve, n, (n - 1) * GT, n * GT, rstd, s_frs)
            rsqrt(s_fve, NG, T - GT, T, rstd, s_frs)

        @block.scalar
        def _(act):
            sc = nc.scalar
            act.wait_ge(s_col, 16)
            sc.activation(dt[:], col[:, C_LOGDT:C_LOGDT + KC], ACT.Exp).then_inc(s_edt, 1)
            act.wait_ge(s_decay_step, 1)
            sc.activation(log_a[:], log_a[:], ACT.Exp).then_inc(s_ea, 1)
            act.wait_ge(s_decay_step, 4)
            sc.activation(half_pow[:, :, :, 1], log_a[:], ACT.Exp, scale=float(P)).then_inc(s_p128, 1)

            def powers(q):
                act.wait_ge(s_dmul, q + 1)
                v = decay_pow[:, 4 * q:4 * q + 4, :, :]
                sc.activation(v, v, ACT.Exp).then_inc(s_dexp, 1)

            def hi_parts(ln, n, first_bank, after=None):
                for c in range(KC):
                    act.wait_ge(ln["turned"], KC * n + c + 1)
                    sc.activation(xh[:, c, n * GN:(n + 1) * GN], ps[:, first_bank + c, :], ACT.Copy)\
                        .then_inc(ln["hi"], 1)

            def x_proj(n):
                for j in range(KC):
                    act.wait_ge(s_proj, KC * n + j + 1)
                    act.wait_ge(s_bin2, 1)
                    sc.activation(xq_t[:, j, n * GN:(n + 1) * GN], ps[:, 2 + j, :], ACT.Identity,
                                  bias=b_in2[:, j:j + 1]).then_inc(s_projc, 1)

            def gate_z(n, c):
                act.wait_ge(s_zp, KC * n + c + 1)
                sc.activation(z_t[:, c, n * GN:(n + 1) * GN], ps[:, 4 + c, :], ACT.Silu,
                              bias=b_in2[:, KC + c:KC + c + 1]).then_inc(s_zc, 1)

            powers(0)
            powers(1)
            act.wait_ge(s_winf, KC)
            sc.activation(wih[:], win[:], ACT.Copy).then_inc(s_wih, 1)
            act.wait_ge(s_bias, 1)
            sc.activation(dt_mean[:], ps[:, 7, 32:33], ACT.Copy).then_inc(s_dtm, 1)
            hi_parts(lns[0], 0, 0)
            powers(2)
            hi_parts(lns[0], 1, 4)
            powers(3)
            x_proj(0)
            hi_parts(lns[0], 2, 0)
            act.wait_ge(s_amean, 1)
            sc.activation(amean[:], ps[:, 7, 0:2 * NS], ACT.Copy).then_inc(s_am_sb, 1)
            x_proj(1)
            act.wait_ge(s_am_t, 1)
            sc.activation(amean_t[:], ps[0:2 * NS, 7, 64:64 + P], ACT.Copy).then_inc(s_amt_sb, 1)
            hi_parts(lns[0], 3, 4)
            x_proj(2)
            x_proj(3)
            gate_z(0, 0)
            gate_z(0, 1)
            act.wait_ge(s_mir, 1)
            sc.activation(bmir[:].rearrange("p c s b -> p (c s b)"), ps[:, 0, 0:2 * NS * B], ACT.Copy)\
                .then_inc(s_mirc, 1)
            gate_z(1, 0)
            gate_z(1, 1)
            gate_z(2, 0)
            gate_z(2, 1)
            act.wait_ge(s_conv, 1)
            sc.activation(xmh[:].rearrange("p c s b -> p (c s b)"), ps[:, 1, 0:2 * NS * B], ACT.Copy).then_inc(s_xm, 1)
            act.wait_ge(s_xm, 1)
            for k in (0, 2):
                sc.activation(xm3[:, :, k, :, :].rearrange("p c s b -> p c (s b)"),
                              xmh[:].bitcast(F32).rearrange("p c s b -> p c (s b)"), ACT.Copy).then_inc(s_xm, 1)
            gate_z(3, 0)
            gate_z(3, 1)
            for n in range(NG):
                act.wait_ge(s_xmt, n + 1)
                sc.activation(xm_t[:, n * GN:(n + 1) * GN], ps[0:3 * NS, n, :], ACT.Copy).then_inc(s_xmtc, 1)
            for n in range(NG + 2):
                if n < NG:
                    for c in range(KC):
                        act.wait_ge(s_y, KC * n + c + 1)
                        wait(act, s_o, 2 * (n - 1))
                        sc.activation(yh[n % 2][:, c, :], ybuf[n % 2][:, c, :], ACT.Copy).then_inc(s_yh, 1)
                if n >= 2:
                    act.wait_ge(s_shift, n - 1)
                    for t in range((n - 2) * GT, (n - 1) * GT):
                        sc.activation(x1[:, t, :], x_tm[:, t, :], ACT.Identity, bias=shift[:, t:t + 1],
                                      scale=rstd[:, t:t + 1]).then_inc(s_x1, 1)
                    for c in range(KC):
                        act.wait_ge(s_x1t, KC * (n - 2) + c + 1)
                        sc.activation(xq_t[:, c, (n - 2) * GN:(n - 1) * GN], ps[:, c, :], ACT.Copy).then_inc(s_q, 1)

            act.wait_ge(s_g, NG)
            sc.activation(small[:].rearrange("p t g -> p (t g)"), ps[:, 6, 0:T * 2 * NH], ACT.Copy)\
                .then_inc(s_gc, 1)
            act.wait_ge(s_gt, 1)
            sc.activation(fa[:], ps[:, 7, S:2 * S], ACT.Abs, bias=col[:, C_GB + 1:C_GB + 2]).then_inc(s_fa, 1)
            act.wait_ge(s_fa, 1)
            sc.activation(fe[:], fa[:], ACT.Exp, scale=-1.0).then_inc(s_fe, 1)
            act.wait_ge(s_fe, 1)
            sc.activation(fl[:], fe[:], ACT.Ln, bias=1.0).then_inc(s_fl, 1)
            act.wait_ge(s_row_step, 6)
            sc.activation(wx[:], g[:, 0:P], ACT.Exp, bias=nr127[:, 0:1]).then_inc(s_wx, 1)
            act.wait_ge(s_row_step, 5)
            sc.activation(e1[:], mx[:, P:S], ACT.Exp, scale=-1.0, bias=mx[:, P - 1:P]).then_inc(s_e1, 1)
            act.wait_ge(s_row_step, 8)
            sc.activation(em[:], mld[:], ACT.Exp, scale=-1.0).then_inc(s_em, 1)

            def act_step(b, i, first=False):
                def decay(gi):
                    g_ = b * 4 + gi
                    act.wait_ge(s_sc, g_ + 1)
                    wait(act, s_c, g_ - 1)
                    sc.activation(dec[:, gi % 2, :, :].rearrange("p h s -> p (h s)"), ps[:, gi % 2, :],
                                  ACT.Exp).then_inc(s_dec, 1)
                decay(0)
                decay(1)
                if not first:
                    square(b - 1, 1 - i)
                decay(2)
                decay(3)
                act.wait_ge(s_num, b * 4 + 2)
                sc.activation(nm[i][:, 0, :, :].rearrange("p h d -> p (h d)"), ps[:, 4, 0:NH * DV],
                              ACT.Copy).then_inc(s_n0, 1)

            def square(b, i):
                act.wait_ge(s_n0, b + 1)
                act.wait_ge(s_n1, b + 1)
                sc.activation(sq[:], nm[i][:, :, :, 0:DH], ACT.Square).then_inc(s_sq, 1)

            act_step(0, 0, first=True)
            with act.Fori(0, B // 2 - 1) as it:
                act_step(it * 2 + 1, 1)
                act_step(it * 2 + 2, 0)
            act_step(B - 1, 1)
            hi_parts(lns[1], 0, 6)
            square(B - 1, 1)

            def silu(u):
                for f in range(KC):
                    act.wait_ge(s_ab, KC * u + f + 1)
                    wait(act, s_h, KC * (u - 1) + f + 1)
                    sc.activation(sil[:, f, :], ps[:, 2 * f, :], ACT.Silu).then_inc(s_sil, 1)
                    act.wait_ge(s_h, KC * u + f + 1)
                    wait(act, s_yr, 2 * (u - 1))
                    sc.activation(hh[u % 2][:, f, :], hbuf[:, f, :], ACT.Copy).then_inc(s_hh, 1)

            hi_parts(lns[1], 1, 4)
            silu(0)
            hi_parts(lns[1], 2, 6)
            hi_parts(lns[1], 3, 6)
            for u in range(1, U):
                silu(u)
                if u == 3:
                    for n in range(NG):
                        act.wait_ge(s_lg, n + 1)
                        sc.activation(lgt[:, n * GN:(n + 1) * GN], ps[0:NE, 6 + n % 2, :], ACT.Copy)\
                            .then_inc(s_lgc, 1)
                elif u == 4:
                    act.wait_ge(s_gate, 1)
                    sc.activation(pe_[:], lg[:], ACT.Exp, scale=-1.0).then_inc(s_pexp, 1)

        @block.vector
        def _(dve):
            v = nc.vector

            def moments(n, src, sems, negate=False):
                st, ag, ve, rs_ = sems
                for t in range(n * GT, (n + 1) * GT):
                    v.bn_stats(stats[:, t, :], src[:, t, :]).then_inc(st, 1)
                for t in range(n * GT, (n + 1) * GT):
                    dve.wait_ge(st, t + 1)
                    v.bn_aggr(mv[:, t, :], stats[:, t, :]).then_inc(ag, 1)
                dve.wait_ge(ag, (n + 1) * GT)
                if negate:
                    v.tensor_scalar(shift[:, n * GT:(n + 1) * GT], mv[:, n * GT:(n + 1) * GT, 0], -1.0, None, ALU.mult)\
                        .then_inc(s_neg, 1)
                v.tensor_scalar(rstd[:, n * GT:(n + 1) * GT], mv[:, n * GT:(n + 1) * GT, 1], EPS, None,
                                ALU.add).then_inc(ve, 1)

            def normalise(n, src, sems, done_norm, dst):
                dve.wait_ge(sems[3], n + 1)
                for t in range(n * GT, (n + 1) * GT):
                    v.tensor_scalar(dst(t), src[:, t, :], mv[:, t, 0:1], rstd[:, t:t + 1],
                                    ALU.subtract, ALU.mult).then_inc(done_norm, 1)

            def stats_of(n, src, sems, done_norm, dst):
                moments(n, src, sems)
                normalise(n, src, sems, done_norm, dst)

            v.memset(inv_d[:], 1.0 / D).then_inc(s_inv, 1)
            dve.wait_ge(s_col, 16)
            v.tensor_scalar(log_a[:], col[:, C_ALOG:C_ALOG + KC * NS].rearrange("p (c s) -> p c s", c=KC),
                            80.0, None, ALU.min).then_inc(s_decay_step, 1)
            dve.wait_ge(s_edt, 1)
            v.tensor_scalar(dt[:], dt[:], 1e-4, 1.0, ALU.max, ALU.min).then_inc(s_decay_step, 1)
            dve.wait_ge(s_decay_step, 2)
            dve.wait_ge(s_ea, 1)
            v.tensor_tensor(log_a[:], log_a[:], dt[:].unsqueeze(2).broadcast_to([P, KC, NS]), ALU.mult)\
                .then_inc(s_decay_step, 1)
            dve.wait_ge(s_decay_step, 3)
            v.tensor_scalar(log_a[:], log_a[:], LOG_FLOOR, -1.0, ALU.min, ALU.mult).then_inc(s_decay_step, 1)
            dve.wait_ge(s_tstep_i, 1)
            v.tensor_copy(tsteps[:], tsteps_i[:]).then_inc(s_decay_step, 1)
            dve.wait_ge(s_decay_step, 5)
            v.memset(half_pow[:, :, :, 0], 1.0 / D).then_inc(s_inv, 1)

            def exponents(q):
                dims = [P, 4, KC, P]
                v.tensor_tensor(decay_pow[:, 4 * q:4 * q + 4, :, :],
                                tsteps[:].unsqueeze(1).unsqueeze(1).broadcast_to(dims),
                                log_a[:, :, 4 * q:4 * q + 4].rearrange("p c s -> p s c").unsqueeze(3)
                                .broadcast_to(dims), ALU.mult).then_inc(s_dmul, 1)

            def lo_parts(ln, n, first_bank):
                for c in range(KC):
                    dve.wait_ge(ln["hi"], KC * n + c + 1)
                    v.tensor_tensor(xl[:, c, n * GN:(n + 1) * GN], ps[:, first_bank + c, :],
                                    xh[:, c, n * GN:(n + 1) * GN].bitcast(F32), ALU.subtract)\
                        .then_inc(ln["lo"], 1)

            ln = lns[0]
            ln1_sems = (ln["stats"], ln["aggr"], ln["vareps"], ln["rstd"])

            def moments1(n):
                dve.wait_ge(s_x[n], 16)
                moments(n, x_tm, ln1_sems)

            def normalise1(n):
                normalise(n, x_tm, ln1_sems, ln["normed"], lambda t: x1[:, t, :])

            exponents(0)
            moments1(0)
            exponents(1)
            normalise1(0)
            dve.wait_ge(s_p128, 1)
            v.tensor_scalar(half_pow[:, :, :, 1], half_pow[:, :, :, 1], 1.0 / D, None, ALU.mult)\
                .then_inc(s_decay_step, 1)
            dve.wait_ge(s_win, 16)
            dve.wait_ge(s_bias, 1)
            v.tensor_tensor(b_in2[:], ps[:, 7, 200:204], col[:, C_BIN:C_BIN + 4], ALU.add).then_inc(s_bin2, 1)
            for c in range(KC):
                v.tensor_scalar(win[:, c, :], win[:, c, :], col[:, C_LNG + c:C_LNG + c + 1], None, ALU.mult)\
                    .then_inc(s_winf, 1)
            moments1(1)
            dve.wait_ge(s_wih, 1)
            v.tensor_tensor(wil[:], win[:], wih[:].bitcast(F32), ALU.subtract).then_inc(s_wil, 1)
            exponents(2)
            lo_parts(ln, 0, 0)
            normalise1(1)
            exponents(3)
            moments1(2)
            lo_parts(ln, 1, 4)
            normalise1(2)
            moments1(3)
            normalise1(3)
            lo_parts(ln, 2, 0)
            dve.wait_ge(s_row, 16)
            v.tensor_scalar(b_half, b_out_row, 0.5, None, ALU.mult).then_inc(s_bhalf, 1)
            lo_parts(ln, 3, 4)
            dve.wait_ge(s_wc, 3 * 16)
            v.tensor_copy(wc3[:], wc[:]).then_inc(s_wc3, 1)
            dve.wait_ge(s_wc3, 1)
            lo = slice(2 * NS, 3 * NS)
            v.tensor_tensor(wc3[lo, :], wc[lo, :], wc3[lo, :].bitcast(F32), ALU.subtract).then_inc(s_wc3, 1)
            dve.wait_ge(s_bp, NG)
            dve.wait_ge(s_dtm, 1)
            v.tensor_scalar(bproj[:].rearrange("p c s b -> p (c s b)"), ps[:, 7, 2 * NS * B:4 * NS * B], dt_mean[:, 0:1],
                            None, ALU.mult).then_inc(s_bps, 1)
            dve.wait_ge(s_xm, 1)
            v.tensor_tensor(xm3[:, :, 1, :, :].rearrange("p c s b -> p c (s b)"),
                            ps[:, 1, 0:2 * NS * B].rearrange("p (c n) -> p c n", c=2),
                            xmh[:].bitcast(F32).rearrange("p c s b -> p c (s b)"), ALU.subtract).then_inc(s_xm3, 1)
            dve.wait_ge(s_zp, KC * NG)
            dve.wait_ge(s_zc, KC * NG)
            r1_sems = (s_st1, s_ag1, s_ve1, s_rs1)
            for n in range(NG + 1):
                if n < NG:
                    yb = ybuf[n % 2]
                    for c in range(KC):
                        sl = slice(n * GN, (n + 1) * GN)
                        dve.wait_ge(s_wcd, KC * n + c + 1)
                        wait(dve, s_yl, KC * (n - 2) + c + 1)
                        v.scalar_tensor_tensor(yb[:, c, :], xq_t[:, c, sl], col[:, C_DSKIP + c:C_DSKIP + c + 1],
                                               ps[:, 4 + c, :], ALU.mult, ALU.add).then_inc(s_u, 1)
                    for c in range(KC):
                        dve.wait_ge(s_u, KC * n + c + 1)
                        v.tensor_tensor(yb[:, c, :], yb[:, c, :], z_t[:, c, n * GN:(n + 1) * GN], ALU.mult)\
                            .then_inc(s_y, 1)
                if n >= 1:
                    m = n - 1
                    dve.wait_ge(s_x2b, m + 1)
                    for k in range(2):
                        dve.wait_ge(s_o, 2 * m + k + 1)
                        xt = x_tm[:, m * GT + 2 * k:m * GT + 2 * k + 2, :].rearrange("p t d -> p (t d)")
                        v.scalar_tensor_tensor(xt, xt, 2.0, ps[:, 2 + k, :], ALU.mult, ALU.add).then_inc(s_r, 1)
                    dve.wait_ge(s_r, 2 * n)
                    moments(m, x_tm, r1_sems, negate=True)

            dve.wait_ge(s_gc, 1)
            gv = small[:].rearrange("p (b c) (i h) -> p c i b h", c=2, i=2)
            for c in range(2):
                for dup in range(2):
                    v.tensor_copy(gsel[:, c, :, dup, :, :], gv[:, c, :, :, :]).then_inc(s_gs, 1)
            dve.wait_ge(s_gt, 1)
            dve.wait_ge(s_fa, 1)
            v.tensor_scalar(fm[:], ps[:, 7, S:2 * S], col[:, C_GB + 1:C_GB + 2], 0.0, ALU.add, ALU.min)\
                .then_inc(s_row_step, 1)
            dve.wait_ge(s_row_step, 1)
            dve.wait_ge(s_fl, 1)
            v.tensor_tensor(ls[:], fm[:], fl[:], ALU.subtract).then_inc(s_row_step, 1)
            dve.wait_ge(s_row_step, 2)
            v.tensor_tensor_scan(fcum[:], ones[:], ls[:], 0.0, ALU.mult, ALU.add).then_inc(s_row_step, 1)
            dve.wait_ge(s_row_step, 3)
            v.scalar_tensor_tensor(g[:], ps[:, 7, 0:S], col[:, C_GB:C_GB + 1], fcum[:], ALU.add, ALU.subtract)\
                .then_inc(s_row_step, 1)
            dve.wait_ge(s_row_step, 4)
            v.tensor_tensor_scan(mx[:], g[:], g[:], -3e38, ALU.max, ALU.max).then_inc(s_row_step, 1)
            dve.wait_ge(s_row_step, 5)
            v.tensor_scalar(nr127[:], mx[:, P - 1:P], -1.0, None, ALU.mult).then_inc(s_row_step, 1)
            v.tensor_scalar(nmx[:], mx[:], -1.0, None, ALU.mult).then_inc(s_row_step, 1)
            v.tensor_tensor(mld[:], fcum[:], mx[:], ALU.add).then_inc(s_row_step, 1)
            v.tensor_copy(gm[:, 0, :], g[:]).then_inc(s_gh, 1)
            dve.wait_ge(s_row_step, 7)
            v.tensor_copy(gm[:, 1, :], nmx[:]).then_inc(s_gh, 1)
            dve.wait_ge(s_gh, 2)
            H = B * NH
            v.tensor_tensor(gm[H:, 0, :], g[H:, :], gm[H:, 0, :].bitcast(F32), ALU.subtract).then_inc(s_gl, 1)
            v.tensor_tensor(gm[H:, 1, :], nmx[H:, :], gm[H:, 1, :].bitcast(F32), ALU.subtract).then_inc(s_gl, 1)
            dve.wait_ge(s_tt, 1)
            v.tensor_copy(tok[:, 0:3, :].rearrange("p k r -> p (k r)"), ps[:, 6, 0:3 * H]).then_inc(s_tok, 1)
            v.tensor_scalar(tok[:, 3, :], ps[:, 6, 3 * H:4 * H], QK_SCALE, None, ALU.mult).then_inc(s_tok, 1)

            def head_means(b, i):
                dve.wait_ge(s_in[i], (b + (2 - i)) * (B * 8) if not isinstance(b, int) else 128 * (b // 2 + 1))
                wait(dve, s_vm, b)
                v.tensor_reduce(vsum[:], ctb[i][:].rearrange("p c (h d) -> p c h d", h=NH), X, ALU.add)\
                    .then_inc(s_vs, 1)
                dve.wait_ge(s_vs, b + 1)
                wait(dve, s_vb, b)
                v.tensor_scalar(vmean[:], vsum[:], 1.0 / DH, None, ALU.mult).then_inc(s_vm, 1)

            def decayed(b, gi):
                g_ = b * 4 + gi
                dve.wait_ge(s_dec, g_ + 1)
                wait(dve, s_num, g_ - 3)
                v.scalar_tensor_tensor(cmat[:, gi, :, :].rearrange("p h s -> p (h s)"),
                                       ps[:, 2 + gi % 2, :], QK_SCALE,
                                       dec[:, gi % 2, :, :].rearrange("p h s -> p (h s)"),
                                       ALU.mult, ALU.mult).then_inc(s_c, 1)

            def mask_state(b):
                dve.wait_ge(s_st, b + 1)
                wait(dve, s_int, b)
                v.tensor_tensor(state[:].rearrange("p c h d -> p c (h d)"),
                                ps[:, 7, 0:2 * HG * DV].rearrange("p (c n) -> p c n", c=KC),
                                block_mask[:].rearrange("p h d -> p (h d)").unsqueeze(1)
                                .broadcast_to([P, KC, HG * DV]), ALU.mult).then_inc(s_sbd, 1)

            def carried(b):
                dve.wait_ge(s_int, b + 1)
                v.tensor_tensor(carry[:], ps[:, 6, 0:NH * DV].rearrange("p (h d) -> p h d", h=NH),
                                tok[:, 2, bass.ds(b * NH, NH)].unsqueeze(2).broadcast_to([P, NH, DV]),
                                ALU.mult).then_inc(s_car, 1)

            def normaliser(b, i):
                dve.wait_ge(s_car, b + 1)
                dve.wait_ge(s_num, b * 4 + 4)
                v.tensor_tensor(nm[i][:, 1, :, :].rearrange("p h d -> p (h d)"), ps[:, 5, 0:NH * DV],
                                carry[:].rearrange("p h d -> p (h d)"), ALU.add).then_inc(s_n1, 1)
                dve.wait_ge(s_n1, b + 1)
                dve.wait_ge(s_n0, b + 1)
                v.tensor_tensor(nrm[:], nm[i][:, :, :, DH], tok[:, 0:2, bass.ds(b * NH, NH)], ALU.max)\
                    .then_inc(s_norm_step, 1)
                dve.wait_ge(s_norm_step, b * 5 + 1)
                v.scalar_tensor_tensor(nrm[:], nm[i][:, :, :, DH], -1.0, nrm[:], ALU.mult, ALU.max)\
                    .then_inc(s_norm_step, 1)
                dve.wait_ge(s_norm_step, b * 5 + 2)
                v.tensor_scalar(nrm[:], nrm[:], 1e-6, None, ALU.add).then_inc(s_norm_step, 1)
                dve.wait_ge(s_norm_step, b * 5 + 3)
                v.reciprocal(rec[:], nrm[:]).then_inc(s_norm_step, 1)
                dve.wait_ge(s_norm_step, b * 5 + 4)
                v.tensor_tensor(rec2[:], rec[:], rec[:], ALU.mult).then_inc(s_norm_step, 1)

            def variance(b):
                dve.wait_ge(s_sq, b + 1)
                v.tensor_reduce(ssum[:], sq[:], X, ALU.add).then_inc(s_var_step, 1)
                dve.wait_ge(s_var_step, b * 3 + 1)
                dve.wait_ge(s_norm_step, b * 5 + 5)
                v.tensor_tensor(ssum[:], ssum[:], rec2[:], ALU.mult).then_inc(s_var_step, 1)
                dve.wait_ge(s_var_step, b * 3 + 2)
                v.tensor_scalar(var[:], ssum[:], 1.0 / DH, EPS, ALU.mult, ALU.add).then_inc(s_var_step, 1)

            def head_norm(b, i):
                dve.wait_ge(s_rsd, b + 1)
                v.tensor_tensor(rr[:], rsd[:], rec[:], ALU.mult).then_inc(s_rr, 1)
                dve.wait_ge(s_rr, b + 1)
                v.tensor_tensor(hn[:], nm[i][:, :, :, 0:DH], rr[:].unsqueeze(3).broadcast_to([P, 2, NH, DH]),
                                ALU.mult).then_inc(s_hn, 1)

            def dve_step(b, i, first=False, last=False):
                decayed(b, 0)
                decayed(b, 1)
                if not first:
                    normaliser(b - 1, 1 - i)
                mask_state(b)
                decayed(b, 2)
                if not first:
                    variance(b - 1)
                decayed(b, 3)
                carried(b)
                if not last and not first:
                    head_means(b + 1, 1 - i)
                if not first:
                    head_norm(b - 1, 1 - i)

            dve.wait_ge(s_tok, 2)
            head_means(0, 0)
            head_means(1, 1)
            dve_step(0, 0, first=True)
            with dve.Fori(0, B // 2 - 1) as it:
                dve_step(it * 2 + 1, 1)
                dve_step(it * 2 + 2, 0)
            dve_step(B - 1, 1, last=True)

            ln = lns[1]
            ln_sems = (ln["stats"], ln["aggr"], ln["vareps"], ln["rstd"])

            def moments2(n):
                dve.wait_ge(s_r2, 2 * (n + 1))
                moments(n, x_tm, ln_sems)

            def normalise2(n):
                normalise(n, x_tm, ln_sems, ln["normed"], lambda t: acc[:, t, :])

            def hidden(u):
                for f in range(KC):
                    dve.wait_ge(s_sil, KC * u + f + 1)
                    wait(dve, s_hl, KC * (u - 1) + f + 1)
                    v.tensor_tensor(hbuf[:, f, :], sil[:, f, :], ps[:, 2 * f + 1, :], ALU.mult).then_inc(s_h, 1)

            def accumulate(u):
                e, n = divmod(u, 4)
                for k in range(GT):
                    t = n * GT + k
                    dve.wait_ge(s_yr, 2 * u + k // 2 + 1)
                    y = ps[:, 4 + k // 2, (k % 2) * D:(k % 2 + 1) * D]
                    if e == 0:
                        v.tensor_tensor(acc[:, t, :], y, acc[:, t, :], ALU.add).then_inc(s_acc, 1)
                    else:
                        dve.wait_ge(s_acc, GT * (u - 4) + k + 1)
                        v.scalar_tensor_tensor(acc[:, t, :], y, ge[:, t, e - 1:e], acc[:, t, :],
                                               ALU.mult, ALU.add).then_inc(s_acc, 1)
                if e == NE:
                    dve.wait_ge(s_acc, GT * (u + 1))
                    stats_of(n, acc, (s_fst, s_fag, s_fve, s_frs), s_fout, lambda t: acc[:, t, :])

            bc = [P, T, NE]
            step = [0]

            def then(ins):
                step[0] += 1
                ins.then_inc(s_gate, 1)
                dve.wait_ge(s_gate, step[0])

            def add_gate_bias():
                dve.wait_ge(s_lg, NG + 1)
                then(v.tensor_tensor(lg[:], ps[:, 7, 0:T * NE].rearrange("p (t e) -> p t e", t=T),
                                     gate_b_row.unsqueeze(1).broadcast_to(bc), ALU.add))

            def gating():
                dve.wait_ge(s_pexp, 1)
                then(v.tensor_scalar(pe_[:], pe_[:], 1.0, None, ALU.add))
                then(v.reciprocal(pr[:], pe_[:]))

                def pick(p, m, onehot_out):
                    then(v.tensor_reduce(m[:], p[:], X, ALU.max))
                    then(v.tensor_tensor(eq[:], p[:], m[:].unsqueeze(2).broadcast_to(bc), ALU.is_equal))
                    then(v.tensor_tensor(kk[:], eq[:], prio[:].unsqueeze(1).broadcast_to(bc), ALU.mult))
                    then(v.tensor_reduce(km[:], kk[:], X, ALU.max))
                    then(v.tensor_tensor(onehot_out[:], kk[:], km[:].unsqueeze(2).broadcast_to(bc), ALU.is_equal))

                pick(pr, m1, oh1)
                then(v.scalar_tensor_tensor(p1[:], oh1[:], -2.0, pr[:], ALU.mult, ALU.add))
                pick(p1, m2, oh2)
                then(v.tensor_tensor(oh1[:], oh1[:], oh2[:], ALU.add))
                then(v.tensor_tensor(oh1[:], oh1[:], pr[:], ALU.mult))
                then(v.tensor_tensor(m1[:], m1[:], m2[:], ALU.add))
                then(v.tensor_scalar(m1[:], m1[:], 1e-8, None, ALU.add))
                then(v.reciprocal(rw[:], m1[:]))
                then(v.tensor_tensor(ge[:], oh1[:], rw[:].unsqueeze(2).broadcast_to(bc), ALU.mult))

            moments2(0)
            moments2(1)
            normalise2(0)
            normalise2(1)
            lo_parts(ln, 0, 6)
            normaliser(B - 1, 1)
            lo_parts(ln, 1, 4)
            variance(B - 1)
            moments2(2)
            head_norm(B - 1, 1)
            normalise2(2)
            hidden(0)
            moments2(3)
            lo_parts(ln, 2, 6)
            normalise2(3)
            hidden(1)
            accumulate(0)
            lo_parts(ln, 3, 6)
            for u in range(2, U):
                hidden(u)
                if u == 4:
                    add_gate_bias()
                elif u == 5:
                    gating()
                accumulate(u - 1)
            accumulate(U - 1)

        @block.tensor
        def _(pe):
            te = nc.tensor

            def three(out_, wh_, wl_, rh_, rl_, first, last):
                te.matmul(out_, wh_, rh_, start=first, stop=False)
                te.matmul(out_, wl_, rh_, start=False, stop=False)
                return te.matmul(out_, wh_, rl_, start=False, stop=last)

            pe.wait_ge(s_ident, 2)
            pe.wait_ge(s_inv, 1)
            pe.wait_ge(s_decay_step, 2)
            for c in range(KC):
                te.matmul(ps[:, 7, 32:33], inv_d[:], dt[:, c:c + 1], start=c == 0, stop=c == KC - 1)
            pe.wait_ge(s_win, 16)
            for j in range(4):
                for c in range(KC):
                    last = te.matmul(ps[:, 7, 200 + j:201 + j], win[:, c, j * P:(j + 1) * P],
                                     col[:, C_LNB + c:C_LNB + c + 1], start=c == 0, stop=c == KC - 1)
            last.then_inc(s_bias, 1)

            def turn(lnx, n, src, first_bank, banks_read):
                pe.wait_ge(lnx["normed"], GT * (n + 1))
                wait(pe, lnx["lo"], banks_read)
                for c in range(KC):
                    for k in range(GT):
                        last_ = te.transpose(tile_ps(first_bank + c, k), src[:, n * GT + k, c * P:(c + 1) * P],
                                             ident[:])
                    last_.then_inc(lnx["turned"], 1)

            def project(n, j, c):
                sl = slice(n * GN, (n + 1) * GN)
                return three(ps[:, 2 + j, :], wih[:, c, j * P:(j + 1) * P], wil[:, c, j * P:(j + 1) * P],
                             xh[:, c, sl], xl[:, c, sl], c == 0, c == KC - 1)

            def project_x(n, j):
                pe.wait_ge(lns[0]["lo"], KC * (n + 1))
                pe.wait_ge(s_wil, 1)
                wait(pe, s_projc, KC * (n - 1) + j + 1)
                for c in range(KC):
                    last_ = project(n, j, c)
                last_.then_inc(s_proj, 1)

            def project_z(n, j, c):
                pe.wait_ge(lns[0]["lo"], KC * NG)
                wait(pe, s_zc, KC * (n - 1) + j + 1)
                last_ = project(n, KC + j, c)
                if c == KC - 1:
                    last_.then_inc(s_zp, 1)

            def b_proj(t):
                pe.wait_ge(s_projc, KC * (t // GT + 1))
                pe.wait_ge(s_wb, 16)
                pe.wait_ge(s_amt_sb, 1)
                o = 2 * NS * B + (t % 2) * NS * B + t // 2
                for c in range(KC):
                    last_ = te.matmul(ps[:, 7, o:o + (NS - 1) * B + 1:B], xq_t[:, c, t * P:(t + 1) * P], wb[:, c, :],
                                      start=c == 0, stop=c == KC - 1)
                if t % GT == GT - 1:
                    last_.then_inc(s_bp, 1)

            def decay_sums(first, last):
                for s in range(first, last):
                    pe.wait_ge(s_dexp, s // 4 + 1)
                    for c in range(KC):
                        last_ = te.matmul(ps[:, 7, s:s + 2 * NS:NS], decay_pow[:, s, c, :], half_pow[:, c, s, :],
                                          start=c == 0, stop=c == KC - 1)
                return last_

            def context_gates(t):
                pe.wait_ge(s_gwc, 1)
                pe.wait_ge(s_cxt, 16)
                for c in range(KC):
                    te.matmul(gate_ps(t), cx_t[:, c, t * P:(t + 1) * P], gw_ctx[:, c, :],
                              start=t == 0 and c == 0, stop=False)

            turn(lns[0], 0, x1, 0, 0)
            pe.wait_ge(s_bin2, 1)
            pe.wait_ge(s_dtm, 1)
            pe.wait_ge(s_decay_step, 6)
            pe.wait_ge(s_inv, 2)
            decay_sums(0, 4)
            project_x(0, 0)
            turn(lns[0], 1, x1, 4, 0)
            decay_sums(4, 8)
            project_x(0, 1)
            decay_sums(8, 12)
            project_x(1, 0)
            turn(lns[0], 2, x1, 0, KC)
            decay_sums(12, NS).then_inc(s_amean, 1)
            project_x(1, 1)
            pe.wait_ge(s_am_sb, 1)
            te.transpose(ps[0:2 * NS, 7, 64:64 + P], amean[:], ident[:]).then_inc(s_am_t, 1)
            turn(lns[0], 3, x1, 4, KC * 2)
            context_gates(0)
            context_gates(1)
            for n in range(2, NG):
                for j in range(KC):
                    project_x(n, j)
                    for t in range(2 * j, 2 * j + 2):
                        b_proj((n - 2) * GT + t)
            for t in range(2, 4):
                context_gates(t)
            for c in range(KC):
                project_z(0, 0, c)
                for t in range(8 + 4 * c, 12 + 4 * c):
                    b_proj(t)
            for c in range(KC):
                project_z(0, 1, c)

            pe.wait_ge(s_bps, 1)
            pe.wait_ge(s_mirror, 2)
            te.matmul(ps[:, 0, 0:2 * NS * B], mirror[:], bproj[:].rearrange("p c s b -> p (c s b)"),
                      start=True, stop=True).then_inc(s_mir, 1)
            for c in range(KC):
                project_z(1, 0, c)
            pe.wait_ge(s_mirc, 1)
            pe.wait_ge(s_toep, 16)
            both = ps[:, 1, 0:2 * NS * B].rearrange("p (c s b) -> p c s b", c=2, s=NS)

            fills = [(n, j, c) for n in range(1, NG) for j in range(KC) for c in range(KC)][KC:]
            for s in range(NS):
                te.matmul(both[:, :, s, :], toep[:, s, 0:P], bmir[:, :, s, :], start=s == 0, stop=False)
                last = te.matmul(both[:, 1, s, :], toep[:, s, P:S], bmir[:, 0, s, :], start=False, stop=s == NS - 1)
                if s % 2:
                    project_z(*fills[s // 2])
            last.then_inc(s_conv, 1)
            for f in fills[NS // 2:]:
                project_z(*f)
            pe.wait_ge(s_xm, 3)
            pe.wait_ge(s_xm3, 1)
            pe.wait_ge(s_projc, KC * NG)
            for n in range(NG):
                for k in range(GT):
                    t = n * GT + k
                    last = te.transpose(ps[0:3 * NS, n, k * P:(k + 1) * P],
                                        xm3[:, t % 2, :, :, t // 2].rearrange("p k s -> p (k s)"), ident[:])
                last.then_inc(s_xmt, 1)

            def mix(n):
                pe.wait_ge(s_xmtc, n + 1)
                pe.wait_ge(s_wc3, 2)
                pe.wait_ge(s_zc, KC * NG)
                for c in range(KC):
                    wait(pe, s_u, KC * (n - 1) + c + 1)
                    te.matmul(ps[:, 4 + c, :], wc3[:, c * P:(c + 1) * P], xm_t[:, n * GN:(n + 1) * GN],
                              start=True, stop=True).then_inc(s_wcd, 1)

            def out_project(n):
                pe.wait_ge(s_xmtc, NG)
                pe.wait_ge(s_wol, 1)
                pe.wait_ge(s_yl, KC * (n + 1))
                for k in range(GT):
                    wait(pe, s_r, 2 * (n - 1) + k // 2 + 1)
                    for c in range(KC):
                        last_ = three(ps[:, 2 + k // 2, (k % 2) * D:(k % 2 + 1) * D], yh[n % 2][:, c, k * P:(k + 1) * P],
                                      yl[n % 2][:, c, k * P:(k + 1) * P], woh[:, c, :], wol[:, c, :], c == 0, c == KC - 1)
                    if k % 2:
                        last_.then_inc(s_o, 1)

            def turn_x1(n):
                pe.wait_ge(s_x1, GT * (n + 1))
                wait(pe, s_q, KC * n)
                for c in range(KC):
                    for k in range(GT):
                        last_ = te.transpose(tile_ps(c, k), x1[:, n * GT + k, c * P:(c + 1) * P], ident[:])
                    last_.then_inc(s_x1t, 1)

            def gates(n):
                pe.wait_ge(s_q, KC * (n + 1))
                for t in range(n * GT, (n + 1) * GT):
                    for c in range(KC):
                        last_ = te.matmul(gate_ps(t), xq_t[:, c, t * P:(t + 1) * P], gw[:, c, :],
                                          start=False, stop=t == T - 1 and c == KC - 1)
                last_.then_inc(s_g, 1)

            for n in range(NG + 3):
                if n < NG:
                    mix(n)
                if n >= 3:
                    gates(n - 3)
                if n >= 1:
                    for t in range(4 + 6 * (n - 1), min(4 + 6 * n, T)):
                        context_gates(t)
                if 1 <= n <= NG:
                    out_project(n - 1)
                if 2 <= n <= NG + 1:
                    turn_x1(n - 2)

            pe.wait_ge(s_gs, 4)
            for c in range(2):
                for i in range(2):
                    last = te.transpose(ps[:, 7, i * S + c * P:i * S + (c + 1) * P],
                                        gsel[:, c, i, :, :, :].rearrange("p a b h -> p (a b h)"), ident[:])
            last.then_inc(s_gt, 1)
            H = B * NH
            pe.wait_ge(s_em, 1)
            pe.wait_ge(s_e1, 1)
            pe.wait_ge(s_wx, 1)
            for k, src in enumerate((em[0:H, 0:P], em[0:H, P:S], e1[0:H, :], wx[0:H, :])):
                last = te.transpose(ps[:, 6, k * H:(k + 1) * H], src, ident[0:H, 0:H])
            last.then_inc(s_tt, 1)

            pe.wait_ge(s_tok, 2)
            pe.wait_ge(s_const, 12)
            pe.wait_ge(s_oneh, 4 * 16)

            def scores(b, i, gi):
                c, hg = divmod(gi, 2)
                g_ = b * 4 + gi
                wait(pe, s_dec, g_ - 1)
                o = ps[:, gi % 2, :]
                te.matmul(o, ident_b[:], mask_b[:].rearrange("p h s -> p (h s)"), start=True, stop=False)
                te.matmul(o, decl[i][:, c * P:(c + 1) * P],
                          decr[i][:, hg * HG:(hg + 1) * HG, c * P:(c + 1) * P], start=False, stop=True)
                wait(pe, s_c, g_ - 1)
                for h in range(HG):
                    last_ = te.matmul(ps[:, 2 + gi % 2, h * P:(h + 1) * P],
                                      kbd[i][:, hg, h, c * P:(c + 1) * P], qb[i][:, hg, c * P:(c + 1) * P],
                                      start=True, stop=True)
                last_.then_inc(s_sc, 1)

            def numerator(b, i, gi):
                c, hg = divmod(gi, 2)
                pe.wait_ge(s_c, b * 4 + (gi + 1))
                pe.wait_ge(s_vb, b + 1)
                wait(pe, s_n1 if c else s_n0, b)
                for h in range(HG):
                    hd = hg * HG + h
                    last_ = te.matmul(ps[:, 4 + c, hd * DV:(hd + 1) * DV], cmat[:, gi, h, :],
                                      vb[i][:, c, hd, :], start=True, stop=True)
                last_.then_inc(s_num, 1)

            def state_sum(b, i):
                pe.wait_ge(s_wv, b + 1)
                wait(pe, s_sbd, b)
                for hg in range(2):
                    last_ = te.matmul(ps[:, 7, hg * HG * DV:(hg + 1) * HG * DV], ctb[i][:, 0, hg * P:(hg + 1) * P],
                                      wv[:, hg * HG:(hg + 1) * HG, :].rearrange("p h d -> p (h d)"),
                                      start=True, stop=True)
                last_.then_inc(s_st, 1)

            def carry_sum(b, i):
                pe.wait_ge(s_sbd, b + 1)
                wait(pe, s_car, b)
                for hg in range(2):
                    last_ = te.matmul(ps[:, 6, hg * HG * DV:(hg + 1) * HG * DV], qb[i][:, hg, P:S],
                                      state[:, hg, :, :].rearrange("p h d -> p (h d)"), start=True, stop=True)
                last_.then_inc(s_int, 1)

            def pe_step(b, i, first=False):
                pe.wait_ge(s_in[i], (b + (2 - i)) * (B * 8) if not isinstance(b, int) else 128 * (b // 2 + 1))
                scores(b, i, 0)
                if not first:
                    numerator(b - 1, 1 - i, 2)
                scores(b, i, 1)
                if not first:
                    numerator(b - 1, 1 - i, 3)
                state_sum(b, i)
                scores(b, i, 2)
                numerator(b, i, 0)
                scores(b, i, 3)
                carry_sum(b, i)
                numerator(b, i, 1)

            pe_step(0, 0, first=True)
            with pe.Fori(0, B // 2 - 1) as it:
                pe_step(it * 2 + 1, 1)
                pe_step(it * 2 + 2, 0)
            pe_step(B - 1, 1)
            numerator(B - 1, 1, 2)
            numerator(B - 1, 1, 3)

            pe.wait_ge(s_car, B)
            pe.wait_ge(s_sbd, B)

            def up(u):
                e, n = divmod(u, 4)
                pe.wait_ge(s_wl, 3 * (e + 1))
                sl = slice(n * GN, (n + 1) * GN)
                for f in range(KC):
                    wait(pe, s_h, KC * (u - 1) + f + 1)
                    for m in range(2):
                        for c in range(KC):
                            fs = slice(f * P, (f + 1) * P)
                            last_ = three(ps[:, 2 * f + m, :], wh[e % 2][:, m, c, fs], wl[e % 2][:, m, c, fs],
                                          xh[:, c, sl], xl[:, c, sl], c == 0, c == KC - 1)
                    last_.then_inc(s_ab, 1)

            def down(u):
                e, n = divmod(u, 4)
                pe.wait_ge(s_hl, KC * (u + 1))
                for k in range(GT):
                    wait(pe, s_acc, GT * (u - 1) + 2 * (k // 2) + 2)
                    for f in range(KC):
                        last_ = three(ps[:, 4 + k // 2, (k % 2) * D:(k % 2 + 1) * D],
                                      hh[u % 2][:, f, k * P:(k + 1) * P], hl[u % 2][:, f, k * P:(k + 1) * P],
                                      wh[e % 2][:, 2, f, :], wl[e % 2][:, 2, f, :], f == 0, f == KC - 1)
                    if k % 2:
                        last_.then_inc(s_yr, 1)

            def logits(n):
                pe.wait_ge(s_wr2, 2)
                wait(pe, s_lgc, n - 1)
                for c in range(KC):
                    sl = slice(n * GN, (n + 1) * GN)
                    last_ = three(ps[0:NE, 6 + n % 2, :], wrh[:, c, :], wrl[:, c, :], xh[:, c, sl], xl[:, c, sl],
                                  c == 0, c == KC - 1)
                last_.then_inc(s_lg, 1)

            turn(lns[1], 0, acc, 6, 0)
            pe.wait_ge(s_n0, B)
            pe.wait_ge(s_n1, B)
            turn(lns[1], 1, acc, 4, 0)
            pe.wait_ge(lns[1]["lo"], KC)
            up(0)
            turn(lns[1], 2, acc, 6, KC)
            pe.wait_ge(lns[1]["lo"], KC * 2)
            up(1)
            down(0)
            turn(lns[1], 3, acc, 6, KC * 3)
            for u in range(2, U):
                if u <= 3:
                    pe.wait_ge(lns[1]["lo"], KC * (u + 1))
                up(u)
                if u == 3:
                    logits(0)
                    logits(1)
                elif u == 4:
                    pe.wait_ge(s_lgc, NG)
                    for t in range(T):
                        last = te.transpose(ps[:, 7, t * NE:(t + 1) * NE], lgt[:, t * P:(t + 1) * P],
                                            ident[0:NE, 0:NE])
                    last.then_inc(s_lg, 1)
                down(u - 1)
                if u == 3:
                    logits(2)
                    logits(3)
            down(U - 1)


def split_expert(pool, gp, nc, raw, wh, wl, s_raw, s_wh, s_wl, e):
    pool.wait_ge(s_raw, 16 * (e + 1))
    for m in range(3):
        gp.tensor_copy(wh[e % 2][:, m], raw[:, m]).then_inc(s_wh, 1)
        pool.wait_ge(s_wh, 3 * e + m + 1)
        gp.tensor_tensor(wl[e % 2][:, m], raw[:, m], wh[e % 2][:, m].bitcast(F32), ALU.subtract).then_inc(s_wl, 1)


def kernel(**inputs):
    import numpy as np
    import concourse.bacc as bacc
    from concourse import mybir as mb
    from concourse.bass_utils import run_bass_kernel_spmd

    a = {k.replace("L0_", ""): np.asarray(v) for k, v in inputs.items()}

    def by_part(v):
        return v.reshape(-1, P).T

    def per_row(v):
        return np.tile(v, 2 * B).reshape(P, 1)

    arrays = {
        "x": a["x"].reshape(B * S, D),
        "ctx": a["ctx_1024"].reshape(B * S, D),
        "ctx_t": a["ctx_1024"].reshape(B * S, D).T,
        "cols": np.concatenate(
            [by_part(a["attn_log_dt"]), by_part(a["attn_D_skip"]), by_part(a["attn_b_in"]), by_part(a["attn_ln_g"]),
             by_part(a["attn_ln_b"]), a["attn_A_log"].reshape(KC, P, NS).transpose(1, 0, 2).reshape(P, KC * NS),
             per_row(a["xattn_igate_b"]), per_row(a["xattn_fgate_b"])], axis=1),
        "rows": np.concatenate([a["attn_b_out"], a["xattn_norm_w"], a["ffn_gate_b"]]),
        "win_t": a["attn_W_in"].T,
        "wb_t": a["attn_W_B"].T,
        "wc_t": a["attn_W_C"].T,
        "wout_t": a["attn_W_out"].T,
        "gates_t": np.concatenate([a["xattn_igate_w"], a["xattn_fgate_w"]], axis=0).T,
        "moe_w": np.stack(
            [np.stack([a["ffn_fc1"].T, a["ffn_fc2"].T, a["ffn_fc3"].T])]
            + [np.stack([a["ffn_ew1"][e].T, a["ffn_ew3"][e].T, a["ffn_ew2"][e].T]) for e in range(NE)]),
        "router_t": a["ffn_gate_w"].T,
    }
    arrays = {f"in_{k}": np.ascontiguousarray(v) for k, v in arrays.items()}
    nc = bacc.Bacc("TRN2", target_bir_lowering=False, num_devices=1)
    args = [nc.dram_tensor(k, v.shape, mb.dt.from_np(v.dtype), kind="ExternalInput").ap() for k, v in arrays.items()]
    o = nc.dram_tensor("out_x", (B * S, D), mb.dt.float32, kind="ExternalOutput").ap()
    build(nc, *args, o)
    r = run_bass_kernel_spmd(nc, [arrays], core_ids=[0])
    return r.results[0]["out_x"].reshape(B, S, D)
```

```python
import math

import concourse.bass as bass
from concourse import mybir

F32 = mybir.dt.float32
F32R = mybir.dt.float32r
BF16 = mybir.dt.bfloat16
I32 = mybir.dt.int32
ALU = mybir.AluOpType
ACT = mybir.ActivationFunctionType
X = mybir.AxisListType.X

P = 128
B, S, D = 8, 256, 256
T = B * S // P
KC = D // P
NG = 4
GT = T // NG
GN = GT * P
NS = 16
NH, DH = 8, 32
HG = P // DH
DV = DH + 1
NE = 6
EPS = 1e-5
LOG_FLOOR = -math.log(1e-8)
QK_SCALE = DH ** -0.5
MASKED = -1e30
EARLY = ((1, 0, 4), (1, 1, 5), (0, 0, 2), (0, 1, 3))
EARLY_FIRST = 2
COPIED = [e for e in EARLY if e[0] > 0]


def copied_at(b, gi):
    places = [k for k, e in enumerate(COPIED) if isinstance(b, int) and e[:2] == (b, gi)]
    return places[0] if places else None


C_LOGDT, C_DSKIP, C_BIN, C_LNG, C_LNB, C_ALOG, C_GB = 0, 2, 4, 8, 10, 12, 44
N_COLS = 46


def build(nc, x, ctx, ctx_t, cols, rows, win_t, wb_t, wc_t, wout_t, gates_t, moe_w, router_t, out):
    class Region:

        def __init__(self, start):
            self.at = start

        def __call__(self, name, shape, dt=F32):
            size = int(np_prod(shape[1:])) * (2 if dt == BF16 else 4)
            t = nc.alloc_sbuf_tensor_at(name, shape, dt, offset=self.at)
            self.at += (size + 31) // 32 * 32
            return t

    def np_prod(xs):
        n = 1
        for v in xs:
            n *= v
        return n

    keep = Region((nc.sbuf_base + 31) // 32 * 32)
    x_tm = keep("x_tm", [P, T, D])
    x1 = keep("x1", [P, T, D])
    xq_t = keep("xq_t", [P, KC, B * S])
    acc = keep("acc", [P, T, D])
    z_t = acc[:, :, :].rearrange("p t d -> p (t d)").rearrange("p (c n) -> p c n", c=KC)
    split_at = keep.at
    xh = keep("xh", [P, KC, B * S], F32R)
    xl = keep("xl", [P, KC, B * S], F32R)
    ident = keep("ident", [P, P])
    mirror = keep("mirror", [P, P])
    ident_b = keep("ident_b", [P, P], BF16)
    mask_b = keep("mask_b", [P, HG, P], BF16)
    block_mask = keep("block_mask", [P, HG, DV])
    onehot_f = keep("onehot_f", [2 * NH, NH, P])
    inv_d = keep("inv_d", [P, P])
    ones = keep("ones", [P, S])
    pow_e = keep("pow_e", [P, 16])
    prio = keep("prio", [P, NE])
    col = keep("col", [P, N_COLS])
    row = keep("row", [P, 2 * D + NE])
    b_half = row[:, 0:D]
    b_out_row, norm_w_row, gate_b_row = row[:, 0:D], row[:, D:2 * D], row[:, 2 * D:]
    wb = keep("wb", [P, KC, NS])
    wc = keep("wc", [3 * NS, D])
    wc3 = keep("wc3", [3 * NS, D], F32R)
    gw = keep("gw", [P, 3 * KC, 2 * NH])
    gw_ctx = keep("gw_ctx", [P, KC, 2 * NH])
    stats = keep("stats", [P, T, 6])
    mv = keep("mv", [P, T, 2])
    rstd = keep("rstd", [P, T])
    shift = keep("shift", [P, T])
    small = keep("small", [P, T, 2 * NH])
    tok = keep("tok", [P, 4, B * NH])
    wr = keep("wr", [P, KC, NE])
    wrh = keep("wrh", [P, KC, NE], F32R)
    wrl = keep("wrl", [P, KC, NE], F32R)
    raw = keep("raw", [P, 3, KC, D])
    winf = raw[:, 0:2, :, :].rearrange("p m c d -> p (m c d)").rearrange("p (c n) -> p c n", c=KC)
    expert0_at = keep.at
    wh0 = keep("wh0", [P, 3, KC, D], F32R)
    wl0 = keep("wl0", [P, 3, KC, D], F32R)
    shared_at = keep.at

    ra = Region(shared_at)
    decay_pow = ra("decay_pow", [P, NS, KC, P])
    rt = Region(shared_at)
    toep = rt("toep", [P, NS, S])
    yset_at = rt.at
    rt.at += 3 * 4 * KC * GN
    ra = Region(max(ra.at, rt.at))
    xm_t = ra("xm_t", [3 * NS, B * S], F32R)
    cx_t = ra("cx_t", [P, KC, B * S])
    win = ra("win", [P, KC, 2 * D])
    ra_top = ra.at
    rw_ = Region(expert0_at)
    wih = rw_("wih", [P, KC, 2 * D], F32R)
    wil = rw_("wil", [P, KC, 2 * D], F32R)
    rs = Region(ra_top)
    wout = rs("wout", [P, KC, D])
    woh = rs("woh", [P, KC, D], F32R)
    wol = rs("wol", [P, KC, D], F32R)
    tsteps_i = rs("tsteps_i", [P, P], I32)
    tsteps = rs("tsteps", [P, P])
    half_pow = rs("half_pow", [P, KC, NS, 2])
    dt = rs("dt", [P, KC])
    dt_mean = rs("dt_mean", [P, 1])
    log_a = rs("log_a", [P, KC, NS])
    b_in2 = rs("b_in2", [P, 4])
    amean = rs("amean", [P, 2 * NS])
    amean_t = rs("amean_t", [2 * NS, P])
    zpad = rs("zpad", [NS, P])
    bproj = rs("bproj", [P, 2, NS, B])
    bmir = rs("bmir", [P, 2, NS, B])
    xmh = rs("xmh", [P, 2, NS, B], F32R)
    xm3 = rs("xm3", [P, 2, 3, NS, B])
    rb = Region(shared_at)
    kbd = [rb(f"kbd{i}", [P, KC, HG, S]) for i in range(2)]
    ctb = [rb(f"ctb{i}", [P, 2, D]) for i in range(2)]
    qb = [rb(f"qb{i}", [P, KC, S]) for i in range(2)]
    decl = [rb(f"decl{i}", [4 * NH, S], F32R) for i in range(2)]
    decr = [rb(f"decr{i}", [4 * NH, NH, S], F32R) for i in range(2)]
    vb = [rb(f"vb{i}", [P, 2, NH, DV]) for i in range(2)]
    wv = rb("wv", [P, NH, DV])
    dec = rb("dec", [P, 2, HG, P])
    cmat = rb("cmat", [P, 4, HG, P])
    state = rb("state", [P, KC, HG, DV])
    nm = [rb(f"nm{i}", [P, 2, NH, DV]) for i in range(2)]
    sq = rb("sq", [P, 2, NH, DH])
    hn = rb("hn", [P, 2, NH, DH])
    carry = rb("carry", [P, NH, DV])
    vsum = rb("vsum", [P, 2, NH])
    vmean = rb("vmean", [P, 2, NH])
    ssum = rb("ssum", [P, 2, NH])
    nrm = rb("nrm", [P, 2, NH])
    rec = rb("rec", [P, 2, NH])
    rec2 = rb("rec2", [P, 2, NH])
    var = rb("var", [P, 2, NH])
    rsd = rb("rsd", [P, 2, NH])
    rr = rb("rr", [P, 2, NH])
    rr_ = Region(split_at)
    gsel = rr_("gsel", [P, 2, 2, 2, B, NH])
    fa = rr_("fa", [P, S])
    fe = rr_("fe", [P, S])
    fl = rr_("fl", [P, S])
    fm = rr_("fm", [P, S])
    ls = rr_("ls", [P, S])
    fcum = rr_("fcum", [P, S])
    g = rr_("g", [P, S])
    mx = rr_("mx", [P, S])
    nmx = rr_("nmx", [P, S])
    mld = rr_("mld", [P, S])
    em = rr_("em", [P, S])
    e1 = rr_("e1", [P, P])
    wx = rr_("wx", [P, P])
    nr127 = rr_("nr127", [P, 1])
    gm = rr_("gm", [P, 2, S], F32R)
    assert rr_.at <= split_at + 16384 + 32
    qk_early = Region(rr_.at)("qk_early", [P, len(COPIED), HG * P])
    ry_ = Region(rr_.at)
    rx_ = Region(yset_at)
    yh = [r(f"yh{i}", [P, KC, GN], F32R) for i, r in enumerate((rx_, ry_))]
    yl = [r(f"yl{i}", [P, KC, GN], F32R) for i, r in enumerate((rx_, ry_))]
    ybuf = [r(f"ybuf{i}", [P, KC, GN]) for i, r in enumerate((rx_, ry_))]
    assert rx_.at <= ra_top
    re_ = Region(shared_at)
    wh1 = re_("wh1", [P, 3, KC, D], F32R)
    wl1 = re_("wl1", [P, 3, KC, D], F32R)
    sil = re_("sil", [P, KC, GN])
    hbuf = re_("hbuf", [P, KC, GN])
    hh = [re_(f"hh{i}", [P, KC, GN], F32R) for i in range(2)]
    hl = [re_(f"hl{i}", [P, KC, GN], F32R) for i in range(2)]
    wh, wl = [wh0, wh1], [wl0, wl1]
    lg = re_("lg", [P, T, NE])
    pe_ = re_("pe_", [P, T, NE])
    pr = re_("pr", [P, T, NE])
    eq = re_("eq", [P, T, NE])
    kk = re_("kk", [P, T, NE])
    oh1 = re_("oh1", [P, T, NE])
    p1 = re_("p1", [P, T, NE])
    oh2 = re_("oh2", [P, T, NE])
    ge = re_("ge", [P, T, NE])
    lgt = re_("lgt", [NE, B * S])
    m1 = re_("m1", [P, T])
    m2 = re_("m2", [P, T])
    km = re_("km", [P, T])
    rw = re_("rw", [P, T])
    assert max(rs.at, rb.at, re_.at) <= nc.sbuf_usable_end, (rs.at, rb.at, re_.at)

    ps = nc.alloc_psum_tensor("ps", [P, 8, 512], F32)
    apad = nc.dram_tensor("apad", [NS, 3 * P], F32).ap()
    gd = nc.dram_tensor("gd", [2, B, NH, S], F32).ap()
    md = nc.dram_tensor("md", [2, B, NH, NH, S], F32).ap()

    names = {}

    def sem(name):
        assert name not in names
        names[name] = nc.alloc_semaphore(name)
        return names[name]

    def wait(eng, s, n):
        if not isinstance(n, int) or n > 0:
            eng.wait_ge(s, n)

    s_col, s_row, s_win, s_wb, s_wc, s_wout, s_gw, s_wr, s_cxt = (
        sem(f"loaded_{n}") for n in ("col", "row", "win", "wb", "wc", "wout", "gw", "wr", "cxt"))
    s_x = [sem(f"loaded_x{n}") for n in range(NG)]
    s_bhalf = sem("b_out_halved")
    s_p128 = sem("powers_of_128")
    s_const = sem("constants_made")
    s_ident, s_inv = sem("ident_made"), sem("inv_made")
    s_onehot = sem("onehot_made")
    s_mirror, s_mir, s_mirc = sem("mirror_made"), sem("bproj_mirrored"), sem("bproj_mirror_copied")
    s_tstep_i, s_edt, s_ea = (
        sem(n) for n in ("tstep_i", "exp_log_dt", "exp_a_log"))
    s_decay_step = sem("decay_step")
    s_neg = sem("means_negated")
    s_hl_last = sem("hidden_lo_last")
    s_zp, s_zc, s_shift = sem("z_projected"), sem("z_copied"), sem("shift_r1")
    s_wc3, s_xm3 = sem("wc_split"), sem("conv_split")
    s_dmul, s_dexp, s_amean, s_am_sb, s_am_t, s_amt_sb, s_pad, s_toep = (
        sem(n) for n in ("decay_scaled", "decay_exp", "decay_summed", "decay_mean_copied", "decay_mean_t",
                         "decay_mean_t_copied", "decay_stored", "toeplitz_loaded"))
    s_dtm, s_bias, s_bin2, s_winf, s_wih, s_wil, s_woh, s_wol, s_gwc = (
        sem(n) for n in ("dt_mean_copied", "bias_summed", "bias_made", "win_scaled", "win_hi", "win_lo", "wout_hi",
                         "wout_lo", "gate_ctx_weights"))
    lns = [{k: sem(f"{k}_{i}") for k in ("stats", "aggr", "vareps", "rstd", "normed", "turned", "hi", "lo")}
           for i in range(2)]
    s_proj, s_projc, s_x2b, s_bp, s_bps, s_conv, s_xm, s_xmt, s_xmtc = (
        sem(n) for n in ("projected", "projected_copied", "x2b_made", "bproj_summed", "bproj_scaled", "conv_done",
                         "conv_copied", "conv_t", "conv_t_copied"))
    s_wcd, s_u, s_y, s_yh, s_yl, s_o, s_r, s_st1, s_ag1, s_ve1, s_rs1, s_x1, s_x1t, s_q, s_g = (
        sem(n) for n in ("mixed", "skip_added", "gated", "gated_hi", "gated_lo", "out_projected", "residual1",
                         "stats_r1", "aggr_r1", "vareps_r1", "rstd_r1", "x1_made", "x1_turned", "q_copied",
                         "gates_summed"))
    s_gc, s_gs, s_gt, s_fa, s_fe, s_fl, s_em, s_e1, s_wx, s_gh, s_gl, s_tt, s_tok, s_gmd = (
        sem(n) for n in ("gates_copied", "gates_ordered", "gates_turned", "f_abs", "f_exp", "f_ln", "exp_neg_max",
                         "carry_weight", "key_weight", "gm_hi", "gm_lo", "rows_turned", "rows_copied", "gm_stored"))
    s_row_step = sem("row_step")
    s_qk, s_qkc, s_qkr = sem("early_qk"), sem("early_qk_copied"), sem("qk_ready")

    def qk_count(b, gi):
        left_out = len([e for e in EARLY if not isinstance(b, int) or e[:2] < (b, gi)])
        return b * 4 + (gi + 1 - left_out)

    s_kz, s_vone = sem("kbd_cleared"), sem("value_ones")
    s_in = [sem(f"batch_loaded{i}") for i in range(2)]
    (s_vs, s_vm, s_vb, s_wv, s_sc, s_dec, s_c, s_st, s_sbd, s_int, s_car, s_n0, s_n1, s_sq, s_rsd, s_rr, s_hn,
     s_hw, s_r2) = (
        sem(n) for n in ("v_summed", "v_mean", "v_centred", "v_weighted", "log_decays_ready", "decay_done", "c_done",
                         "state_summed", "state_masked", "carry_summed", "carry_scaled", "num0_copied",
                         "num1_summed", "squared", "var_rsqrt", "head_scale", "head_normed", "head_weighted",
                         "residual2"))
    s_norm_step, s_var_step = sem("norm_step"), sem("var_step")
    s_num, s_zero, s_oneh = (
        sem(n) for n in ("numerators", "zeros_stored", "onehot_placed"))
    s_raw, s_wh, s_wl, s_wr2, s_ab, s_sil, s_h, s_hh, s_hl, s_yr, s_acc = (
        sem(n) for n in ("raw_loaded", "expert_hi", "expert_lo", "router_split", "up_ready", "silu_done",
                         "hidden_done", "hidden_hi", "hidden_lo", "down_ready", "acc_done"))
    s_lg, s_lgc, s_gate, s_pexp = sem("logits_summed"), sem("logits_copied"), sem("gating_step"), sem("router_exp")
    s_fst, s_fag, s_fve, s_frs, s_fout, s_store = (
        sem(n) for n in ("stats_out", "aggr_out", "vareps_out", "rstd_out", "out_made", "out_stored"))

    U = 4 * (NE + 1)

    assert NE % 2 == 0

    def unit_before(e, n, odd):
        return (e, n - 1, odd) if n else (e - 1, NG - 1, 1 - odd)

    def is_last(e, n):
        return isinstance(e, int) and (e, n) == (NE, NG - 1)

    def tile_ps(bank, k):
        return ps[:, bank, k * P:(k + 1) * P]

    def gate_ps(t):
        return ps[:, 6, t * 2 * NH:(t + 1) * 2 * NH]

    block_cm = nc.Block()
    with block_cm as block:

        @block.sync
        def _(sp):
            xv = x.rearrange("(t p) d -> p t d", p=P)
            sp.dma_start(col[:], cols).then_inc(s_col, 16)
            sp.dma_start(x_tm[:, 0:GT, :], xv[:, 0:GT, :]).then_inc(s_x[0], 16)
            sp.dma_start(win[:], win_t.rearrange("(c p) n -> p c n", p=P)).then_inc(s_win, 16)
            for n in range(1, NG):
                sp.dma_start(x_tm[:, n * GT:(n + 1) * GT, :], xv[:, n * GT:(n + 1) * GT, :]).then_inc(s_x[n], 16)
            sp.dma_start(wb[:], wb_t.rearrange("(c p) n -> p c n", p=P)).then_inc(s_wb, 16)
            sp.dma_start(row[:], rows.partition_broadcast(P)).then_inc(s_row, 16)
            for k in range(3):
                sp.dma_start(wc[k * NS:(k + 1) * NS, :], wc_t).then_inc(s_wc, 16)
            sp.dma_start(wout[:], wout_t.rearrange("(c p) n -> p c n", p=P)).then_inc(s_wout, 16)
            sp.dma_start(gw[:], gates_t.rearrange("(c p) n -> p c n", p=P)).then_inc(s_gw, 16)
            sp.dma_start(cx_t[:], ctx_t.rearrange("(c p) n -> p c n", p=P)).then_inc(s_cxt, 16)
            sp.dma_start(wr[:], router_t.rearrange("(c p) n -> p c n", p=P)).then_inc(s_wr, 16)
            sp.wait_ge(s_const, 1)
            sp.dma_start(apad[:, 0:P], zpad[:]).then_inc(s_pad, 16)
            sp.wait_ge(s_amt_sb, 1)
            sp.dma_start(bass.AP(apad.tensor, P, [[P, 2], [3 * P, NS], [1, P]]), amean_t[:]).then_inc(s_pad, 16)
            sp.wait_ge(s_pad, 32)
            sp.dma_start(toep[:], bass.AP(apad.tensor, 1, [[1, P], [3 * P, NS], [1, S]])).then_inc(s_toep, 16)
            sp.wait_ge(s_wil, 1)
            sp.dma_start(raw[:], moe_w[0].rearrange("m (c p) n -> p m c n", p=P)).then_inc(s_raw, 16)

            cxv = ctx_t.rearrange("(c h p) n -> p c h n", h=HG, p=DH)
            ctv = ctx.rearrange("(t p) d -> p t d", p=P)

            def load_k(i, b):
                for h in range(HG):
                    sp.dma_start(kbd[i][h * DH:(h + 1) * DH, :, h, :], cxv[:, :, h, bass.ds(b * S, S)])\
                        .then_inc(s_in[i], 16)

            def load_ctx_q(i, b):
                sp.dma_start(ctb[i][:], ctv[:, bass.ds(b * 2, 2), :]).then_inc(s_in[i], 16)
                sp.dma_start(qb[i][:], xq_t[:, :, bass.ds(b * S, S)]).then_inc(s_in[i], 16)

            def load_gates(i, b):
                sp.dma_start(decl[i][0:2 * NH, :].bitcast(F32),
                             bass.AP(gd.tensor, b * (NH * S), [[B * NH * S, 2], [S, NH], [1, S]])).then_inc(s_in[i], 16)
                sp.dma_start(decr[i][2 * NH:, :, :].rearrange("p h n -> p (h n)").bitcast(F32),
                             bass.AP(md.tensor, b * (NH * NH * S),
                                     [[B * NH * NH * S, 2], [NH * S, NH], [1, NH * S]])).then_inc(s_in[i], 16)

            sp.wait_ge(s_kz, 2)
            sp.dma_start(md.rearrange("a b h k n -> (a b h k n)").rearrange("(p n) -> p n", p=P),
                         kbd[0][:].rearrange("p c h n -> p (c h n)")).then_inc(s_zero, 16)
            sp.wait_ge(s_zero, 16)
            for i in range(2):
                load_k(i, i)
            sp.wait_ge(s_vone, 4)
            for i in range(2):
                for half in range(2):
                    sp.dma_start(decr[i][0:2 * NH, :, half * P:(half + 1) * P].bitcast(F32), onehot_f[:])\
                        .then_inc(s_oneh, 16)
            sp.wait_ge(s_yl, KC * NG)
            sp.wait_ge(s_o, 2 * NG)
            sp.wait_ge(s_q, KC)
            for i in range(2):
                load_ctx_q(i, i)
            sp.wait_ge(s_gl, 1)
            sp.dma_start(gd.rearrange("a b h n -> (a b h) n"), gm[:, 0, :].bitcast(F32)).then_inc(s_gmd, 16)
            sp.wait_ge(s_gl, 2)
            sp.dma_start(bass.AP(md.tensor, 0, [[NH * NH * S, 2 * B], [NH * S + S, NH], [1, S]]),
                         gm[:, 1, :].bitcast(F32)).then_inc(s_gmd, 16)
            sp.wait_ge(s_gmd, 32)
            for i in range(2):
                sp.wait_ge(s_in[i], 6 * 16)
                load_gates(i, i)
            with sp.Fori(0, B // 2 - 1) as it:
                for i in range(2):
                    b = it * 2 + (i + 2)
                    sp.wait_ge(s_num, it * 8 + (i * 4 + 2))
                    load_k(i, b)
                    load_ctx_q(i, b)
                    load_gates(i, b)

            with sp.Fori(0, NE) as it:
                sp.wait_ge(s_wl, it * 3 + 3)
                sp.dma_start(raw[:], bass.AP(moe_w.tensor, it * (3 * D * D) + 3 * D * D,
                                             [[D, P], [D * D, 3], [P * D, KC], [1, D]])).then_inc(s_raw, 16)
            ov = out.rearrange("(t p) d -> p t d", p=P)
            for lo_, hi_ in ((0, GT), (GT, 2 * GT), (2 * GT, 3 * GT), (3 * GT, T - 2), (T - 2, T)):
                sp.wait_ge(s_fout, hi_)
                sp.dma_start(ov[:, lo_:hi_, :], acc[:, lo_:hi_, :]).then_inc(s_store, 16)
            sp.wait_ge(s_store, 16 * (NG + 1))

        @block.gpsimd
        def _(pool):
            gp = nc.gpsimd
            gp.memset(zpad[:], 0.0).then_inc(s_const, 1)
            gp.iota(tsteps_i[:], [[1, P]], base=0, channel_multiplier=0).then_inc(s_tstep_i, 1)
            gp.memset(pow_e[:], -0.5).then_inc(s_const, 1)
            gp.memset(ones[:], 1.0).then_inc(s_const, 1)
            gp.memset(ident[:], 0.0).then_inc(s_ident, 1)
            pool.wait_ge(s_ident, 1)
            gp.affine_select(out=ident[:], in_=ident[:], compare_op=ALU.not_equal, fill=1.0, base=0,
                             pattern=[[-1, P]], channel_multiplier=1).then_inc(s_ident, 1)
            gp.memset(mirror[:], 0.0).then_inc(s_mirror, 1)
            pool.wait_ge(s_mirror, 1)
            gp.affine_select(out=mirror[:], in_=mirror[:], compare_op=ALU.not_equal, fill=1.0, base=1 - P,
                             pattern=[[1, P]], channel_multiplier=1).then_inc(s_mirror, 1)

            def rsqrt(eps_sem, n, lo, hi, src, done):
                pool.wait_ge(eps_sem, n)
                gp.tensor_tensor(src[:, lo:hi], src[:, lo:hi], pow_e[:, 0:hi - lo], ALU.pow).then_inc(done, 1)

            pool.wait_ge(s_const, 3)
            for n in range(NG):
                rsqrt(lns[0]["vareps"], n + 1, n * GT, (n + 1) * GT, rstd, lns[0]["rstd"])
                if n == 0:
                    pool.wait_ge(s_gw, 16)
                    gp.tensor_tensor(gw_ctx[:], gw[:, KC:2 * KC, :], gw[:, 2 * KC:3 * KC, :], ALU.add)\
                        .then_inc(s_gwc, 1)
            pool.wait_ge(s_wout, 16)
            gp.tensor_copy(woh[:], wout[:]).then_inc(s_woh, 1)
            pool.wait_ge(s_woh, 1)
            gp.tensor_tensor(wol[:], wout[:], woh[:].bitcast(F32), ALU.subtract).then_inc(s_wol, 1)
            gp.memset(mask_b[:], 0.0).then_inc(s_const, 1)
            gp.memset(ident_b[:], 0.0).then_inc(s_const, 1)
            gp.memset(block_mask[:], 1.0).then_inc(s_const, 1)
            gp.memset(onehot_f[:], 0.0).then_inc(s_const, 1)
            pool.wait_ge(s_const, 7)
            gp.affine_select(out=mask_b[:], in_=mask_b[:], compare_op=ALU.is_ge, fill=MASKED, base=0,
                             pattern=[[0, HG], [1, P]], channel_multiplier=-1).then_inc(s_const, 1)
            gp.affine_select(out=ident_b[:], in_=ident_b[:], compare_op=ALU.not_equal, fill=1.0, base=0,
                             pattern=[[-1, P]], channel_multiplier=1).then_inc(s_const, 1)
            gp.affine_select(out=block_mask[:], in_=block_mask[:], compare_op=ALU.is_ge, fill=0.0, base=0,
                             pattern=[[-DH, HG], [0, DV]], channel_multiplier=1).then_inc(s_const, 1)
            pool.wait_ge(s_const, 10)
            gp.affine_select(out=block_mask[:], in_=block_mask[:], compare_op=ALU.is_ge, fill=0.0, base=DH - 1,
                             pattern=[[DH, HG], [0, DV]], channel_multiplier=-1).then_inc(s_const, 1)
            gp.affine_select(out=onehot_f[:], in_=onehot_f[:], compare_op=ALU.not_equal, fill=1.0, base=0,
                             pattern=[[-1, NH], [0, P]], channel_multiplier=1).then_inc(s_onehot, 1)
            pool.wait_ge(s_onehot, 1)
            gp.affine_select(out=onehot_f[:], in_=onehot_f[:], compare_op=ALU.not_equal, fill=1.0, base=-NH,
                             pattern=[[-1, NH], [0, P]], channel_multiplier=1).then_inc(s_onehot, 1)
            gp.iota(prio[:], [[-1, NE]], base=NE, channel_multiplier=0,
                    allow_small_or_imprecise_dtypes=True).then_inc(s_const, 1)
            pool.wait_ge(s_bhalf, 1)
            for n in range(NG):
                pool.wait_ge(lns[0]["normed"], GT * (n + 1))
                xg = x_tm[:, n * GT:(n + 1) * GT, :]
                gp.tensor_tensor(xg, xg, b_half.unsqueeze(1).broadcast_to([P, GT, D]), ALU.add).then_inc(s_x2b, 1)
            pool.wait_ge(s_conv, 1)
            for i in range(2):
                gp.memset(kbd[i][:], 0.0).then_inc(s_kz, 1)

            def root_and_shift(n):
                rsqrt(s_ve1, n + 1, n * GT, (n + 1) * GT, rstd, s_rs1)
                pool.wait_ge(s_rs1, n + 1)
                gs = slice(n * GT, (n + 1) * GT)
                pool.wait_ge(s_neg, n + 1)
                gp.tensor_tensor(shift[:, gs], shift[:, gs], rstd[:, gs], ALU.mult).then_inc(s_shift, 1)

            for n in range(NG):
                for c in range(KC):
                    pool.wait_ge(s_yh, KC * n + c + 1)
                    gp.tensor_tensor(yl[n % 2][:, c, :], ybuf[n % 2][:, c, :], yh[n % 2][:, c, :].bitcast(F32),
                                     ALU.subtract).then_inc(s_yl, 1)
                if n >= 1:
                    root_and_shift(n - 1)
            root_and_shift(NG - 1)

            pool.wait_ge(s_o, 2 * NG)
            for i in range(2):
                gp.memset(decl[i][:].bitcast(F32), 1.0).then_inc(s_vone, 1)
            for i in range(2):
                gp.memset(vb[i][:, :, :, DH:DV], 1.0).then_inc(s_vone, 1)
            pool.wait_ge(s_raw, 16)
            split_expert(pool, gp, raw, wh, wl, s_wh, s_wl, 0, 0)
            pool.wait_ge(s_wr, 16)
            gp.tensor_copy(wrh[:], wr[:]).then_inc(s_wr2, 1)
            pool.wait_ge(s_wr2, 1)
            gp.tensor_tensor(wrl[:], wr[:], wrh[:].bitcast(F32), ALU.subtract).then_inc(s_wr2, 1)

            def values(b, i):
                pool.wait_ge(s_vm, b + 1)
                gp.tensor_tensor(vb[i][:, :, :, 0:DH],
                                 ctb[i][:, :, :].rearrange("p c (h d) -> p c h d", h=NH),
                                 vmean[:, :, :].unsqueeze(3).broadcast_to([P, 2, NH, DH]),
                                 ALU.subtract).then_inc(s_vb, 1)
                pool.wait_ge(s_vb, b + 1)
                wait(pool, s_st, b)
                if isinstance(b, int) and b == 0:
                    pool.wait_ge(s_tok, 2)
                gp.tensor_tensor(wv[:], vb[i][:, 0, :, :],
                                 tok[:, 3, bass.ds(b * NH, NH)].unsqueeze(2).broadcast_to([P, NH, DV]),
                                 ALU.mult).then_inc(s_wv, 1)

            def head_root(b):
                pool.wait_ge(s_var_step, b * 3 + 3)
                gp.tensor_tensor(rsd[:].rearrange("p a h -> p (a h)"), var[:].rearrange("p a h -> p (a h)"),
                                 pow_e[:, 0:2 * NH], ALU.pow).then_inc(s_rsd, 1)

            def residual(b):
                pool.wait_ge(s_hn, b + 1)
                hnv = hn[:].rearrange("p a h d -> p a (h d)")
                gp.tensor_tensor(hnv, hnv, norm_w_row.unsqueeze(1).broadcast_to([P, 2, D]), ALU.mult)\
                    .then_inc(s_hw, 1)
                pool.wait_ge(s_hw, b + 1)
                gp.tensor_tensor(x_tm[:, bass.ds(b * 2, 2), :], hnv, x1[:, bass.ds(b * 2, 2), :],
                                 ALU.add).then_inc(s_r2, 1)

            def norm2_root(b, i):
                pool.wait_ge(lns[1]["vareps"], b + 1)
                gp.tensor_tensor(rstd[:, 2 * i:2 * i + 2], rstd[:, 2 * i:2 * i + 2], pow_e[:, 0:2], ALU.pow)\
                    .then_inc(lns[1]["rstd"], 1)

            values(0, 0)
            values(1, 1)

            def pool_step(b, i):
                if not isinstance(b, int) or b >= 3:
                    norm2_root(b - 3, 1 - i)
                if not isinstance(b, int) or b >= 2:
                    residual(b - 2)
                if not isinstance(b, int) or b < B - 1:
                    values(b + 1, 1 - i)
                head_root(b - 1)

            pool_step(1, 1)
            pool_step(2, 0)
            with pool.Fori(0, B // 2 - 2) as it:
                pool_step(it * 2 + 3, 1)
                pool_step(it * 2 + 4, 0)
            pool_step(B - 1, 1)
            norm2_root(B - 3, 1)
            residual(B - 2)
            head_root(B - 1)
            norm2_root(B - 2, 0)

            def hidden_lo(e, n):
                u = e * NG + n
                for f in range(KC):
                    pool.wait_ge(s_hh, u * KC + (f + 1))
                    if not isinstance(e, int) or u >= 2:
                        pool.wait_ge(s_yr, (u - 1) * 2)
                    gp.tensor_tensor(hl[n % 2][:, f, :], hbuf[:, f, :], hh[n % 2][:, f, :].bitcast(F32),
                                     ALU.subtract).then_inc(s_hl, 1)

            def pool_expert(e, odd):
                hidden_lo(e, 0)
                pool.wait_ge(s_raw, e * 16 + 32)
                hidden_lo(e, 1)
                split_expert(pool, gp, raw, wh, wl, s_wh, s_wl, e + 1, 1 - odd)
                hidden_lo(e, 2)
                hidden_lo(e, 3)

            hidden_lo(0, 0)
            residual(B - 1)
            norm2_root(B - 1, 1)
            hidden_lo(0, 1)
            pool.wait_ge(s_raw, 32)
            split_expert(pool, gp, raw, wh, wl, s_wh, s_wl, 1, 1)
            hidden_lo(0, 2)
            hidden_lo(0, 3)
            pool_expert(1, 1)
            with pool.Fori(0, NE // 2 - 1) as it:
                pool_expert(it * 2 + 2, 0)
                pool_expert(it * 2 + 3, 1)
            for n in range(NG):
                if n < NG - 1:
                    hidden_lo(NE, n)
                if n >= 1:
                    rsqrt(s_fve, n, (n - 1) * GT, n * GT, rstd, s_frs)
            rsqrt(s_fve, NG, T - GT, T - 2, rstd, s_frs)
            rsqrt(s_fve, NG + 1, T - 2, T, rstd, s_frs)

        @block.scalar
        def _(act):
            sc = nc.scalar
            act.wait_ge(s_col, 16)
            sc.activation(dt[:], col[:, C_LOGDT:C_LOGDT + KC], ACT.Exp).then_inc(s_edt, 1)
            act.wait_ge(s_decay_step, 1)
            sc.activation(log_a[:], log_a[:], ACT.Exp).then_inc(s_ea, 1)
            act.wait_ge(s_decay_step, 4)
            sc.activation(half_pow[:, :, :, 1], log_a[:], ACT.Exp, scale=float(P)).then_inc(s_p128, 1)

            def powers(q):
                act.wait_ge(s_dmul, q + 1)
                v = decay_pow[:, 4 * q:4 * q + 4, :, :]
                sc.activation(v, v, ACT.Exp).then_inc(s_dexp, 1)

            def hi_parts(ln, n, first_bank, after=None):
                for c in range(KC):
                    act.wait_ge(ln["turned"], KC * n + c + 1)
                    sc.activation(xh[:, c, n * GN:(n + 1) * GN], ps[:, first_bank + c, :], ACT.Copy)\
                        .then_inc(ln["hi"], 1)

            def x_proj(n):
                for j in range(KC):
                    act.wait_ge(s_proj, KC * n + j + 1)
                    act.wait_ge(s_bin2, 1)
                    sc.activation(xq_t[:, j, n * GN:(n + 1) * GN], ps[:, 2 + j, :], ACT.Identity,
                                  bias=b_in2[:, j:j + 1]).then_inc(s_projc, 1)

            def gate_z(n, c):
                act.wait_ge(s_zp, KC * n + c + 1)
                sc.activation(z_t[:, c, n * GN:(n + 1) * GN], ps[:, 4 + c, :], ACT.Silu,
                              bias=b_in2[:, KC + c:KC + c + 1]).then_inc(s_zc, 1)

            powers(0)
            act.wait_ge(s_winf, KC)
            sc.activation(wih[:], winf, ACT.Copy).then_inc(s_wih, 1)
            act.wait_ge(s_bin2, 1)
            sc.activation(dt_mean[:], ps[:, 7, 32:33], ACT.Copy).then_inc(s_dtm, 1)
            hi_parts(lns[0], 0, 0)
            powers(1)
            powers(2)
            hi_parts(lns[0], 1, 4)
            x_proj(0)
            powers(3)
            hi_parts(lns[0], 2, 0)
            act.wait_ge(s_amean, 1)
            sc.activation(amean[:], ps[:, 7, 0:2 * NS], ACT.Copy).then_inc(s_am_sb, 1)
            x_proj(1)
            act.wait_ge(s_am_t, 1)
            sc.activation(amean_t[:], ps[0:2 * NS, 7, 64:64 + P], ACT.Copy).then_inc(s_amt_sb, 1)
            hi_parts(lns[0], 3, 4)
            x_proj(2)
            x_proj(3)
            gate_z(0, 0)
            gate_z(0, 1)
            act.wait_ge(s_mir, 1)
            sc.activation(bmir[:].rearrange("p c s b -> p (c s b)"), ps[:, 0, 0:2 * NS * B], ACT.Copy)\
                .then_inc(s_mirc, 1)
            gate_z(1, 0)
            gate_z(1, 1)
            gate_z(2, 0)
            gate_z(2, 1)
            act.wait_ge(s_conv, 1)
            sc.activation(xmh[:].rearrange("p c s b -> p (c s b)"), ps[:, 1, 0:2 * NS * B], ACT.Copy).then_inc(s_xm, 1)
            act.wait_ge(s_xm, 1)
            for k in (0, 2):
                sc.activation(xm3[:, :, k, :, :].rearrange("p c s b -> p c (s b)"),
                              xmh[:].bitcast(F32).rearrange("p c s b -> p c (s b)"), ACT.Copy).then_inc(s_xm, 1)
            gate_z(3, 0)
            gate_z(3, 1)
            for n in range(NG):
                act.wait_ge(s_xmt, n + 1)
                sc.activation(xm_t[:, n * GN:(n + 1) * GN], ps[0:3 * NS, n, :], ACT.Copy).then_inc(s_xmtc, 1)
            for n in range(NG + 2):
                if n < NG:
                    for c in range(KC):
                        act.wait_ge(s_y, KC * n + c + 1)
                        wait(act, s_o, 2 * (n - 1))
                        sc.activation(yh[n % 2][:, c, :], ybuf[n % 2][:, c, :], ACT.Copy).then_inc(s_yh, 1)
                if n >= 2:
                    act.wait_ge(s_shift, n - 1)
                    for t in range((n - 2) * GT, (n - 1) * GT):
                        sc.activation(x1[:, t, :], x_tm[:, t, :], ACT.Identity, bias=shift[:, t:t + 1],
                                      scale=rstd[:, t:t + 1]).then_inc(s_x1, 1)
                    for c in range(KC):
                        act.wait_ge(s_x1t, KC * (n - 2) + c + 1)
                        sc.activation(xq_t[:, c, (n - 2) * GN:(n - 1) * GN], ps[:, c, :], ACT.Copy).then_inc(s_q, 1)

            sc.activation(fa[0:1, 0:1], ident[0:1, 0:1], ACT.Exp).then_inc(s_fa, 1)
            act.wait_ge(s_g, NG)
            sc.activation(small[:].rearrange("p t g -> p (t g)"), ps[:, 6, 0:T * 2 * NH], ACT.Copy)\
                .then_inc(s_gc, 1)
            act.wait_ge(s_gt, 1)
            sc.activation(fa[:], ps[:, 7, S:2 * S], ACT.Abs, bias=col[:, C_GB + 1:C_GB + 2]).then_inc(s_fa, 1)
            act.wait_ge(s_fa, 2)
            sc.activation(fe[:], fa[:], ACT.Exp, scale=-1.0).then_inc(s_fe, 1)
            act.wait_ge(s_fe, 1)
            sc.activation(fl[:], fe[:], ACT.Ln, bias=1.0).then_inc(s_fl, 1)

            def copy_qk(k):
                b, gi, bank = COPIED[k]
                act.wait_ge(s_qk, EARLY.index(COPIED[k]) + 1)
                sc.activation(qk_early[:, k, :], ps[:, bank, :], ACT.Copy).then_inc(s_qkc, 1)

            first = [k for k in range(len(COPIED)) if EARLY.index(COPIED[k]) < EARLY_FIRST]
            for k in first:
                copy_qk(k)
            act.wait_ge(s_row_step, 7)
            sc.activation(wx[:], g[:, 0:P], ACT.Exp, bias=nr127[:, 0:1]).then_inc(s_wx, 1)
            act.wait_ge(s_row_step, 5)
            sc.activation(e1[:], mx[:, P:S], ACT.Exp, scale=-1.0, bias=mx[:, P - 1:P]).then_inc(s_e1, 1)
            act.wait_ge(s_row_step, 8)
            sc.activation(em[:], mld[:], ACT.Exp, scale=-1.0).then_inc(s_em, 1)
            for k in range(len(first), len(COPIED)):
                copy_qk(k)

            def act_step(b, i, first=False):
                def decay(gi):
                    g_ = b * 4 + gi
                    act.wait_ge(s_sc, g_ + 1)
                    wait(act, s_c, g_ - 1)
                    sc.activation(dec[:, gi % 2, :, :].rearrange("p h s -> p (h s)"), ps[:, gi % 2, :],
                                  ACT.Exp).then_inc(s_dec, 1)
                decay(0)
                decay(1)
                if not first:
                    square(b - 1, 1 - i)
                decay(2)
                decay(3)
                act.wait_ge(s_num, b * 4 + 2)
                wait(act, s_hn, b - 1)
                sc.activation(nm[i][:, 0, :, :].rearrange("p h d -> p (h d)"), ps[:, 4, 0:NH * DV],
                              ACT.Copy).then_inc(s_n0, 1)

            def square(b, i):
                act.wait_ge(s_n0, b + 1)
                act.wait_ge(s_n1, b + 1)
                sc.activation(sq[:], nm[i][:, :, :, 0:DH], ACT.Square).then_inc(s_sq, 1)

            act_step(0, 0, first=True)
            act_step(1, 1)
            act_step(2, 0)
            with act.Fori(0, B // 2 - 2) as it:
                act_step(it * 2 + 3, 1)
                act_step(it * 2 + 4, 0)
            act_step(B - 1, 1)
            hi_parts(lns[1], 0, 6)
            hi_parts(lns[1], 1, 2)
            square(B - 1, 1)

            def silu(e, n):
                u = e * NG + n
                for f in range(KC):
                    act.wait_ge(s_ab, u * KC + (f + 1))
                    if not isinstance(e, int) or u >= 1:
                        act.wait_ge(s_h, (u - 1) * KC + (f + 1))
                    sc.activation(sil[:, f, :], ps[:, 2 * f, :], ACT.Silu).then_inc(s_sil, 1)
                    act.wait_ge(s_h, u * KC + (f + 1))
                    if not isinstance(e, int) or u >= 2:
                        act.wait_ge(s_yr, (u - 1) * 2)
                    sc.activation(hh[n % 2][:, f, :], hbuf[:, f, :], ACT.Copy).then_inc(s_hh, 1)

            silu(0, 0)
            hi_parts(lns[1], 2, 6)
            silu(0, 1)
            silu(0, 2)
            hi_parts(lns[1], 3, 6)
            silu(0, 3)
            for n in range(NG):
                act.wait_ge(s_lg, n + 1)
                sc.activation(lgt[:, n * GN:(n + 1) * GN], ps[0:NE, 6 + n % 2, :], ACT.Copy).then_inc(s_lgc, 1)
            silu(1, 0)
            act.wait_ge(s_gate, 1)
            sc.activation(pe_[:], lg[:], ACT.Exp, scale=-1.0).then_inc(s_pexp, 1)
            for n in range(1, NG):
                silu(1, n)
            with act.Fori(0, NE // 2 - 1) as it:
                for odd in range(2):
                    for n in range(NG):
                        silu(it * 2 + (2 + odd), n)
            for n in range(NG):
                silu(NE, n)

        @block.vector
        def _(dve):
            v = nc.vector

            def moments(n, src, sems, negate=False, tiles=None):
                st, ag, ve, rs_ = sems
                lo_, hi_ = tiles or (n * GT, (n + 1) * GT)
                for t in range(lo_, hi_):
                    v.bn_stats(stats[:, t, :], src[:, t, :]).then_inc(st, 1)
                for t in range(lo_, hi_):
                    dve.wait_ge(st, t + 1)
                    v.bn_aggr(mv[:, t, :], stats[:, t, :]).then_inc(ag, 1)
                dve.wait_ge(ag, hi_)
                if negate:
                    v.tensor_scalar(shift[:, lo_:hi_], mv[:, lo_:hi_, 0], -1.0, None, ALU.mult).then_inc(s_neg, 1)
                v.tensor_scalar(rstd[:, lo_:hi_], mv[:, lo_:hi_, 1], EPS, None, ALU.add).then_inc(ve, 1)

            def normalise(n, src, sems, done_norm, dst, tiles=None):
                lo_, hi_ = tiles or (n * GT, (n + 1) * GT)
                dve.wait_ge(sems[3], n + 1)
                for t in range(lo_, hi_):
                    v.tensor_scalar(dst(t), src[:, t, :], mv[:, t, 0:1], rstd[:, t:t + 1],
                                    ALU.subtract, ALU.mult).then_inc(done_norm, 1)

            def stats_of(n, src, sems, done_norm, dst):
                moments(n, src, sems)
                normalise(n, src, sems, done_norm, dst)

            v.memset(inv_d[:], 1.0 / D).then_inc(s_inv, 1)
            dve.wait_ge(s_col, 16)
            v.tensor_scalar(log_a[:], col[:, C_ALOG:C_ALOG + KC * NS].rearrange("p (c s) -> p c s", c=KC),
                            80.0, None, ALU.min).then_inc(s_decay_step, 1)
            dve.wait_ge(s_edt, 1)
            v.tensor_scalar(dt[:], dt[:], 1e-4, 1.0, ALU.max, ALU.min).then_inc(s_decay_step, 1)
            dve.wait_ge(s_decay_step, 2)
            dve.wait_ge(s_ea, 1)
            v.tensor_tensor(log_a[:], log_a[:], dt[:].unsqueeze(2).broadcast_to([P, KC, NS]), ALU.mult)\
                .then_inc(s_decay_step, 1)
            dve.wait_ge(s_decay_step, 3)
            v.tensor_scalar(log_a[:], log_a[:], LOG_FLOOR, -1.0, ALU.min, ALU.mult).then_inc(s_decay_step, 1)
            dve.wait_ge(s_tstep_i, 1)
            v.tensor_copy(tsteps[:], tsteps_i[:]).then_inc(s_decay_step, 1)
            dve.wait_ge(s_decay_step, 5)
            v.memset(half_pow[:, :, :, 0], 1.0 / D).then_inc(s_inv, 1)

            def exponents(q):
                dims = [P, 4, KC, P]
                v.tensor_tensor(decay_pow[:, 4 * q:4 * q + 4, :, :],
                                tsteps[:].unsqueeze(1).unsqueeze(1).broadcast_to(dims),
                                log_a[:, :, 4 * q:4 * q + 4].rearrange("p c s -> p s c").unsqueeze(3)
                                .broadcast_to(dims), ALU.mult).then_inc(s_dmul, 1)

            def lo_parts(ln, n, first_bank):
                for c in range(KC):
                    dve.wait_ge(ln["hi"], KC * n + c + 1)
                    v.tensor_tensor(xl[:, c, n * GN:(n + 1) * GN], ps[:, first_bank + c, :],
                                    xh[:, c, n * GN:(n + 1) * GN].bitcast(F32), ALU.subtract)\
                        .then_inc(ln["lo"], 1)

            ln = lns[0]
            ln1_sems = (ln["stats"], ln["aggr"], ln["vareps"], ln["rstd"])

            def moments1(n):
                dve.wait_ge(s_x[n], 16)
                moments(n, x_tm, ln1_sems)

            def normalise1(n):
                normalise(n, x_tm, ln1_sems, ln["normed"], lambda t: x1[:, t, :])

            exponents(0)
            moments1(0)
            dve.wait_ge(s_win, 16)
            for c in range(KC):
                v.tensor_scalar(winf[:, c, :], win[:, c, :], col[:, C_LNG + c:C_LNG + c + 1], None, ALU.mult)\
                    .then_inc(s_winf, 1)
            normalise1(0)
            dve.wait_ge(s_bias, 1)
            v.tensor_tensor(b_in2[:], ps[:, 7, 200:204], col[:, C_BIN:C_BIN + 4], ALU.add).then_inc(s_bin2, 1)
            dve.wait_ge(s_p128, 1)
            v.tensor_scalar(half_pow[:, :, :, 1], half_pow[:, :, :, 1], 1.0 / D, None, ALU.mult)\
                .then_inc(s_decay_step, 1)
            dve.wait_ge(s_wih, 1)
            v.tensor_tensor(wil[:], winf, wih[:].bitcast(F32), ALU.subtract).then_inc(s_wil, 1)
            moments1(1)
            lo_parts(ln, 0, 0)
            normalise1(1)
            exponents(1)
            exponents(2)
            moments1(2)
            lo_parts(ln, 1, 4)
            normalise1(2)
            exponents(3)
            moments1(3)
            normalise1(3)
            lo_parts(ln, 2, 0)
            dve.wait_ge(s_row, 16)
            v.tensor_scalar(b_half, b_out_row, 0.5, None, ALU.mult).then_inc(s_bhalf, 1)
            lo_parts(ln, 3, 4)
            dve.wait_ge(s_wc, 3 * 16)
            v.tensor_copy(wc3[:], wc[:]).then_inc(s_wc3, 1)
            dve.wait_ge(s_wc3, 1)
            lo = slice(2 * NS, 3 * NS)
            v.tensor_tensor(wc3[lo, :], wc[lo, :], wc3[lo, :].bitcast(F32), ALU.subtract).then_inc(s_wc3, 1)
            dve.wait_ge(s_bp, NG)
            dve.wait_ge(s_dtm, 1)
            v.tensor_scalar(bproj[:].rearrange("p c s b -> p (c s b)"),
                            ps[:, 7, 2 * NS * B:4 * NS * B], dt_mean[:, 0:1],
                            None, ALU.mult).then_inc(s_bps, 1)
            dve.wait_ge(s_xm, 1)
            v.tensor_tensor(xm3[:, :, 1, :, :].rearrange("p c s b -> p c (s b)"),
                            ps[:, 1, 0:2 * NS * B].rearrange("p (c n) -> p c n", c=2),
                            xmh[:].bitcast(F32).rearrange("p c s b -> p c (s b)"), ALU.subtract).then_inc(s_xm3, 1)
            dve.wait_ge(s_zp, KC * NG)
            dve.wait_ge(s_zc, KC * NG)
            r1_sems = (s_st1, s_ag1, s_ve1, s_rs1)
            for n in range(NG + 1):
                if n < NG:
                    yb = ybuf[n % 2]
                    for c in range(KC):
                        sl = slice(n * GN, (n + 1) * GN)
                        dve.wait_ge(s_wcd, KC * n + c + 1)
                        wait(dve, s_yl, KC * (n - 2) + c + 1)
                        v.scalar_tensor_tensor(yb[:, c, :], xq_t[:, c, sl], col[:, C_DSKIP + c:C_DSKIP + c + 1],
                                               ps[:, 4 + c, :], ALU.mult, ALU.add).then_inc(s_u, 1)
                    for c in range(KC):
                        dve.wait_ge(s_u, KC * n + c + 1)
                        v.tensor_tensor(yb[:, c, :], yb[:, c, :], z_t[:, c, n * GN:(n + 1) * GN], ALU.mult)\
                            .then_inc(s_y, 1)
                if n >= 1:
                    m = n - 1
                    dve.wait_ge(s_x2b, m + 1)
                    for k in range(2):
                        dve.wait_ge(s_o, 2 * m + k + 1)
                        xt = x_tm[:, m * GT + 2 * k:m * GT + 2 * k + 2, :].rearrange("p t d -> p (t d)")
                        v.scalar_tensor_tensor(xt, xt, 2.0, ps[:, 2 + k, :], ALU.mult, ALU.add).then_inc(s_r, 1)
                    dve.wait_ge(s_r, 2 * n)
                    moments(m, x_tm, r1_sems, negate=True)

            def head_means(b, i):
                if isinstance(b, int) and b < 2:
                    dve.wait_ge(s_in[i], 6 * 16)
                else:
                    dve.wait_ge(s_in[i], (b + (2 - i)) * (B * 8) if not isinstance(b, int) else 128 * (b // 2 + 1))
                wait(dve, s_vm, b)
                v.tensor_reduce(vsum[:], ctb[i][:].rearrange("p c (h d) -> p c h d", h=NH), X, ALU.add)\
                    .then_inc(s_vs, 1)
                dve.wait_ge(s_vs, b + 1)
                wait(dve, s_vb, b)
                v.tensor_scalar(vmean[:], vsum[:], 1.0 / DH, None, ALU.mult).then_inc(s_vm, 1)

            dve.wait_ge(s_gc, 1)
            gv = small[:].rearrange("p (b c) (i h) -> p c i b h", c=2, i=2)
            for c in range(2):
                for dup in range(2):
                    v.tensor_copy(gsel[:, c, :, dup, :, :], gv[:, c, :, :, :]).then_inc(s_gs, 1)
            dve.wait_ge(s_gt, 1)
            dve.wait_ge(s_fa, 2)
            v.tensor_scalar(fm[:], ps[:, 7, S:2 * S], col[:, C_GB + 1:C_GB + 2], 0.0, ALU.add, ALU.min)\
                .then_inc(s_row_step, 1)
            head_means(0, 0)
            dve.wait_ge(s_row_step, 1)
            dve.wait_ge(s_fl, 1)
            v.tensor_tensor(ls[:], fm[:], fl[:], ALU.subtract).then_inc(s_row_step, 1)
            dve.wait_ge(s_row_step, 2)
            v.tensor_tensor_scan(fcum[:], ones[:], ls[:], 0.0, ALU.mult, ALU.add).then_inc(s_row_step, 1)
            dve.wait_ge(s_row_step, 3)
            v.scalar_tensor_tensor(g[:], ps[:, 7, 0:S], col[:, C_GB:C_GB + 1], fcum[:], ALU.add, ALU.subtract)\
                .then_inc(s_row_step, 1)
            dve.wait_ge(s_row_step, 4)
            v.tensor_tensor_scan(mx[:], g[:], g[:], -3e38, ALU.max, ALU.max).then_inc(s_row_step, 1)
            H = B * NH
            v.tensor_copy(gm[:, 0, :], g[:]).then_inc(s_gh, 1)
            dve.wait_ge(s_row_step, 5)
            v.tensor_scalar(nmx[:], mx[:], -1.0, None, ALU.mult).then_inc(s_row_step, 1)
            dve.wait_ge(s_gh, 1)
            v.tensor_tensor(gm[H:, 0, :], g[H:, :], gm[H:, 0, :].bitcast(F32), ALU.subtract).then_inc(s_gl, 1)
            dve.wait_ge(s_row_step, 6)
            v.tensor_copy(gm[:, 1, :], nmx[:]).then_inc(s_gh, 1)
            v.tensor_scalar(nr127[:], mx[:, P - 1:P], -1.0, None, ALU.mult).then_inc(s_row_step, 1)
            dve.wait_ge(s_gh, 2)
            v.tensor_tensor(gm[H:, 1, :], nmx[H:, :], gm[H:, 1, :].bitcast(F32), ALU.subtract).then_inc(s_gl, 1)
            v.tensor_tensor(mld[:], fcum[:], mx[:], ALU.add).then_inc(s_row_step, 1)
            dve.wait_ge(s_tt, 1)
            v.tensor_copy(tok[:, 0:3, :].rearrange("p k r -> p (k r)"), ps[:, 6, 0:3 * H]).then_inc(s_tok, 1)
            v.tensor_scalar(tok[:, 3, :], ps[:, 6, 3 * H:4 * H], QK_SCALE, None, ALU.mult).then_inc(s_tok, 1)
            head_means(1, 1)

            def decayed(b, gi):
                g_ = b * 4 + gi
                dve.wait_ge(s_dec, g_ + 1)
                wait(dve, s_num, g_ - 3)
                k = copied_at(b, gi)
                if k is not None:
                    dve.wait_ge(s_qkc, k + 1)
                elif isinstance(b, int) and (b, gi) in [e[:2] for e in EARLY]:
                    dve.wait_ge(s_qk, len(EARLY))
                else:
                    dve.wait_ge(s_qkr, qk_count(b, gi))
                v.scalar_tensor_tensor(cmat[:, gi, :, :].rearrange("p h s -> p (h s)"),
                                       ps[:, 2 + gi % 2, :] if k is None else qk_early[:, k, :], QK_SCALE,
                                       dec[:, gi % 2, :, :].rearrange("p h s -> p (h s)"),
                                       ALU.mult, ALU.mult).then_inc(s_c, 1)

            def mask_state(b):
                dve.wait_ge(s_st, b + 1)
                wait(dve, s_int, b)
                v.tensor_tensor(state[:].rearrange("p c h d -> p c (h d)"),
                                ps[:, 7, 0:2 * HG * DV].rearrange("p (c n) -> p c n", c=KC),
                                block_mask[:].rearrange("p h d -> p (h d)").unsqueeze(1)
                                .broadcast_to([P, KC, HG * DV]), ALU.mult).then_inc(s_sbd, 1)

            def carried(b):
                dve.wait_ge(s_int, b + 1)
                v.tensor_tensor(carry[:], ps[:, 6, 0:NH * DV].rearrange("p (h d) -> p h d", h=NH),
                                tok[:, 2, bass.ds(b * NH, NH)].unsqueeze(2).broadcast_to([P, NH, DV]),
                                ALU.mult).then_inc(s_car, 1)

            def normaliser(b, i):
                dve.wait_ge(s_car, b + 1)
                dve.wait_ge(s_num, b * 4 + 4)
                v.tensor_tensor(nm[i][:, 1, :, :].rearrange("p h d -> p (h d)"), ps[:, 5, 0:NH * DV],
                                carry[:].rearrange("p h d -> p (h d)"), ALU.add).then_inc(s_n1, 1)
                dve.wait_ge(s_n1, b + 1)
                dve.wait_ge(s_n0, b + 1)
                v.tensor_tensor(nrm[:], nm[i][:, :, :, DH], tok[:, 0:2, bass.ds(b * NH, NH)], ALU.max)\
                    .then_inc(s_norm_step, 1)
                dve.wait_ge(s_norm_step, b * 5 + 1)
                v.scalar_tensor_tensor(nrm[:], nm[i][:, :, :, DH], -1.0, nrm[:], ALU.mult, ALU.max)\
                    .then_inc(s_norm_step, 1)
                dve.wait_ge(s_norm_step, b * 5 + 2)
                v.tensor_scalar(nrm[:], nrm[:], 1e-6, None, ALU.add).then_inc(s_norm_step, 1)
                dve.wait_ge(s_norm_step, b * 5 + 3)
                v.reciprocal(rec[:], nrm[:]).then_inc(s_norm_step, 1)
                dve.wait_ge(s_norm_step, b * 5 + 4)
                v.tensor_tensor(rec2[:], rec[:], rec[:], ALU.mult).then_inc(s_norm_step, 1)

            def variance(b):
                dve.wait_ge(s_sq, b + 1)
                v.tensor_reduce(ssum[:], sq[:], X, ALU.add).then_inc(s_var_step, 1)
                dve.wait_ge(s_var_step, b * 3 + 1)
                dve.wait_ge(s_norm_step, b * 5 + 5)
                v.tensor_tensor(ssum[:], ssum[:], rec2[:], ALU.mult).then_inc(s_var_step, 1)
                dve.wait_ge(s_var_step, b * 3 + 2)
                v.tensor_scalar(var[:], ssum[:], 1.0 / DH, EPS, ALU.mult, ALU.add).then_inc(s_var_step, 1)

            def head_norm(b, i):
                dve.wait_ge(s_rsd, b + 1)
                v.tensor_tensor(rr[:], rsd[:], rec[:], ALU.mult).then_inc(s_rr, 1)
                dve.wait_ge(s_rr, b + 1)
                v.tensor_tensor(hn[:], nm[i][:, :, :, 0:DH], rr[:].unsqueeze(3).broadcast_to([P, 2, NH, DH]),
                                ALU.mult).then_inc(s_hn, 1)

            ln = lns[1]

            def stats2(b, i):
                for k in range(2):
                    v.bn_stats(stats[:, 2 * i + k, :], x_tm[:, bass.ds(b * 2 + k, 1), :]
                               .rearrange("p t d -> p (t d)")).then_inc(ln["stats"], 1)

            def moments2(b, i):
                for k in range(2):
                    v.bn_aggr(mv[:, 2 * i + k, :], stats[:, 2 * i + k, :]).then_inc(ln["aggr"], 1)
                dve.wait_ge(ln["aggr"], b * 2 + 2)
                v.tensor_scalar(rstd[:, 2 * i:2 * i + 2], mv[:, 2 * i:2 * i + 2, 1], EPS, None, ALU.add)\
                    .then_inc(ln["vareps"], 1)

            def normalise2(b, i):
                dve.wait_ge(ln["rstd"], b + 1)
                for k in range(2):
                    v.tensor_scalar(acc[:, bass.ds(b * 2 + k, 1), :].rearrange("p t d -> p (t d)"),
                                    x_tm[:, bass.ds(b * 2 + k, 1), :].rearrange("p t d -> p (t d)"),
                                    mv[:, 2 * i + k, 0:1], rstd[:, 2 * i + k:2 * i + k + 1],
                                    ALU.subtract, ALU.mult).then_inc(ln["normed"], 1)

            def dve_step(b, i):
                dynamic = not isinstance(b, int)
                decayed(b, 0)
                decayed(b, 1)
                if dynamic or b >= 2:
                    head_norm(b - 2, i)
                if dynamic or b >= 1:
                    normaliser(b - 1, 1 - i)
                mask_state(b)
                if dynamic or 1 <= b < B - 1:
                    head_means(b + 1, 1 - i)
                decayed(b, 2)
                if dynamic or b >= 1:
                    variance(b - 1)
                if dynamic or b >= 3:
                    normalise2(b - 3, 1 - i)
                if dynamic or b >= 2:
                    dve.wait_ge(s_r2, b - 1)
                decayed(b, 3)
                if dynamic or b >= 2:
                    stats2(b - 2, i)
                    dve.wait_ge(ln["stats"], b * 2 - 2)
                carried(b)
                if dynamic or b >= 2:
                    moments2(b - 2, i)

            dve.wait_ge(s_tok, 2)
            for b in range(3):
                dve_step(b, b % 2)
            with dve.Fori(0, B // 2 - 2) as it:
                dve_step(it * 2 + 3, 1)
                dve_step(it * 2 + 4, 0)
            dve_step(B - 1, 1)

            def hidden(e, n, fs=range(KC)):
                u = e * NG + n
                for f in fs:
                    dve.wait_ge(s_sil, u * KC + (f + 1))
                    if not isinstance(e, int) or u >= 1:
                        dve.wait_ge(s_hl, (u - 1) * KC + (f + 1))
                    v.tensor_tensor(hbuf[:, f, :], sil[:, f, :], ps[:, 2 * f + 1, :], ALU.mult).then_inc(s_h, 1)

            def accumulate(e, n, ks=range(GT)):
                u = e * NG + n
                for k in ks:
                    t = n * GT + k
                    dve.wait_ge(s_yr, u * 2 + (k // 2 + 1))
                    y = ps[:, 4 + k // 2, (k % 2) * D:(k % 2 + 1) * D]
                    if isinstance(e, int) and e == 0:
                        v.tensor_tensor(acc[:, t, :], y, acc[:, t, :], ALU.add).then_inc(s_acc, 1)
                    else:
                        dve.wait_ge(s_acc, (u - NG) * GT + (k + 1))
                        v.scalar_tensor_tensor(acc[:, t, :], y, ge[:, t, bass.ds(e - 1, 1)], acc[:, t, :],
                                               ALU.mult, ALU.add).then_inc(s_acc, 1)

            def dve_expert(e, odd):
                for n in range(NG):
                    hidden(e, n)
                    accumulate(*unit_before(e, n, odd)[:2])

            out_sems = (s_fst, s_fag, s_fve, s_frs)

            def moments3(n):
                dve.wait_ge(s_acc, GT * (U - 4 + n + 1))
                moments(n, acc, out_sems)

            def normalise3(n):
                normalise(n, acc, out_sems, s_fout, lambda t: acc[:, t, :])

            bc = [P, T, NE]
            step = [0]

            def then(ins):
                step[0] += 1
                ins.then_inc(s_gate, 1)
                dve.wait_ge(s_gate, step[0])

            def add_gate_bias():
                dve.wait_ge(s_lg, NG + 1)
                then(v.tensor_tensor(lg[:], ps[:, 7, 0:T * NE].rearrange("p (t e) -> p t e", t=T),
                                     gate_b_row.unsqueeze(1).broadcast_to(bc), ALU.add))

            def gating():
                dve.wait_ge(s_pexp, 1)
                then(v.tensor_scalar(pe_[:], pe_[:], 1.0, None, ALU.add))
                then(v.reciprocal(pr[:], pe_[:]))

                def pick(p, m, onehot_out):
                    then(v.tensor_reduce(m[:], p[:], X, ALU.max))
                    then(v.tensor_tensor(eq[:], p[:], m[:].unsqueeze(2).broadcast_to(bc), ALU.is_equal))
                    then(v.tensor_tensor(kk[:], eq[:], prio[:].unsqueeze(1).broadcast_to(bc), ALU.mult))
                    then(v.tensor_reduce(km[:], kk[:], X, ALU.max))
                    then(v.tensor_tensor(onehot_out[:], kk[:], km[:].unsqueeze(2).broadcast_to(bc), ALU.is_equal))

                pick(pr, m1, oh1)
                then(v.scalar_tensor_tensor(p1[:], oh1[:], -2.0, pr[:], ALU.mult, ALU.add))
                pick(p1, m2, oh2)
                then(v.tensor_tensor(oh1[:], oh1[:], oh2[:], ALU.add))
                then(v.tensor_tensor(oh1[:], oh1[:], pr[:], ALU.mult))
                then(v.tensor_tensor(m1[:], m1[:], m2[:], ALU.add))
                then(v.tensor_scalar(m1[:], m1[:], 1e-8, None, ALU.add))
                then(v.reciprocal(rw[:], m1[:]))
                then(v.tensor_tensor(ge[:], oh1[:], rw[:].unsqueeze(2).broadcast_to(bc), ALU.mult))

            lo_parts(ln, 0, 6)
            head_norm(B - 2, 0)
            lo_parts(ln, 1, 2)
            normalise2(B - 3, 1)
            normaliser(B - 1, 1)
            variance(B - 1)
            hidden(0, 0, [0])
            dve.wait_ge(s_r2, B - 1)
            stats2(B - 2, 0)
            dve.wait_ge(ln["stats"], T - 2)
            moments2(B - 2, 0)
            hidden(0, 0, [1])
            head_norm(B - 1, 1)
            normalise2(B - 2, 0)
            lo_parts(ln, 2, 6)
            hidden(0, 1)
            dve.wait_ge(s_r2, B)
            stats2(B - 1, 1)
            dve.wait_ge(ln["stats"], T)
            moments2(B - 1, 1)
            accumulate(0, 0)
            normalise2(B - 1, 1)
            hidden(0, 2)
            lo_parts(ln, 3, 6)
            accumulate(0, 1)
            hidden(0, 3)
            accumulate(0, 2)
            hidden(1, 0)
            add_gate_bias()
            accumulate(0, 3)
            hidden(1, 1)
            gating()
            accumulate(1, 0)
            for n in range(2, NG):
                hidden(1, n)
                accumulate(1, n - 1)
            with dve.Fori(0, NE // 2 - 1) as it:
                dve_expert(it * 2 + 2, 0)
                dve_expert(it * 2 + 3, 1)
            hidden(NE, 0)
            accumulate(NE - 1, NG - 1)
            hidden(NE, 1)
            accumulate(NE, 0)
            moments3(0)
            normalise3(0)
            hidden(NE, 2)
            accumulate(NE, 1)
            moments3(1)
            hidden(NE, 3)
            for f in range(KC):
                dve.wait_ge(s_hh, KC * (U - 1) + f + 1)
                v.tensor_tensor(hl[1][:, f, :], hbuf[:, f, :], hh[1][:, f, :].bitcast(F32), ALU.subtract)\
                    .then_inc(s_hl_last, 1)
            accumulate(NE, 2)
            normalise3(1)
            moments3(2)
            for k in range(2):
                accumulate(NE, NG - 1, range(2 * k, 2 * k + 2))
                dve.wait_ge(s_acc, GT * U - 2 + 2 * k)
                moments(NG - 1, acc, out_sems, tiles=(T - GT + 2 * k, T - GT + 2 * k + 2))
                if k == 0:
                    normalise3(2)
            for k in range(2):
                normalise(NG - 1 + k, acc, out_sems, s_fout, lambda t: acc[:, t, :],
                          tiles=(T - GT + 2 * k, T - GT + 2 * k + 2))

        @block.tensor
        def _(pe):
            te = nc.tensor

            def three(out_, wh_, wl_, rh_, rl_, first, last):
                te.matmul(out_, wh_, rh_, start=first, stop=False)
                te.matmul(out_, wl_, rh_, start=False, stop=False)
                return te.matmul(out_, wh_, rl_, start=False, stop=last)

            pe.wait_ge(s_ident, 2)
            pe.wait_ge(s_inv, 1)
            pe.wait_ge(s_decay_step, 2)
            for c in range(KC):
                te.matmul(ps[:, 7, 32:33], inv_d[:], dt[:, c:c + 1], start=c == 0, stop=c == KC - 1)
            pe.wait_ge(s_win, 16)
            for j in range(4):
                for c in range(KC):
                    last = te.matmul(ps[:, 7, 200 + j:201 + j], win[:, c, j * P:(j + 1) * P],
                                     col[:, C_LNB + c:C_LNB + c + 1], start=c == 0, stop=c == KC - 1)
            last.then_inc(s_bias, 1)

            def turn(lnx, n, src, first_bank, banks_read):
                pe.wait_ge(lnx["normed"], GT * (n + 1))
                wait(pe, lnx["lo"], banks_read)
                for c in range(KC):
                    for k in range(GT):
                        last_ = te.transpose(tile_ps(first_bank + c, k), src[:, n * GT + k, c * P:(c + 1) * P],
                                             ident[:])
                    last_.then_inc(lnx["turned"], 1)

            def project(n, j, c):
                sl = slice(n * GN, (n + 1) * GN)
                return three(ps[:, 2 + j, :], wih[:, c, j * P:(j + 1) * P], wil[:, c, j * P:(j + 1) * P],
                             xh[:, c, sl], xl[:, c, sl], c == 0, c == KC - 1)

            def project_x(n, j):
                pe.wait_ge(lns[0]["lo"], KC * (n + 1))
                pe.wait_ge(s_wil, 1)
                wait(pe, s_projc, KC * (n - 1) + j + 1)
                for c in range(KC):
                    last_ = project(n, j, c)
                last_.then_inc(s_proj, 1)

            def project_z(n, j, c):
                pe.wait_ge(lns[0]["lo"], KC * NG)
                wait(pe, s_zc, KC * (n - 1) + j + 1)
                last_ = project(n, KC + j, c)
                if c == KC - 1:
                    last_.then_inc(s_zp, 1)

            def b_proj(t):
                pe.wait_ge(s_projc, KC * (t // GT + 1))
                pe.wait_ge(s_wb, 16)
                pe.wait_ge(s_amt_sb, 1)
                o = 2 * NS * B + (t % 2) * NS * B + t // 2
                for c in range(KC):
                    last_ = te.matmul(ps[:, 7, o:o + (NS - 1) * B + 1:B], xq_t[:, c, t * P:(t + 1) * P], wb[:, c, :],
                                      start=c == 0, stop=c == KC - 1)
                if t % GT == GT - 1:
                    last_.then_inc(s_bp, 1)

            def decay_sums(first, last):
                for s in range(first, last):
                    pe.wait_ge(s_dexp, s // 4 + 1)
                    for c in range(KC):
                        last_ = te.matmul(ps[:, 7, s:s + 2 * NS:NS], decay_pow[:, s, c, :], half_pow[:, c, s, :],
                                          start=c == 0, stop=c == KC - 1)
                return last_

            def context_gates(t):
                pe.wait_ge(s_gwc, 1)
                pe.wait_ge(s_cxt, 16)
                for c in range(KC):
                    te.matmul(gate_ps(t), cx_t[:, c, t * P:(t + 1) * P], gw_ctx[:, c, :],
                              start=t == 0 and c == 0, stop=False)

            turn(lns[0], 0, x1, 0, 0)
            pe.wait_ge(s_bin2, 1)
            pe.wait_ge(s_dtm, 1)
            pe.wait_ge(s_decay_step, 6)
            pe.wait_ge(s_inv, 2)
            decay_sums(0, 4)
            project_x(0, 0)
            project_x(0, 1)
            turn(lns[0], 1, x1, 4, 0)
            decay_sums(4, 8)
            project_x(1, 0)
            decay_sums(8, 12)
            turn(lns[0], 2, x1, 0, KC)
            decay_sums(12, NS).then_inc(s_amean, 1)
            project_x(1, 1)
            pe.wait_ge(s_am_sb, 1)
            te.transpose(ps[0:2 * NS, 7, 64:64 + P], amean[:], ident[:]).then_inc(s_am_t, 1)
            turn(lns[0], 3, x1, 4, KC * 2)
            context_gates(0)
            context_gates(1)
            for n in range(2, NG):
                for j in range(KC):
                    project_x(n, j)
                    for t in range(2 * j, 2 * j + 2):
                        b_proj((n - 2) * GT + t)
            for t in range(2, 4):
                context_gates(t)
            for c in range(KC):
                project_z(0, 0, c)
                for t in range(8 + 4 * c, 12 + 4 * c):
                    b_proj(t)
            for c in range(KC):
                project_z(0, 1, c)

            pe.wait_ge(s_bps, 1)
            pe.wait_ge(s_mirror, 2)
            te.matmul(ps[:, 0, 0:2 * NS * B], mirror[:], bproj[:].rearrange("p c s b -> p (c s b)"),
                      start=True, stop=True).then_inc(s_mir, 1)
            for c in range(KC):
                project_z(1, 0, c)
            pe.wait_ge(s_mirc, 1)
            pe.wait_ge(s_toep, 16)
            both = ps[:, 1, 0:2 * NS * B].rearrange("p (c s b) -> p c s b", c=2, s=NS)

            fills = [(n, j, c) for n in range(1, NG) for j in range(KC) for c in range(KC)][KC:]
            for s in range(NS):
                te.matmul(both[:, :, s, :], toep[:, s, 0:P], bmir[:, :, s, :], start=s == 0, stop=False)
                last = te.matmul(both[:, 1, s, :], toep[:, s, P:S], bmir[:, 0, s, :], start=False, stop=s == NS - 1)
                if s % 2:
                    project_z(*fills[s // 2])
            last.then_inc(s_conv, 1)
            for f in fills[NS // 2:]:
                project_z(*f)
            pe.wait_ge(s_xm, 3)
            pe.wait_ge(s_xm3, 1)
            pe.wait_ge(s_projc, KC * NG)
            for n in range(NG):
                for k in range(GT):
                    t = n * GT + k
                    last = te.transpose(ps[0:3 * NS, n, k * P:(k + 1) * P],
                                        xm3[:, t % 2, :, :, t // 2].rearrange("p k s -> p (k s)"), ident[:])
                last.then_inc(s_xmt, 1)

            def mix(n):
                pe.wait_ge(s_xmtc, n + 1)
                pe.wait_ge(s_wc3, 2)
                pe.wait_ge(s_zc, KC * NG)
                for c in range(KC):
                    wait(pe, s_u, KC * (n - 1) + c + 1)
                    te.matmul(ps[:, 4 + c, :], wc3[:, c * P:(c + 1) * P], xm_t[:, n * GN:(n + 1) * GN],
                              start=True, stop=True).then_inc(s_wcd, 1)

            def out_project(n):
                pe.wait_ge(s_xmtc, NG)
                pe.wait_ge(s_wol, 1)
                pe.wait_ge(s_yl, KC * (n + 1))
                for k in range(GT):
                    wait(pe, s_r, 2 * (n - 1) + k // 2 + 1)
                    for c in range(KC):
                        ks = slice(k * P, (k + 1) * P)
                        last_ = three(ps[:, 2 + k // 2, (k % 2) * D:(k % 2 + 1) * D], yh[n % 2][:, c, ks],
                                      yl[n % 2][:, c, ks], woh[:, c, :], wol[:, c, :], c == 0, c == KC - 1)
                    if k % 2:
                        last_.then_inc(s_o, 1)

            def turn_x1(n):
                pe.wait_ge(s_x1, GT * (n + 1))
                wait(pe, s_q, KC * n)
                for c in range(KC):
                    for k in range(GT):
                        last_ = te.transpose(tile_ps(c, k), x1[:, n * GT + k, c * P:(c + 1) * P], ident[:])
                    last_.then_inc(s_x1t, 1)

            def gates(n):
                pe.wait_ge(s_q, KC * (n + 1))
                for t in range(n * GT, (n + 1) * GT):
                    for c in range(KC):
                        last_ = te.matmul(gate_ps(t), xq_t[:, c, t * P:(t + 1) * P], gw[:, c, :],
                                          start=False, stop=t == T - 1 and c == KC - 1)
                last_.then_inc(s_g, 1)

            def q_k(b, i, gi, bank):
                c, hg = divmod(gi, 2)
                for h in range(HG):
                    last_ = te.matmul(ps[:, bank, h * P:(h + 1) * P],
                                      kbd[i][:, hg, h, c * P:(c + 1) * P], qb[i][:, hg, c * P:(c + 1) * P],
                                      start=True, stop=True)
                return last_

            def early_qk(e):
                b, gi, bank = EARLY[e]
                pe.wait_ge(s_in[b], 6 * 16)
                before = [k for k in range(e) if EARLY[k][2] == bank]
                if before:
                    pe.wait_ge(s_qkc, COPIED.index(EARLY[before[-1]]) + 1)
                elif bank >= 4:
                    pe.wait_ge(s_u, KC * NG)
                elif bank >= 2:
                    pe.wait_ge(s_r, 2 * NG)
                else:
                    pe.wait_ge(s_q, KC * NG)
                q_k(b, b, gi, bank).then_inc(s_qk, 1)

            for n in range(NG + 3):
                if n < NG:
                    mix(n)
                if n >= 1:
                    for t in range(4 + 6 * (n - 1), min(4 + 6 * n, T)):
                        context_gates(t)
                if 1 <= n <= NG:
                    out_project(n - 1)
                if n >= 3:
                    gates(n - 3)
                if 2 <= n <= NG + 1:
                    turn_x1(n - 2)

            pe.wait_ge(s_gs, 4)
            for c in range(2):
                for i in range(2):
                    last = te.transpose(ps[:, 7, i * S + c * P:i * S + (c + 1) * P],
                                        gsel[:, c, i, :, :, :].rearrange("p a b h -> p (a b h)"), ident[:])
            last.then_inc(s_gt, 1)
            for e in range(EARLY_FIRST):
                early_qk(e)
            H = B * NH
            pe.wait_ge(s_em, 1)
            pe.wait_ge(s_e1, 1)
            pe.wait_ge(s_wx, 1)
            for k, src in enumerate((em[0:H, 0:P], em[0:H, P:S], e1[0:H, :], wx[0:H, :])):
                last = te.transpose(ps[:, 6, k * H:(k + 1) * H], src, ident[0:H, 0:H])
            last.then_inc(s_tt, 1)
            for e in range(EARLY_FIRST, len(EARLY)):
                early_qk(e)

            pe.wait_ge(s_tok, 2)
            pe.wait_ge(s_const, 12)
            pe.wait_ge(s_oneh, 4 * 16)

            def scores(b, i, gi):
                c, hg = divmod(gi, 2)
                g_ = b * 4 + gi
                wait(pe, s_dec, g_ - 1)
                if isinstance(b, int) and b == 0:
                    pe.wait_ge(s_qkc, len(COPIED))
                o = ps[:, gi % 2, :]
                te.matmul(o, ident_b[:], mask_b[:].rearrange("p h s -> p (h s)"), start=True, stop=False)
                te.matmul(o, decl[i][:, c * P:(c + 1) * P],
                          decr[i][:, hg * HG:(hg + 1) * HG, c * P:(c + 1) * P], start=False, stop=True)\
                    .then_inc(s_sc, 1)
                if isinstance(b, int) and (b, gi) in [e[:2] for e in EARLY]:
                    return
                wait(pe, s_c, g_ - 1)
                q_k(b, i, gi, 2 + gi % 2).then_inc(s_qkr, 1)

            def numerator(b, i, gi):
                c, hg = divmod(gi, 2)
                pe.wait_ge(s_c, b * 4 + (gi + 1))
                pe.wait_ge(s_vb, b + 1)
                wait(pe, s_n1 if c else s_n0, b)
                for h in range(HG):
                    hd = hg * HG + h
                    last_ = te.matmul(ps[:, 4 + c, hd * DV:(hd + 1) * DV], cmat[:, gi, h, :],
                                      vb[i][:, c, hd, :], start=True, stop=True)
                last_.then_inc(s_num, 1)

            def state_sum(b, i):
                pe.wait_ge(s_wv, b + 1)
                wait(pe, s_sbd, b)
                for hg in range(2):
                    last_ = te.matmul(ps[:, 7, hg * HG * DV:(hg + 1) * HG * DV], ctb[i][:, 0, hg * P:(hg + 1) * P],
                                      wv[:, hg * HG:(hg + 1) * HG, :].rearrange("p h d -> p (h d)"),
                                      start=True, stop=True)
                last_.then_inc(s_st, 1)

            def carry_sum(b, i):
                pe.wait_ge(s_sbd, b + 1)
                wait(pe, s_car, b)
                for hg in range(2):
                    last_ = te.matmul(ps[:, 6, hg * HG * DV:(hg + 1) * HG * DV], qb[i][:, hg, P:S],
                                      state[:, hg, :, :].rearrange("p h d -> p (h d)"), start=True, stop=True)
                last_.then_inc(s_int, 1)

            def pe_step(b, i, first=False):
                pe.wait_ge(s_in[i], (b + (2 - i)) * (B * 8) if not isinstance(b, int) else 128 * (b // 2 + 1))
                scores(b, i, 0)
                if not first:
                    numerator(b - 1, 1 - i, 2)
                scores(b, i, 1)
                if not first:
                    numerator(b - 1, 1 - i, 3)
                state_sum(b, i)
                scores(b, i, 2)
                numerator(b, i, 0)
                scores(b, i, 3)
                carry_sum(b, i)
                numerator(b, i, 1)

            pe_step(0, 0, first=True)
            pe_step(1, 1)
            pe_step(2, 0)
            with pe.Fori(0, B // 2 - 2) as it:
                pe_step(it * 2 + 3, 1)
                pe_step(it * 2 + 4, 0)
            pe_step(B - 1, 1)

            def up(e, n, odd, second_banks_read=0):
                u = e * NG + n
                pe.wait_ge(s_wl, e * 3 + 3)
                sl = slice(n * GN, (n + 1) * GN)
                for f in range(KC):
                    if f == 1:
                        wait(pe, lns[1]["lo"], second_banks_read)
                    if not isinstance(e, int) or u >= 1:
                        pe.wait_ge(s_h, (u - 1) * KC + (f + 1))
                    for m in range(2):
                        for c in range(KC):
                            fs = slice(f * P, (f + 1) * P)
                            last_ = three(ps[:, 2 * f + m, :], wh[odd][:, m, c, fs], wl[odd][:, m, c, fs],
                                          xh[:, c, sl], xl[:, c, sl], c == 0, c == KC - 1)
                    last_.then_inc(s_ab, 1)

            def down(e, n, odd):
                u = e * NG + n
                if is_last(e, n):
                    pe.wait_ge(s_hl_last, KC)
                else:
                    pe.wait_ge(s_hl, u * KC + KC)
                for k in range(GT):
                    if not isinstance(e, int) or u >= 1:
                        pe.wait_ge(s_acc, (u - 1) * GT + (2 * (k // 2) + 2))
                    for f in range(KC):
                        last_ = three(ps[:, 4 + k // 2, (k % 2) * D:(k % 2 + 1) * D],
                                      hh[n % 2][:, f, k * P:(k + 1) * P], hl[n % 2][:, f, k * P:(k + 1) * P],
                                      wh[odd][:, 2, f, :], wl[odd][:, 2, f, :], f == 0, f == KC - 1)
                    if k % 2:
                        last_.then_inc(s_yr, 1)

            def pe_expert(e, odd):
                for n in range(NG):
                    up(e, n, odd)
                    down(*unit_before(e, n, odd))

            def logits(n):
                pe.wait_ge(s_wr2, 2)
                wait(pe, s_lgc, n - 1)
                for c in range(KC):
                    sl = slice(n * GN, (n + 1) * GN)
                    last_ = three(ps[0:NE, 6 + n % 2, :], wrh[:, c, :], wrl[:, c, :], xh[:, c, sl], xl[:, c, sl],
                                  c == 0, c == KC - 1)
                last_.then_inc(s_lg, 1)

            numerator(B - 1, 1, 2)
            numerator(B - 1, 1, 3)
            pe.wait_ge(s_car, B)
            pe.wait_ge(s_sbd, B)
            turn(lns[1], 0, acc, 6, 0)
            pe.wait_ge(s_c, 4 * B)
            turn(lns[1], 1, acc, 2, 0)
            pe.wait_ge(s_dec, 4 * B)
            pe.wait_ge(lns[1]["lo"], KC)
            up(0, 0, 0, KC * 2)
            turn(lns[1], 2, acc, 6, KC)
            up(0, 1, 0)
            pe.wait_ge(s_n0, B)
            pe.wait_ge(s_n1, B)
            down(0, 0, 0)
            pe.wait_ge(lns[1]["lo"], KC * 3)
            up(0, 2, 0)
            turn(lns[1], 3, acc, 6, KC * 3)
            down(0, 1, 0)
            pe.wait_ge(lns[1]["lo"], KC * 4)
            up(0, 3, 0)
            logits(0)
            logits(1)
            down(0, 2, 0)
            logits(2)
            logits(3)
            up(1, 0, 1)
            pe.wait_ge(s_lgc, NG)
            for t in range(T):
                last = te.transpose(ps[:, 7, t * NE:(t + 1) * NE], lgt[:, t * P:(t + 1) * P], ident[0:NE, 0:NE])
            last.then_inc(s_lg, 1)
            down(0, 3, 0)
            for n in range(1, NG):
                up(1, n, 1)
                down(1, n - 1, 1)
            with pe.Fori(0, NE // 2 - 1) as it:
                pe_expert(it * 2 + 2, 0)
                pe_expert(it * 2 + 3, 1)
            pe_expert(NE, 0)
            down(NE, NG - 1, 0)


def split_expert(pool, gp, raw, wh, wl, s_wh, s_wl, e, odd):
    for m in range(3):
        gp.tensor_copy(wh[odd][:, m], raw[:, m]).then_inc(s_wh, 1)
        pool.wait_ge(s_wh, e * 3 + (m + 1))
        gp.tensor_tensor(wl[odd][:, m], raw[:, m], wh[odd][:, m].bitcast(F32), ALU.subtract).then_inc(s_wl, 1)


def kernel(**inputs):
    import numpy as np
    import concourse.bacc as bacc
    from concourse import mybir as mb
    from concourse.bass_utils import run_bass_kernel_spmd

    a = {k.replace("L0_", ""): np.asarray(v) for k, v in inputs.items()}

    def by_part(v):
        return v.reshape(-1, P).T

    def per_row(v):
        return np.tile(v, 2 * B).reshape(P, 1)

    arrays = {
        "x": a["x"].reshape(B * S, D),
        "ctx": a["ctx_1024"].reshape(B * S, D),
        "ctx_t": a["ctx_1024"].reshape(B * S, D).T,
        "cols": np.concatenate(
            [by_part(a["attn_log_dt"]), by_part(a["attn_D_skip"]), by_part(a["attn_b_in"]), by_part(a["attn_ln_g"]),
             by_part(a["attn_ln_b"]), a["attn_A_log"].reshape(KC, P, NS).transpose(1, 0, 2).reshape(P, KC * NS),
             per_row(a["xattn_igate_b"]), per_row(a["xattn_fgate_b"])], axis=1),
        "rows": np.concatenate([a["attn_b_out"], a["xattn_norm_w"], a["ffn_gate_b"]]),
        "win_t": a["attn_W_in"].T,
        "wb_t": a["attn_W_B"].T,
        "wc_t": a["attn_W_C"].T,
        "wout_t": a["attn_W_out"].T,
        "gates_t": np.concatenate([a["xattn_igate_w"], a["xattn_fgate_w"]], axis=0).T,
        "moe_w": np.stack(
            [np.stack([a["ffn_fc1"].T, a["ffn_fc2"].T, a["ffn_fc3"].T])]
            + [np.stack([a["ffn_ew1"][e].T, a["ffn_ew3"][e].T, a["ffn_ew2"][e].T]) for e in range(NE)]),
        "router_t": a["ffn_gate_w"].T,
    }
    arrays = {f"in_{k}": np.ascontiguousarray(v) for k, v in arrays.items()}
    nc = bacc.Bacc("TRN2", target_bir_lowering=False, num_devices=1)
    args = [nc.dram_tensor(k, v.shape, mb.dt.from_np(v.dtype), kind="ExternalInput").ap() for k, v in arrays.items()]
    o = nc.dram_tensor("out_x", (B * S, D), mb.dt.float32, kind="ExternalOutput").ap()
    build(nc, *args, o)
    r = run_bass_kernel_spmd(nc, [arrays], core_ids=[0])
    return r.results[0]["out_x"].reshape(B, S, D)
```
